# Optimizing a Trainium2 kernel written in Bass

```python
import numpy as np
import jax
import jax.numpy as jnp

def _softmax(x, axis=-1):
    return jax.nn.softmax(x, axis=axis)

def _gelu(x):
    return jax.nn.gelu(x, approximate=True)

def _silu(x):
    return jax.nn.silu(x)

def _sigmoid(x):
    return jax.nn.sigmoid(x)

def _layernorm(x, axis=-1, eps=1e-05):
    m = jnp.mean(x, axis=axis, keepdims=True)
    v = jnp.var(x, axis=axis, keepdims=True)
    return (x - m) / jnp.sqrt(v + eps)

def _scatter_add(tgt, idx, src, axis=0):
    return tgt.at[idx].add(src)

def _segment_sum(src, seg, n):
    return jax.ops.segment_sum(src, seg, n)
kernel_name = 'mk_hybrid_d1_jaxref_r8_3db85a'

def setup_inputs(seed: int=0):
    np.random.seed(seed)
    _w = jnp.asarray

    def _L0_attn_a_setup():
        import jax, jax.numpy as jnp
        import numpy as np
        from jax import lax
        B_SZ, L, D_MODEL = (2, 256, 128)
        D_INNER, D_STATE, D_CONV, DT_RANK = (256, 16, 4, 64)

        def _silu(v):
            return v * jax.nn.sigmoid(v)

        def _mamba_fwd(x, W_in, conv_w, conv_b, W_x, W_dt, b_dt, A_log, D, W_out):
            b, l, _ = x.shape
            xz = x @ W_in
            xs, res = jnp.split(xz, 2, axis=-1)
            xc = xs.transpose(0, 2, 1)
            xc = lax.conv_general_dilated(xc, conv_w[:, None, :], window_strides=(1,), padding=[(D_CONV - 1, 0)], feature_group_count=D_INNER, dimension_numbers=('NCH', 'OIH', 'NCH')) + conv_b[None, :, None]
            u = _silu(xc.transpose(0, 2, 1))
            x_dbl = u @ W_x
            dt, Bm, Cm = jnp.split(x_dbl, [DT_RANK, DT_RANK + D_STATE], axis=-1)
            delta = jax.nn.softplus(dt @ W_dt + b_dt)
            A = -jnp.exp(A_log)

            def step(h, inp):
                d_t, B_t, C_t, u_t = inp
                dA = jnp.exp(d_t[:, :, None] * A)
                h = dA * h + d_t[:, :, None] * B_t[:, None, :] * u_t[:, :, None]
                y = jnp.einsum('bdn,bn->bd', h, C_t)
                return (h, y)
            h0 = jnp.zeros((b, D_INNER, D_STATE), dtype=u.dtype)
            _, ys = lax.scan(step, h0, (delta.transpose(1, 0, 2), Bm.transpose(1, 0, 2), Cm.transpose(1, 0, 2), u.transpose(1, 0, 2)))
            y = ys.transpose(1, 0, 2) + u * D
            y = y * _silu(res)
            return y @ W_out
        key = jax.random.key(seed)
        ks = jax.random.split(key, 9)
        s = 0.02
        x = jax.random.normal(ks[0], (B_SZ, L, D_MODEL), dtype=jnp.float32)
        W_in = jax.random.normal(ks[1], (D_MODEL, 2 * D_INNER), dtype=jnp.float32) * s
        conv_w = jax.random.normal(ks[2], (D_INNER, D_CONV), dtype=jnp.float32) * s
        conv_b = jax.random.normal(ks[3], (D_INNER,), dtype=jnp.float32) * s
        W_x = jax.random.normal(ks[4], (D_INNER, DT_RANK + 2 * D_STATE), dtype=jnp.float32) * s
        W_dt = jax.random.normal(ks[5], (DT_RANK, D_INNER), dtype=jnp.float32) * s
        b_dt = jax.random.normal(ks[6], (D_INNER,), dtype=jnp.float32) * s
        A_log = jnp.log(jnp.broadcast_to(jnp.arange(1, D_STATE + 1, dtype=jnp.float32), (D_INNER, D_STATE)))
        D = jnp.ones((D_INNER,), dtype=jnp.float32)
        W_out = jax.random.normal(ks[7], (D_INNER, D_MODEL), dtype=jnp.float32) * s
        return {'x': x, 'W_in': W_in, 'conv_w': conv_w, 'conv_b': conv_b, 'W_x': W_x, 'W_dt': W_dt, 'b_dt': b_dt, 'A_log': A_log, 'D': D, 'W_out': W_out}
    _L0_attn_a_in = _L0_attn_a_setup()

    def _L0_attn_b_setup():
        import jax, jax.numpy as jnp
        import numpy as np
        D_MODEL = 128
        NHEAD = 16
        HEAD_DIM = D_MODEL // NHEAD
        NPOS_MAX = 125
        SEQ = 128
        BATCH = 4

        def _cope(query, attn_logits, pos_emb):
            gates = jax.nn.sigmoid(attn_logits)
            pos = jnp.cumsum(gates[..., ::-1], axis=-1)[..., ::-1]
            pos = jnp.minimum(pos, NPOS_MAX - 1)
            pos_ceil = jnp.ceil(pos).astype(jnp.int32)
            pos_floor = jnp.floor(pos).astype(jnp.int32)
            logits_int = jnp.einsum('hbsd,dn->hbsn', query, pos_emb[0])
            logits_ceil = jnp.take_along_axis(logits_int, pos_ceil, axis=-1)
            logits_floor = jnp.take_along_axis(logits_int, pos_floor, axis=-1)
            w = pos - pos_floor.astype(pos.dtype)
            return logits_ceil * w + logits_floor * (1.0 - w)
        key = jax.random.key(seed)
        ks = jax.random.split(key, 10)
        s = 0.02
        return {'x': jax.random.normal(ks[0], (SEQ, BATCH, D_MODEL), dtype=jnp.float32), 'Wq': jax.random.normal(ks[1], (D_MODEL, D_MODEL), dtype=jnp.float32) * s, 'bq': jnp.zeros((D_MODEL,), dtype=jnp.float32), 'Wk': jax.random.normal(ks[2], (D_MODEL, D_MODEL), dtype=jnp.float32) * s, 'bk': jnp.zeros((D_MODEL,), dtype=jnp.float32), 'Wv': jax.random.normal(ks[3], (D_MODEL, D_MODEL), dtype=jnp.float32) * s, 'bv': jnp.zeros((D_MODEL,), dtype=jnp.float32), 'Wo': jax.random.normal(ks[4], (D_MODEL, D_MODEL), dtype=jnp.float32) * s, 'bo': jnp.zeros((D_MODEL,), dtype=jnp.float32), 'pos_emb': jax.random.normal(ks[5], (1, HEAD_DIM, NPOS_MAX), dtype=jnp.float32) * s}
    _L0_attn_b_in = _L0_attn_b_setup()

    def _L0_ffn_setup():
        import jax, jax.numpy as jnp
        import numpy as np
        D_MODEL = 128
        key = jax.random.key(seed)
        k_x, k_w, k_a1, k_a2 = jax.random.split(key, 4)
        x = jax.random.normal(k_x, (4, 256, D_MODEL), dtype=jnp.float32)
        weight = jax.random.normal(k_w, (D_MODEL, D_MODEL), dtype=jnp.float32) * 0.02
        aux_weight1 = jax.random.normal(k_a1, (D_MODEL, D_MODEL), dtype=jnp.float32) * 0.02
        aux_weight2 = jax.random.normal(k_a2, (D_MODEL, D_MODEL), dtype=jnp.float32) * 0.02
        bias = jnp.zeros((D_MODEL,), dtype=jnp.float32)
        return {'x': x, 'weight': weight, 'aux_weight1': aux_weight1, 'aux_weight2': aux_weight2, 'bias': bias}
    _L0_ffn_in = _L0_ffn_setup()
    _d = {'L0_attn_a_x': _L0_attn_a_in['x'], 'L0_attn_a_W_in': _L0_attn_a_in['W_in'], 'L0_attn_a_conv_w': _L0_attn_a_in['conv_w'], 'L0_attn_a_conv_b': _L0_attn_a_in['conv_b'], 'L0_attn_a_W_x': _L0_attn_a_in['W_x'], 'L0_attn_a_W_dt': _L0_attn_a_in['W_dt'], 'L0_attn_a_b_dt': _L0_attn_a_in['b_dt'], 'L0_attn_a_A_log': _L0_attn_a_in['A_log'], 'L0_attn_a_D': _L0_attn_a_in['D'], 'L0_attn_a_W_out': _L0_attn_a_in['W_out'], 'L0_attn_b_Wq': _L0_attn_b_in['Wq'], 'L0_attn_b_bq': _L0_attn_b_in['bq'], 'L0_attn_b_Wk': _L0_attn_b_in['Wk'], 'L0_attn_b_bk': _L0_attn_b_in['bk'], 'L0_attn_b_Wv': _L0_attn_b_in['Wv'], 'L0_attn_b_bv': _L0_attn_b_in['bv'], 'L0_attn_b_Wo': _L0_attn_b_in['Wo'], 'L0_attn_b_bo': _L0_attn_b_in['bo'], 'L0_attn_b_pos_emb': _L0_attn_b_in['pos_emb'], 'L0_ffn_weight': _L0_ffn_in['weight'], 'L0_ffn_aux_weight1': _L0_ffn_in['aux_weight1'], 'L0_ffn_aux_weight2': _L0_ffn_in['aux_weight2'], 'L0_ffn_bias': _L0_ffn_in['bias']}
    _x0 = _d['L0_attn_a_x']
    _d['L0_attn_a_x'] = jax.random.normal(jax.random.fold_in(jax.random.key(seed), 1), (4, 1024, 128), dtype=_x0.dtype)
    del _x0
    return _d

def reference(L0_attn_a_x, L0_attn_a_W_in, L0_attn_a_conv_w, L0_attn_a_conv_b, L0_attn_a_W_x, L0_attn_a_W_dt, L0_attn_a_b_dt, L0_attn_a_A_log, L0_attn_a_D, L0_attn_a_W_out, L0_attn_b_Wq, L0_attn_b_bq, L0_attn_b_Wk, L0_attn_b_bk, L0_attn_b_Wv, L0_attn_b_bv, L0_attn_b_Wo, L0_attn_b_bo, L0_attn_b_pos_emb, L0_ffn_weight, L0_ffn_aux_weight1, L0_ffn_aux_weight2, L0_ffn_bias):

    def _L0_attn_a_ref(x, W_in, conv_w, conv_b, W_x, W_dt, b_dt, A_log, D, W_out):
        import jax, jax.numpy as jnp
        import numpy as np
        from jax import lax
        B_SZ, L, D_MODEL = (2, 256, 128)
        D_INNER, D_STATE, D_CONV, DT_RANK = (256, 16, 4, 64)

        def _silu(v):
            return v * jax.nn.sigmoid(v)

        def _mamba_fwd(x, W_in, conv_w, conv_b, W_x, W_dt, b_dt, A_log, D, W_out):
            b, l, _ = x.shape
            xz = x @ W_in
            xs, res = jnp.split(xz, 2, axis=-1)
            xc = xs.transpose(0, 2, 1)
            xc = lax.conv_general_dilated(xc, conv_w[:, None, :], window_strides=(1,), padding=[(D_CONV - 1, 0)], feature_group_count=D_INNER, dimension_numbers=('NCH', 'OIH', 'NCH')) + conv_b[None, :, None]
            u = _silu(xc.transpose(0, 2, 1))
            x_dbl = u @ W_x
            dt, Bm, Cm = jnp.split(x_dbl, [DT_RANK, DT_RANK + D_STATE], axis=-1)
            delta = jax.nn.softplus(dt @ W_dt + b_dt)
            A = -jnp.exp(A_log)

            def step(h, inp):
                d_t, B_t, C_t, u_t = inp
                dA = jnp.exp(d_t[:, :, None] * A)
                h = dA * h + d_t[:, :, None] * B_t[:, None, :] * u_t[:, :, None]
                y = jnp.einsum('bdn,bn->bd', h, C_t)
                return (h, y)
            h0 = jnp.zeros((b, D_INNER, D_STATE), dtype=u.dtype)
            _, ys = lax.scan(step, h0, (delta.transpose(1, 0, 2), Bm.transpose(1, 0, 2), Cm.transpose(1, 0, 2), u.transpose(1, 0, 2)))
            y = ys.transpose(1, 0, 2) + u * D
            y = y * _silu(res)
            return y @ W_out
        return _mamba_fwd(x, W_in, conv_w, conv_b, W_x, W_dt, b_dt, A_log, D, W_out)

    def _L0_attn_b_ref(x, Wq, bq, Wk, bk, Wv, bv, Wo, bo, pos_emb):
        import jax, jax.numpy as jnp
        import numpy as np
        D_MODEL = 128
        NHEAD = 16
        HEAD_DIM = D_MODEL // NHEAD
        NPOS_MAX = 125
        SEQ = 128
        BATCH = 4

        def _cope(query, attn_logits, pos_emb):
            gates = jax.nn.sigmoid(attn_logits)
            pos = jnp.cumsum(gates[..., ::-1], axis=-1)[..., ::-1]
            pos = jnp.minimum(pos, NPOS_MAX - 1)
            pos_ceil = jnp.ceil(pos).astype(jnp.int32)
            pos_floor = jnp.floor(pos).astype(jnp.int32)
            logits_int = jnp.einsum('hbsd,dn->hbsn', query, pos_emb[0])
            logits_ceil = jnp.take_along_axis(logits_int, pos_ceil, axis=-1)
            logits_floor = jnp.take_along_axis(logits_int, pos_floor, axis=-1)
            w = pos - pos_floor.astype(pos.dtype)
            return logits_ceil * w + logits_floor * (1.0 - w)
        S, B, _ = x.shape

        def split_heads(t):
            return t.reshape(S, B, NHEAD, HEAD_DIM).transpose(2, 1, 0, 3)
        q = split_heads(x @ Wq + bq)
        k = split_heads(x @ Wk + bk)
        v = split_heads(x @ Wv + bv)
        scale = 1.0 / HEAD_DIM ** 0.5
        attn_logits = jnp.einsum('hbsd,hbtd->hbst', q, k) * scale
        attn_logits = attn_logits + _cope(q, attn_logits, pos_emb)
        attn = jax.nn.softmax(attn_logits, axis=-1)
        out = jnp.einsum('hbst,hbtd->hbsd', attn, v)
        out = out.transpose(2, 1, 0, 3).reshape(S, B, D_MODEL)
        return out @ Wo + bo

    def _L0_ffn_ref(x, weight, aux_weight1, aux_weight2, bias):
        import jax, jax.numpy as jnp
        import numpy as np
        D_MODEL = 128
        h = jnp.einsum('btc,cd->btd', x, weight)
        h = jnp.einsum('btc,cd->btd', h, aux_weight1)
        h = jnp.einsum('btc,cd->btd', h, aux_weight2)
        return jnp.tanh(h + bias)
    x = L0_attn_a_x
    x = x + _L0_attn_a_ref(_layernorm(x, axis=-1), L0_attn_a_W_in, L0_attn_a_conv_w, L0_attn_a_conv_b, L0_attn_a_W_x, L0_attn_a_W_dt, L0_attn_a_b_dt, L0_attn_a_A_log, L0_attn_a_D, L0_attn_a_W_out)
    x = x + _L0_ffn_ref(_layernorm(x, axis=-1), L0_ffn_weight, L0_ffn_aux_weight1, L0_ffn_aux_weight2, L0_ffn_bias)
    x = x + _L0_attn_b_ref(_layernorm(x, axis=-1), L0_attn_b_Wq, L0_attn_b_bq, L0_attn_b_Wk, L0_attn_b_bk, L0_attn_b_Wv, L0_attn_b_bv, L0_attn_b_Wo, L0_attn_b_bo, L0_attn_b_pos_emb)
    x = x + _L0_ffn_ref(_layernorm(x, axis=-1), L0_ffn_weight, L0_ffn_aux_weight1, L0_ffn_aux_weight2, L0_ffn_bias)
    return x

_drawn_inputs = setup_inputs


def setup_inputs(seed=0):
    import zlib

    import numpy as np

    out = dict(_drawn_inputs(seed))
    spreads = {'L0_attn_a_D': (1.0, 0.6),
     'L0_attn_b_bq': (0.0, 2.0),
     'L0_attn_b_bk': (0.0, 2.0),
     'L0_attn_b_bv': (0.0, 1.479),
     'L0_attn_b_bo': (0.0, 0.319),
     'L0_ffn_bias': (0.0, 0.304)}
    factors = {'L0_attn_a_W_in': 8.0,
     'L0_attn_a_conv_w': 8.0,
     'L0_attn_a_conv_b': 8.0,
     'L0_attn_a_W_x': 8.0,
     'L0_attn_a_W_dt': 8.0,
     'L0_attn_a_b_dt': 8.0,
     'L0_attn_a_A_log': 8.0,
     'L0_attn_a_W_out': 8.0,
     'L0_attn_b_Wq': 61.216,
     'L0_attn_b_Wk': 56.944,
     'L0_attn_b_pos_emb': 64.0,
     'L0_attn_b_Wv': 5.753,
     'L0_attn_b_Wo': 2.738,
     'L0_ffn_weight': 8.0,
     'L0_ffn_aux_weight1': 8.0,
     'L0_ffn_aux_weight2': 8.0}
    for name, (base, spread) in spreads.items():
        noise = np.random.default_rng([zlib.crc32(name.encode()), seed]).standard_normal(out[name].shape)
        drawn = base * np.exp(spread * noise) if base else spread * noise
        out[name] = jnp.asarray(drawn.astype(out[name].dtype))
    for name, factor in factors.items():
        out[name] = (out[name] * factor).astype(out[name].dtype)
    return out
```

```python
import concourse.bass as bass
from concourse import mybir
from contextlib import ExitStack

F32 = mybir.dt.float32
ALU = mybir.AluOpType
ACT = mybir.ActivationFunctionType
AX = mybir.AxisListType


def build_hybrid_block(nc, x, W_in, conv_wT, conv_b, W_x, W_dt, b_dt, A_log, D, W_out,
                       Wq, bq, Wk, bk, Wv, bv, Wo, bo, pos_emb,
                       ffn_wT, ffn_a1, ffn_a2, ffn_b, out):
    P = 128
    NB, L, DM = x.shape
    TT = L // P
    DT = W_out.shape[0] // P
    DI = DT * P
    NS = A_log.shape[1]
    TAPS = conv_wT.shape[0]
    R = W_dt.shape[0]
    XD = R + 2 * NS
    HALF = 512
    TPH = HALF // P
    NH = 16
    HD = DM // NH
    SCALE = 1.0 / HD ** 0.5
    EPS = 1e-5
    NKNOT = NB + 1
    PW = NKNOT * NH
    SP_CAP = 30.0

    xf = x.rearrange("s (j p) c -> p s j c", p=P)
    of = out.rearrange("s (j p) c -> p s j c", p=P)
    c_scratch = nc.dram_tensor("c_scratch", [NB, NS, L], F32).ap()

    ctx = ExitStack()
    with ctx:
        def sb(name, shape, scope=ctx):
            return scope.enter_context(nc.sbuf_tensor(name, shape, F32))

        def ps(name, shape):
            return ctx.enter_context(nc.psum_tensor(name, shape, F32))

        def sem(name):
            return ctx.enter_context(nc.semaphore(name))

        ident = sb("ident", [P, P])
        ones_row = sb("ones_row", [1, P])
        head_mask = sb("head_mask", [P, NH])
        neg_half = sb("neg_half", [P, TT])
        w_in = sb("w_in", [P, 2 * DI])
        conv_w_all = sb("conv_w_all", [P, TAPS, DI])
        w_tap = sb("w_tap", [P, TAPS, DI])
        conv_bias = sb("conv_bias", [P, DT])
        w_x = sb("w_x", [P, DT, XD])
        w_dt = sb("w_dt", [R, DI])
        dt_bias = sb("dt_bias", [P, DT])
        a_log = sb("a_log", [P, DT * NS])
        a_exp = sb("a_exp", [P, DT * NS])
        a_neg = sb("a_neg", [P, DT * NS])
        d_col = sb("d_col", [P, DT])
        d_diag = sb("d_diag", [P, DT, P])
        w_out = sb("w_out", [P, DT, DM])
        w_q = sb("w_q", [P, DM])
        w_k = sb("w_k", [P, DM])
        w_v = sb("w_v", [P, DM])
        bq_col = sb("bq_col", [P, 1])
        bk_col = sb("bk_col", [P, 1])
        bv_col = sb("bv_col", [P, 1])
        w_o = sb("w_o", [P, DM])
        bo_row = sb("bo_row", [1, NB, DM])
        emb = sb("emb", [P, NKNOT])
        emb_step = sb("emb_step", [P, NKNOT])
        emb_blocks = sb("emb_blocks", [P, NKNOT, NH])
        f_wT = sb("f_wT", [P, DM])
        f_a1 = sb("f_a1", [P, DM])
        f_a2 = sb("f_a2", [P, DM])
        f_pT = sb("f_pT", [P, DM])
        f_w = sb("f_w", [P, DM])
        f_brow = sb("f_brow", [1, TPH, DM])

        xs = sb("xs", [P, NB * L])
        x_in = sb("x_in", [P, TT, P])
        x_res = sb("x_res", [P, TT, P])

        mamba = ExitStack()
        stats = sb("stats", [P, TT, 6], mamba)
        mv = sb("mv", [P, TT, 2], mamba)
        var_eps = sb("var_eps", [P, TT], mamba)
        rstd = sb("rstd", [P, TT], mamba)
        xn = sb("xn", [P, TT, P], mamba)
        xnT = sb("xnT", [P, TAPS - 1 + L], mamba)
        hT = sb("hT", [P, L], mamba)
        u = sb("u", [P, DT, L], mamba)
        gate = sb("gate", [P, DT, L], mamba)
        xdbl = sb("xdbl", [XD, L], mamba)
        b_tok = sb("b_tok", [P, TT * NS], mamba)
        z = sb("z", [P, DT, L], mamba)
        z_exp = sb("z_exp", [P, DT, L], mamba)
        delta = sb("delta", [P, DT, L], mamba)
        du = sb("du", [P, DT, L], mamba)
        duT = sb("duT", [P, TT, DI], mamba)
        ffn_t = sb("ffn_t", [P, 2, HALF], mamba)

        NDA, NC = 2, 4
        dA = sb("dA", [P, NDA, DT, L], mamba)
        duB = sb("duB", [P, 2, TPH, DI], mamba)
        h = sb("h", [P, 4, HALF], mamba)
        hC = sb("hC", [P, 4, HALF], mamba)
        c_all = sb("c_all", [P, NC, L], mamba)

        mamba.close()

        xa = sb("xa", [P, NB, P])
        c_stats = sb("c_stats", [P, 2, NB, 6])
        c_mv = sb("c_mv", [P, 2, NB, 2])
        c_ve = sb("c_ve", [P, 2, NB])
        c_rstd = sb("c_rstd", [P, 2, NB])
        xn3 = sb("xn3", [P, NB, P])
        xn4 = sb("xn4", [P, NB, P])
        xT3 = sb("xT3", [P, NB * P])
        xT4 = sb("xT4", [P, NB * P])
        qT = sb("qT", [P, NB, P])
        kT = sb("kT", [P, NB, P])
        vt = sb("vt", [P, NB * DM])
        pk = sb("pk", [P, NB, NKNOT, NH])
        qk = sb("qk", [P, NB, NB, P])
        g = sb("g", [P, NB, NB, NH])
        cl = sb("cl", [P, NB, NB * NB * NH])
        lg = sb("lg", [P, NB, NB, NH])
        mx = sb("mx", [P, NB, NH])
        sm = sb("sm", [P, NB, NH])
        rc = sb("rc", [P, NB, NH])
        at = sb("at", [P, NB, NB * NH])
        pv = sb("pv", [P, NB, NB, DM])
        o_tok = sb("o_tok", [P, NB, DM])
        oT = sb("oT", [P, NB * P])
        x3 = sb("x3", [P, NB * P])
        ft = sb("ft", [P, NB * P])
        ob = sb("ob", [P, NB * P])

        p_y = ps("p_y", [P, DT, 2, HALF])
        p_tr = ps("p_tr", [P, 2, HALF])
        p_a = ps("p_a", [P, 2, HALF])

        s_xin, s_xres, s_out = sem("x_in_loaded"), sem("x_res_loaded"), sem("out_stored")
        s_w1, s_w2 = sem("mamba_weights"), sem("other_weights")
        s_mask = sem("masks_step")
        s_cst = sem("constants_ready")
        s_aexp = sem("a_exp_ready")
        s_prep = sem("dve_prep_step")
        s_pprep = sem("pe_prep_step")
        s_bn, s_var, s_ve, s_rstd, s_xn = sem("bn_stats_done"), sem("var_ready"), sem("var_eps_ready"), sem("rstd_ready"), sem("xn_ready")
        s_full = sem("pa_full")
        s_empty = [sem("pa_empty0"), sem("pa_empty1")]
        s_xdbl = sem("xdbl_ready")
        s_cst_dram = sem("c_stored")
        s_cld = [sem(f"c_loaded{i}") for i in range(NC)]
        s_zmin, s_zexp, s_zln, s_delta, s_du = sem("z_capped"), sem("z_exp_ready"), sem("z_ln_ready"), sem("delta_ready"), sem("du_ready")
        s_duB, s_tr, s_dA, s_scan, s_hC, s_sum = sem("duB_ready"), sem("tr_ready"), sem("dA_ready"), sem("scan_done"), sem("hC_ready"), sem("sum_done")
        s_yg = sem("y_gated")
        s_x1, s_tanh, s_x2 = sem("x1_ready"), sem("ffn_tanh_ready"), sem("x2_ready")
        s_stage3 = sem("attn_constants_step")
        c_xa, c_bn = sem("attn_x_loaded"), sem("attn_bn_stats_done")
        c_var = [sem("attn_var3"), sem("attn_var4")]
        c_vep = [sem("attn_ve3"), sem("attn_ve4")]
        c_rs = [sem("attn_rstd3"), sem("attn_rstd4")]
        c_xn = [sem("attn_xn3"), sem("attn_xn4")]
        c_bnd = [sem("attn_bn3"), sem("attn_bn4")]
        c_t1, c_t2, c_t3 = sem("x_turned"), sem("o_turned"), sem("x3_turned")
        c_e1, c_e2, c_e3 = sem("xT3_ready"), sem("oT_ready"), sem("xT4_ready")
        c_proj, c_qk, c_p, c_vp, c_prod, c_L = sem("qkv_projected"), sem("qkT_ready"), sem("p_projected"), sem("v_p_ready"), sem("qk_products"), sem("scores_ready")
        c_th, c_lgp, c_sub, c_exp, c_step = sem("gates_tanh"), sem("scores_read"), sem("logits_ready"), sem("exp_ready"), sem("attention_step")
        c_pvd, c_o, c_wo, c_x3, c_ffn, c_tanh, c_out = sem("pv_products"), sem("o_ready"), sem("wo_ready"), sem("x3_ready"), sem("ffn_ready"), sem("ffn_tanh"), sem("out_tile")
        SCAN0, TR0, HC0, SUM0, YG0, X20 = 8, 4, 16, 4, 2, 2

        block = ctx.enter_context(nc.Block())
        NJOB = 28
        (J_XNT, J_CONV, J_GATE, J_XDBL, J_BT, J_Z, J_DUT, J_OUT, J_HT, J_FFN) = (0, 2, 6, 10, 12, 14, 18, 22, 24, 26)

        def wait_full(eng, b, q):
            eng.wait_ge(s_full, b * NJOB + q + 1)

        def wait_empty(eng, b, q):
            eng.wait_ge(s_empty[q % 2], b * (NJOB // 2) + q // 2 + 1)

        def xcols(b, c):
            return xs[:, bass.ds(b * L + c * HALF, HALF)]

        def xtile(b, j):
            return xs[:, bass.ds(b * L + j * P, P)]

        def x_at(j):
            v = xs[:, :].rearrange("p (s j c) -> p s j c", s=NB, c=P)
            return v[:, :, j, :] if isinstance(j, int) else v[:, :, bass.ds(j, 1), :].rearrange("p s j c -> p (s j) c")

        NW1 = 12
        NW2 = 3 + TPH + 4 + 3 + NB + NH

        @block.sync
        def _(sp):
            sp.dma_start(w_in[:, :], W_in).then_inc(s_w1, 16)
            sp.dma_start(conv_w_all[:, :, :], conv_wT.partition_broadcast(P)).then_inc(s_w1, 16)
            sp.dma_start(w_x[:, :, :], W_x.rearrange("(t p) n -> p t n", p=P)).then_inc(s_w1, 16)
            sp.dma_start(w_dt[:, :], W_dt).then_inc(s_w1, 16)
            with sp.Fori(0, NB) as b:
                sp.wait_ge(s_x2, 2 * b + X20)
                sp.dma_start(x_in[:, :, :], xf[:, bass.ds(b, 1)].rearrange("p s j c -> p (s j) c")).then_inc(s_xin, 16)
                sp.dma_start(x_res[:, :, :], xf[:, bass.ds(b, 1)].rearrange("p s j c -> p (s j) c")).then_inc(s_xres, 16)
                sp.wait_ge(s_xdbl, 2 * b + 2)
                sp.dma_start(c_scratch[bass.ds(b, 1)].rearrange("b n t -> (b n) t"), xdbl[R + NS:XD, :]).then_inc(s_cst_dram, 16)
                sp.wait_ge(s_cst_dram, 16 * b + 16)
                sp.nop(nofuse=True)
                with sp.Fori(0, NS // 4) as q:
                    for i in range(4):
                        sp.wait_ge(s_hC, (b * NS + q * 4 + i - NC + 1) * 4 + HC0)
                        sp.dma_start(c_all[:, i, :],
                                     c_scratch[bass.ds(b, 1), bass.ds(q * 4 + i, 1), :].rearrange("b n t -> (b n t)").partition_broadcast(P)
                                     ).then_inc(s_cld[i], 16)
            def load_x(j):
                sp.dma_start(xa[:, :, :], x_at(j)).then_inc(c_xa, 16)

            def store(j):
                sp.wait_ge(c_out, j + 1)
                sp.dma_start(of[:, :, j, :] if isinstance(j, int) else of[:, :, bass.ds(j, 1), :].rearrange("p s j c -> p (s j) c"),
                             ob[:, :].rearrange("p (s c) -> p s c", c=P)).then_inc(s_out, 16)

            sp.wait_ge(s_x2, 2 * NB + X20)
            load_x(0)
            sp.wait_ge(c_xn[0], 1)
            load_x(1)
            with sp.Fori(1, TT - 1) as j:
                sp.wait_ge(c_xn[0], j + 1)
                load_x(j + 1)
                store(j - 1)
            store(TT - 2)
            store(TT - 1)
            sp.wait_ge(s_out, 16 * TT)

        @block.gpsimd
        def _(pool):
            pool.memset(ident[:, :], 0.0).then_inc(s_mask, 1)
            pool.memset(head_mask[:, :], 1.0).then_inc(s_mask, 1)
            pool.memset(ones_row[:, :], 1.0)
            pool.memset(xnT[:, 0:TAPS - 1], 0.0)
            pool.memset(neg_half[:, :], -0.5).then_inc(s_cst, 1)
            pool.wait_ge(s_mask, 2)
            pool.affine_select(out=ident[:, :], in_=ident[:, :], compare_op=ALU.not_equal, fill=1.0,
                               base=0, pattern=[[-1, P]], channel_multiplier=1).then_inc(s_cst, 1)
            pool.affine_select(out=head_mask[:, :], in_=head_mask[:, :], compare_op=ALU.is_ge, fill=0.0,
                               base=0, pattern=[[-HD, NH]], channel_multiplier=1).then_inc(s_mask, 1)
            pool.wait_ge(s_mask, 3)
            pool.affine_select(out=head_mask[:, :], in_=head_mask[:, :], compare_op=ALU.is_ge, fill=0.0,
                               base=HD - 1, pattern=[[HD, NH]], channel_multiplier=-1).then_inc(s_cst, 1)
            pool.wait_ge(s_cst, 3)
            pool.memset(hC[:, 0, 0:1], 0.0).then_inc(s_hC, HC0)
            pool.memset(hC[:, 1, 0:1], 0.0).then_inc(s_x2, X20)

            def rstd_of(e):
                pool.wait_ge(s_var, e + 1)
                pool.nop(nofuse=True)
                pool.tensor_scalar(var_eps[:, :], mv[:, :, 1], EPS, None, ALU.add).then_inc(s_ve, 1)
                pool.wait_ge(s_ve, e + 1)
                pool.nop(nofuse=True)
                pool.tensor_tensor(rstd[:, :], var_eps[:, :], neg_half[:, :], ALU.pow).then_inc(s_rstd, 1)

            with pool.Fori(0, NB) as b:
                rstd_of(2 * b)
                for dt in range(DT):
                    pool.wait_ge(s_delta, b * DT + dt + 1)
                    pool.tensor_tensor(du[:, dt, :], delta[:, dt, :], u[:, dt, :], ALU.mult).then_inc(s_du, 1)
                with pool.Fori(0, NS // 4) as q:
                    for i in range(4):
                        n = b * NS + q * 4 + i
                        pool.wait_ge(s_cld[i], 16 * (b * (NS // 4) + q) + 16)
                        for k in range(4):
                            half = k // 2
                            pool.wait_ge(s_scan, n * 4 + k + 1 + SCAN0)
                            pool.wait_ge(s_sum, n * 4 + k - 3 + SUM0)
                            pool.tensor_tensor(hC[:, k, :], h[:, k, :], c_all[:, i, half * HALF:(half + 1) * HALF],
                                               ALU.mult).then_inc(s_hC, 1)
                rstd_of(2 * b + 1)
                for c in range(2):
                    pool.wait_ge(s_tanh, 2 * b + c + 1)
                    pool.tensor_tensor(xcols(b, c), x_res[:, c * TPH:(c + 1) * TPH, :].rearrange("p j c -> p (j c)"), ffn_t[:, c, :], ALU.add).then_inc(s_x2, 1)

            def attn_rstd(a, j):
                pool.wait_ge(c_var[a], j + 1)
                pool.nop(nofuse=True)
                pool.tensor_scalar(c_ve[:, a, :], c_mv[:, a, :, 1], EPS, None, ALU.add).then_inc(c_vep[a], 1)
                pool.wait_ge(c_vep[a], j + 1)
                pool.nop(nofuse=True)
                pool.tensor_tensor(c_rstd[:, a, :], c_ve[:, a, :], neg_half[:, 0:NB], ALU.pow).then_inc(c_rs[a], 1)

            def products(j, first=False):
                pool.wait_ge(c_qk, j + 1)
                if not first:
                    pool.wait_ge(c_L, j)
                pool.tensor_tensor(qk[:, :, :, :], qT[:, :, :].unsqueeze(2).to_broadcast([P, NB, NB, P]),
                                   kT[:, :, :].unsqueeze(1).to_broadcast([P, NB, NB, P]), ALU.mult).then_inc(c_prod, 1)

            def finish(j, first=False):
                pool.wait_ge(c_tanh, j + 1)
                if not first:
                    pool.wait_ge(s_out, 16 * j)
                pool.tensor_tensor(ob[:, :], x3[:, :], ft[:, :], ALU.add).then_inc(c_out, 1)

            attn_rstd(0, 0)
            products(0, first=True)
            attn_rstd(0, 1)
            products(1)
            attn_rstd(1, 0)
            attn_rstd(0, 2)
            products(2)
            finish(0, first=True)
            with pool.Fori(2, TT - 1) as j:
                attn_rstd(1, j - 1)
                attn_rstd(0, j + 1)
                products(j + 1)
                finish(j - 1)
            attn_rstd(1, TT - 2)
            finish(TT - 2)
            attn_rstd(1, TT - 1)
            finish(TT - 1)

        @block.scalar
        def _(act):
            for dt in range(DT):
                act.dma_start(conv_bias[:, dt:dt + 1], conv_b[dt * P:(dt + 1) * P].rearrange("(p a) -> p a", a=1)).then_inc(s_w1, 16)
            for dt in range(DT):
                act.dma_start(dt_bias[:, dt:dt + 1], b_dt[dt * P:(dt + 1) * P].rearrange("(p a) -> p a", a=1)).then_inc(s_w1, 16)
            act.dma_start(a_log[:, :].rearrange("p (t n) -> p t n", n=NS), A_log.rearrange("(t p) n -> p t n", p=P)).then_inc(s_w1, 16)
            for dt in range(DT):
                act.dma_start(d_col[:, dt:dt + 1], D[dt * P:(dt + 1) * P].rearrange("(p a) -> p a", a=1)).then_inc(s_w1, 16)
            act.dma_start(w_out[:, :, :], W_out.rearrange("(t p) n -> p t n", p=P)).then_inc(s_w1, 16)
            act.dma_start(f_wT[:, :], ffn_wT).then_inc(s_w2, 16)
            act.dma_start(f_a1[:, :], ffn_a1).then_inc(s_w2, 16)
            act.dma_start(f_a2[:, :], ffn_a2).then_inc(s_w2, 16)
            for k in range(TPH):
                act.dma_start(f_brow[0:1, k, :], ffn_b.rearrange("(a n) -> a n", a=1)).then_inc(s_w2, 16)
            for w, src in ((w_q, Wq), (w_k, Wk), (w_v, Wv), (w_o, Wo)):
                act.dma_start(w[:, :], src).then_inc(s_w2, 16)
            for w, src in ((bq_col, bq), (bk_col, bk), (bv_col, bv)):
                act.dma_start(w[:, :], src.rearrange("(p a) -> p a", a=1)).then_inc(s_w2, 16)
            for k in range(NB):
                act.dma_start(bo_row[0:1, k, :], bo.rearrange("(a n) -> a n", a=1)).then_inc(s_w2, 16)
            for hd in range(NH):
                act.dma_start(emb[hd * HD:(hd + 1) * HD, :], pos_emb[0, :, 0:NKNOT]).then_inc(s_w2, 16)
            act.wait_ge(s_w1, 16 * NW1)
            nc.scalar.activation(a_exp[:, :], a_log[:, :], ACT.Exp).then_inc(s_aexp, 1)

            with act.Fori(0, NB) as b:
                for c in range(2):
                    wait_full(act, b, J_XNT + c)
                    nc.scalar.activation(xnT[:, TAPS - 1 + c * HALF:TAPS - 1 + (c + 1) * HALF], p_a[:, c % 2, :],
                                         ACT.Copy).then_inc(s_empty[c % 2], 1)
                for k in range(4):
                    c, dt = k // 2, k % 2
                    wait_full(act, b, J_CONV + k)
                    nc.scalar.activation(u[:, dt, c * HALF:(c + 1) * HALF], p_a[:, k % 2, :], ACT.Silu,
                                         bias=conv_bias[:, dt:dt + 1]).then_inc(s_empty[k % 2], 1)
                for k in range(4):
                    c, dt = k // 2, k % 2
                    wait_full(act, b, J_GATE + k)
                    nc.scalar.activation(gate[:, dt, c * HALF:(c + 1) * HALF], p_a[:, k % 2, :], ACT.Silu
                                         ).then_inc(s_empty[k % 2], 1)
                for dt in range(DT):
                    act.wait_ge(s_zmin, b * DT + dt + 1)
                    nc.scalar.activation(z_exp[:, dt, :], z_exp[:, dt, :], ACT.Exp).then_inc(s_zexp, 1)
                for dt in range(DT):
                    act.wait_ge(s_zexp, b * DT + dt + 1)
                    nc.scalar.activation(z_exp[:, dt, :], z_exp[:, dt, :], ACT.Ln, bias=1.0).then_inc(s_zln, 1)
                for k in range(4):
                    wait_full(act, b, J_DUT + k)
                    nc.scalar.activation(duT[:, 2 * k:2 * k + 2, :].rearrange("p a d -> p (a d)"), p_a[:, k % 2, :],
                                         ACT.Copy).then_inc(s_empty[k % 2], 1)
                act.wait_ge(s_empty[1], b * (NJOB // 2) + (J_DUT + 3) // 2 + 2)
                with act.Fori(0, NS // 4) as q:
                    for i in range(4):
                        n = b * NS + q * 4 + i

                        def spread(half):
                            act.wait_ge(s_tr, n * 4 + 2 * half - 2 + TR0)
                            for t in range(TPH):
                                last = nc.scalar.activation(duB[:, half, t, :], duT[:, half * TPH + t, :], ACT.Copy,
                                                            scale=b_tok[:, bass.ds((half * TPH + t) * NS + q * 4 + i, 1)])
                            last.then_inc(s_duB, 1)

                        spread(0)
                        act.wait_ge(s_scan, (n - 1) * 4 + SCAN0)
                        for dt in range(DT):
                            nc.scalar.activation(dA[:, i % NDA, dt, :], delta[:, dt, :], ACT.Exp,
                                                 scale=a_neg[:, bass.ds(dt * NS + q * 4 + i, 1)]).then_inc(s_dA, 1)
                        spread(1)
                for c in range(2):
                    wait_full(act, b, J_HT + c)
                    nc.scalar.activation(hT[:, c * HALF:(c + 1) * HALF], p_a[:, c % 2, :], ACT.Copy
                                         ).then_inc(s_empty[c % 2], 1)
                for c in range(2):
                    wait_full(act, b, J_FFN + c)
                    nc.scalar.activation(ffn_t[:, c, :], p_a[:, c % 2, :], ACT.Tanh).then_inc(s_tanh, 1)
                    act.wait_ge(s_tanh, 2 * b + c + 1)
                    act.sem_inc(s_empty[c % 2], 1)

            def exps(j):
                act.wait_ge(c_sub, j + 1)
                nc.scalar.activation(lg[:, :, :, :], lg[:, :, :, :], ACT.Exp).then_inc(c_exp, 1)

            def turned(full, dst, done, j):
                act.wait_ge(full, j + 1)
                nc.scalar.activation(dst[:, :], p_tr[:, 1, :], ACT.Copy).then_inc(done, 1)

            def qk_out(j):
                act.wait_ge(c_proj, j + 1)
                nc.scalar.activation(qT[:, :, :].rearrange("p s t -> p (s t)"), p_y[:, 0, 0, :], ACT.Identity, bias=bq_col[:, :])
                nc.scalar.activation(kT[:, :, :].rearrange("p s t -> p (s t)"), p_y[:, 0, 1, :], ACT.Identity, bias=bk_col[:, :]
                                     ).then_inc(c_qk, 1)

            def vp_out(j):
                act.wait_ge(c_p, j + 1)
                nc.scalar.activation(vt[:, :], p_y[:, 1, 0, :], ACT.Copy)
                nc.scalar.activation(pk[:, :, :, :].rearrange("p s m h -> p (s m h)"), p_y[:, 1, 1, 0:NB * PW], ACT.Copy
                                     ).then_inc(c_vp, 1)

            def gates(j):
                act.wait_ge(c_L, j + 1)
                nc.scalar.activation(g[:, :, :, :].rearrange("p s t h -> p (s t h)"), p_tr[:, 0, 0:NB * NB * NH], ACT.Tanh,
                                     scale=0.5 * SCALE).then_inc(c_th, 1)

            def ffn_out(j, first=False):
                act.wait_ge(c_ffn, j + 1)
                if not first:
                    act.wait_ge(c_out, j)
                nc.scalar.activation(ft[:, :], p_a[:, 1, :], ACT.Tanh).then_inc(c_tanh, 1)

            def act_step(j, first=False, last=False, second=False):
                exps(j)
                if not first:
                    turned(c_t3, xT4, c_e3, j - 1)
                if not last:
                    turned(c_t1, xT3, c_e1, j + 1)
                    qk_out(j + 1)
                if not first:
                    ffn_out(j - 1, first=second)
                turned(c_t2, oT, c_e2, j)
                if not last:
                    vp_out(j + 1)
                    gates(j + 1)

            turned(c_t1, xT3, c_e1, 0)
            qk_out(0)
            vp_out(0)
            gates(0)
            act_step(0, first=True)
            act_step(1, second=True)
            with act.Fori(2, TT - 1) as j:
                act_step(j)
            act_step(TT - 1, last=True)
            turned(c_t3, xT4, c_e3, TT - 1)
            ffn_out(TT - 1)

        @block.vector
        def _(dve):
            dve.wait_ge(s_w1, 16 * NW1)
            nc.vector.tensor_tensor(w_tap[:, :, :], conv_w_all[:, :, :],
                                    w_in[:, 0:DI].unsqueeze(1).to_broadcast([P, TAPS, DI]), ALU.mult)
            dve.wait_ge(s_aexp, 1)
            nc.vector.tensor_scalar(a_neg[:, :], a_exp[:, :], -1.0, None, ALU.mult)
            dve.wait_ge(s_cst, 3)
            for dt in range(DT):
                nc.vector.tensor_scalar(d_diag[:, dt, :], ident[:, :], d_col[:, dt:dt + 1], None, ALU.mult)
            nc.vector.memset(stats[:, 0, 0:1], 0.0).then_inc(s_prep, 1)
            dve.wait_ge(s_prep, 1)
            nc.vector.memset(stats[:, 0, 0:1], 0.0).then_inc(s_scan, SCAN0)
            dve.wait_ge(s_pprep, 1)
            nc.vector.tensor_copy(f_pT[:, :], p_tr[:, 0, 0:DM]).then_inc(s_prep, 1)
            dve.wait_ge(s_pprep, 2)
            nc.vector.tensor_copy(f_w[:, :], p_tr[:, 1, 0:DM]).then_inc(s_prep, 1)

            dve.wait_ge(s_w2, 16 * NW2)
            nc.vector.tensor_copy(emb_step[:, 0:1], emb[:, 0:1])
            nc.vector.tensor_tensor(emb_step[:, 1:NKNOT], emb[:, 1:NKNOT], emb[:, 0:NKNOT - 1], ALU.subtract).then_inc(s_stage3, 1)
            dve.wait_ge(s_stage3, 1)
            nc.vector.tensor_tensor(emb_blocks[:, :, :], emb_step[:, :].unsqueeze(2).to_broadcast([P, NKNOT, NH]),
                                    head_mask[:, :].unsqueeze(1).to_broadcast([P, NKNOT, NH]), ALU.mult).then_inc(s_stage3, 1)
            dve.wait_ge(s_pprep, 3)
            nc.vector.tensor_tensor(bo_row[:, :, :], bo_row[:, :, :], p_a[0:1, 0, 0:DM].unsqueeze(1).to_broadcast([1, NB, DM]),
                                    ALU.add).then_inc(s_stage3, 1)

            def layernorm(xb, e):
                for j in range(TT):
                    last = nc.vector.bn_stats(stats[:, j, :], xb[:, j, :])
                last.then_inc(s_bn, 1)
                dve.wait_ge(s_bn, e + 1)
                dve.nop(nofuse=True)
                for j in range(TT):
                    last = nc.vector.bn_aggr(mv[:, j, :], stats[:, j, :])
                last.then_inc(s_var, 1)
                dve.wait_ge(s_rstd, e + 1)
                for j in range(TT):
                    last = nc.vector.tensor_scalar(xn[:, j, :], xb[:, j, :], mv[:, j, 0:1], rstd[:, j:j + 1],
                                                   ALU.subtract, ALU.mult)
                    if j % TPH == TPH - 1:
                        last.then_inc(s_xn, 1)

            with dve.Fori(0, NB) as b:
                dve.wait_ge(s_xin, 16 * b + 16)
                dve.nop(nofuse=True)
                layernorm(x_in, 2 * b)
                for c in range(2):
                    wait_full(dve, b, J_XDBL + c)
                    nc.vector.tensor_copy(xdbl[:, c * HALF:(c + 1) * HALF], p_a[0:XD, c % 2, :]).then_inc(s_xdbl, 1)
                    dve.wait_ge(s_xdbl, 2 * b + c + 1)
                    dve.sem_inc(s_empty[c % 2], 1)
                for c in range(2):
                    wait_full(dve, b, J_BT + c)
                    nc.vector.tensor_copy(b_tok[:, c * TPH * NS:(c + 1) * TPH * NS].rearrange("p (t n) -> p t n", n=NS),
                                          p_a[:, c % 2, :].rearrange("p (t n) -> p t n", n=P)[:, :, R:R + NS]
                                          ).then_inc(s_empty[c % 2], 1)
                for k in range(4):
                    c, dt = k // 2, k % 2
                    wait_full(dve, b, J_Z + k)
                    nc.vector.tensor_scalar(z[:, dt, c * HALF:(c + 1) * HALF], p_a[:, k % 2, :],
                                            dt_bias[:, dt:dt + 1], None, ALU.add).then_inc(s_empty[k % 2], 1)
                for dt in range(DT):
                    dve.wait_ge(s_empty[dt], b * (NJOB // 2) + (J_Z + 2 + dt) // 2 + 2)
                    nc.vector.tensor_scalar(z_exp[:, dt, :], z[:, dt, :], SP_CAP, None, ALU.min).then_inc(s_zmin, 1)
                for dt in range(DT):
                    dve.wait_ge(s_zln, b * DT + dt + 1)
                    nc.vector.tensor_tensor(delta[:, dt, :], z[:, dt, :], z_exp[:, dt, :], ALU.max).then_inc(s_delta, 1)
                with dve.Fori(0, NS // 4) as q:
                    for i in range(4):
                        n = b * NS + q * 4 + i
                        for k in range(4):
                            half, dt = k // 2, k % 2
                            if half == 0:
                                dve.wait_ge(s_dA, n * DT + dt + 1)
                            dve.wait_ge(s_tr, n * 4 + k + 1 + TR0)
                            dve.wait_ge(s_hC, n * 4 + k - 3 + HC0)
                            dve.wait_ge(s_scan, n * 4 + k - 1 + SCAN0)
                            nc.vector.tensor_tensor_scan(h[:, k, :], dA[:, i % NDA, dt, half * HALF:(half + 1) * HALF],
                                                         p_tr[:, k % 2, :],
                                                         0.0 if half == 0 else h[:, dt, HALF - 1:HALF],
                                                         ALU.mult, ALU.add).then_inc(s_scan, 1)
                for dt in range(DT):
                    dve.wait_ge(s_sum, (b * NS + NS) * 4 + SUM0)
                    nc.vector.tensor_tensor(gate[:, dt, :], p_y[:, dt, :, :].rearrange("p a t -> p (a t)"), gate[:, dt, :],
                                            ALU.mult).then_inc(s_yg, 1)
                dve.wait_ge(s_xres, 16 * b + 16)
                for c in range(2):
                    wait_full(dve, b, J_OUT + c)
                    xh = x_res[:, c * TPH:(c + 1) * TPH, :].rearrange("p j c -> p (j c)")
                    nc.vector.tensor_tensor(xh, p_a[:, c % 2, :], xh, ALU.add).then_inc(s_empty[c % 2], 1)
                for c in range(2):
                    dve.wait_ge(s_empty[c], b * (NJOB // 2) + (J_OUT + c) // 2 + 2)
                dve.nop(nofuse=True)
                layernorm(x_res, 2 * b + 1)

            NSTEP = 13

            def attn_stats(a, xb, j):
                for t in range(NB):
                    last = nc.vector.bn_stats(c_stats[:, a, t, :], xb[:, t * P:(t + 1) * P])
                last.then_inc(c_bnd[a], 1)
                dve.wait_ge(c_bnd[a], j + 1)
                dve.nop(nofuse=True)
                for t in range(NB):
                    last = nc.vector.bn_aggr(c_mv[:, a, t, :], c_stats[:, a, t, :])
                last.then_inc(c_var[a], 1)

            def attn_norm(a, xb, xnb, j):
                dve.wait_ge(c_rs[a], j + 1)
                for t in range(NB):
                    last = nc.vector.tensor_scalar(xnb[:, t, :], xb[:, t * P:(t + 1) * P], c_mv[:, a, t, 0:1],
                                                   c_rstd[:, a, t:t + 1], ALU.subtract, ALU.mult)
                last.then_inc(c_xn[a], 1)

            xaf = xa[:, :, :].rearrange("p s c -> p (s c)")

            def stats3(j):
                dve.wait_ge(c_xa, 16 * j + 16)
                dve.nop(nofuse=True)
                attn_stats(0, xaf, j)

            def residual(j, first=False):
                dve.wait_ge(c_wo, j + 1)
                if not first:
                    dve.wait_ge(c_out, j)
                nc.vector.tensor_tensor(x3[:, :].rearrange("p (s c) -> p s c", c=P), p_a[:, 0, :].rearrange("p (s c) -> p s c", c=P),
                                        x_at(j), ALU.add).then_inc(c_x3, 1)
                dve.wait_ge(c_x3, j + 1)
                dve.nop(nofuse=True)
                attn_stats(1, x3, j)

            def logits(j):
                k = [0]

                def link(ins):
                    k[0] += 1
                    ins.then_inc(c_step, 1)
                    dve.wait_ge(c_step, j * NSTEP + k[0])

                gf = g[:, :, :, :].rearrange("p s t h -> p (s t h)")
                lf = lg[:, :, :, :].rearrange("p s t h -> p (s t h)")
                dve.wait_ge(c_th, j + 1)
                link(nc.vector.tensor_scalar(gf, gf, 0.5, 0.5, ALU.mult, ALU.add))
                for t in range(NB - 2, -1, -1):
                    link(nc.vector.tensor_tensor(g[:, :, t, :], g[:, :, t, :], g[:, :, t + 1, :], ALU.add))
                for m in range(NB):
                    last = nc.vector.tensor_scalar(cl[:, m, :], gf, float(m), float(m + 1), ALU.max, ALU.min)
                link(last)
                dve.wait_ge(c_vp, j + 1)
                for s in range(NB):
                    last = nc.vector.scalar_tensor_tensor(lg[:, s, :, :], p_tr[:, 0, s * NB * NH:(s + 1) * NB * NH].rearrange("p (t h) -> p t h", h=NH),
                                                   SCALE, pk[:, s, 0, :].unsqueeze(1).to_broadcast([P, NB, NH]), ALU.mult, ALU.add)
                last.then_inc(c_lgp, 1)
                for m in range(NB):
                    for s in range(NB):
                        c = cl[:, m, s * NB * NH:(s + 1) * NB * NH].rearrange("p (t h) -> p t h", h=NH)
                        last = nc.vector.scalar_tensor_tensor(c, c, float(m), pk[:, s, m + 1, :].unsqueeze(1).to_broadcast([P, NB, NH]),
                                                              ALU.subtract, ALU.mult)
                link(last)
                nc.vector.tensor_tensor(cl[:, 0, :], cl[:, 0, :], cl[:, 1, :], ALU.add)
                link(nc.vector.tensor_tensor(cl[:, 2, :], cl[:, 2, :], cl[:, 3, :], ALU.add))
                link(nc.vector.tensor_tensor(cl[:, 0, :], cl[:, 0, :], cl[:, 2, :], ALU.add))
                link(nc.vector.tensor_tensor(lf, lf, cl[:, 0, :], ALU.add))
                link(nc.vector.tensor_reduce(mx[:, :, :], lg[:, :, :, :].rearrange("p s t h -> p s h t"), AX.X, ALU.max))
                nc.vector.tensor_tensor(lg[:, :, :, :], lg[:, :, :, :], mx[:, :, :].unsqueeze(2).to_broadcast([P, NB, NB, NH]),
                                        ALU.subtract).then_inc(c_sub, 1)
                return k[0]

            def weights(j, k0):
                k = [k0]

                def link(ins):
                    k[0] += 1
                    ins.then_inc(c_step, 1)
                    dve.wait_ge(c_step, j * NSTEP + k[0])

                dve.wait_ge(c_exp, j + 1)
                link(nc.vector.tensor_reduce(sm[:, :, :], lg[:, :, :, :].rearrange("p s t h -> p s h t"), AX.X, ALU.add))
                link(nc.vector.reciprocal(rc[:, :, :], sm[:, :, :]))
                link(nc.vector.tensor_tensor(at[:, :, :].rearrange("p s (t h) -> p s t h", h=NH), lg[:, :, :, :],
                                             rc[:, :, :].unsqueeze(2).to_broadcast([P, NB, NB, NH]), ALU.mult))
                nc.vector.tensor_tensor(pv[:, :, :, :].rearrange("p s t (h d) -> p s (t h) d", d=HD),
                                        at[:, :, :].unsqueeze(3).to_broadcast([P, NB, NB * NH, HD]),
                                        vt[:, :].rearrange("p (a d) -> p a d", d=HD).unsqueeze(1).to_broadcast([P, NB, NB * NH, HD]),
                                        ALU.mult).then_inc(c_pvd, 1)
                assert k[0] == NSTEP, k[0]

            def mix(j):
                dve.wait_ge(c_pvd, j + 1)
                nc.vector.tensor_reduce(o_tok[:, :, :], pv[:, :, :, :].rearrange("p s t c -> p s c t"), AX.X, ALU.add).then_inc(c_o, 1)

            def dve_step(j, first=False, last=False, second=False):
                if not first:
                    residual(j - 1, first=second)
                k = logits(j)
                if not first:
                    attn_norm(1, x3, xn4, j - 1)
                if not last:
                    stats3(j + 1)
                weights(j, k)
                if not last:
                    attn_norm(0, xaf, xn3, j + 1)
                mix(j)

            stats3(0)
            attn_norm(0, xaf, xn3, 0)
            dve_step(0, first=True)
            dve_step(1, second=True)
            with dve.Fori(2, TT - 1) as j:
                dve_step(j)
            dve_step(TT - 1, last=True)
            residual(TT - 1)
            attn_norm(1, x3, xn4, TT - 1)

        @block.tensor
        def _(pe):
            pe.wait_ge(s_w2, 16 * NW2)
            nc.tensor.matmul(p_tr[:, 0, 0:DM], f_a1[:, :], f_wT[:, :], start=True, stop=True).then_inc(s_pprep, 1)
            pe.wait_ge(s_prep, 2)
            nc.tensor.matmul(p_tr[:, 1, 0:DM], f_pT[:, :], f_a2[:, :], start=True, stop=True).then_inc(s_pprep, 1)
            nc.tensor.matmul(p_a[0:1, 0, 0:DM], bv_col[:, :], w_o[:, :], start=True, stop=True).then_inc(s_pprep, 1)
            pe.wait_ge(s_prep, 3)
            pe.wait_ge(s_stage3, 3)
            nc.tensor.matmul(p_tr[:, 0, 0:2], ident[:, :], ident[:, 0:2], start=True, stop=True).then_inc(s_tr, TR0)
            pe.sem_inc(s_sum, SUM0)
            pe.sem_inc(s_yg, YG0)
            for bank in range(2):
                pe.sem_inc(s_empty[bank], 1)

            def start_job(b, q):
                wait_empty(pe, b, q)
                return p_a[:, q % 2, :]

            def transposes(b, q, src, cols=P):
                o = start_job(b, q)
                for t, a in enumerate(src):
                    last = nc.tensor.transpose(o[:, t * P:t * P + cols], a, ident[0:cols, 0:cols])
                last.then_inc(s_full, 1)

            with pe.Fori(0, NB) as b:
                for c in range(2):
                    pe.wait_ge(s_xn, 4 * b + c + 1)
                    transposes(b, J_XNT + c, [xn[:, c * TPH + t, :] for t in range(TPH)])
                for k in range(4):
                    c, dt = k // 2, k % 2
                    pe.wait_ge(s_empty[c], b * (NJOB // 2) + 2)
                    o = start_job(b, J_CONV + k)
                    for tap in range(TAPS):
                        last = nc.tensor.matmul(o, w_tap[:, tap, dt * P:(dt + 1) * P],
                                                xnT[:, c * HALF + tap:c * HALF + tap + HALF],
                                                start=(tap == 0), stop=(tap == TAPS - 1))
                    last.then_inc(s_full, 1)
                for k in range(4):
                    c, dt = k // 2, k % 2
                    nc.tensor.matmul(start_job(b, J_GATE + k), w_in[:, DI + dt * P:DI + (dt + 1) * P],
                                     xnT[:, TAPS - 1 + c * HALF:TAPS - 1 + (c + 1) * HALF],
                                     start=True, stop=True).then_inc(s_full, 1)
                for c in range(2):
                    o = start_job(b, J_XDBL + c)
                    for dt in range(DT):
                        last = nc.tensor.matmul(o[0:XD, :], w_x[:, dt, :], u[:, dt, c * HALF:(c + 1) * HALF],
                                                start=(dt == 0), stop=(dt == DT - 1))
                    last.then_inc(s_full, 1)
                for c in range(2):
                    pe.wait_ge(s_xdbl, 2 * b + c + 1)
                    transposes(b, J_BT + c, [xdbl[:, (c * TPH + t) * P:(c * TPH + t + 1) * P] for t in range(TPH)], XD)
                for k in range(4):
                    c, dt = k // 2, k % 2
                    nc.tensor.matmul(start_job(b, J_Z + k), w_dt[:, dt * P:(dt + 1) * P], xdbl[0:R, c * HALF:(c + 1) * HALF],
                                     start=True, stop=True).then_inc(s_full, 1)
                pe.wait_ge(s_du, b * DT + DT)
                for k in range(4):
                    transposes(b, J_DUT + k, [du[:, dt, (2 * k + t) * P:(2 * k + t + 1) * P] for t in range(2) for dt in range(DT)])

                pe.wait_ge(s_yg, b * DT + YG0)
                for dt in range(DT):
                    for c in range(2):
                        nc.tensor.matmul(p_y[:, dt, c, :], d_diag[:, dt, :], u[:, dt, c * HALF:(c + 1) * HALF],
                                         start=True, stop=False, skip_group_check=True)

                def turn(q, k16):
                    i, k = k16 // 4, k16 % 4
                    half, dt = k // 2, k % 2
                    n = b * NS + q * 4 + i
                    pe.wait_ge(s_duB, n * 2 + half + 1)
                    pe.wait_ge(s_scan, n * 4 + k - 1 + SCAN0)
                    for t in range(TPH):
                        last = nc.tensor.transpose(p_tr[:, k % 2, t * P:(t + 1) * P], duB[:, half, t, dt * P:(dt + 1) * P], ident[:, :])
                    last.then_inc(s_tr, 1)

                def add(q, k16, stop=False):
                    i, k = k16 // 4, k16 % 4
                    half, dt = k // 2, k % 2
                    n = b * NS + q * 4 + i
                    pe.wait_ge(s_hC, n * 4 + k + 1 + HC0)
                    nc.tensor.matmul(p_y[:, dt, half, :], ident[:, :], hC[:, k, :], start=False, stop=stop,
                                     skip_group_check=True).then_inc(s_sum, 1)

                LAG = 3
                for k16 in range(LAG):
                    turn(0, k16)
                with pe.Fori(0, NS // 4 - 1) as q:
                    for k16 in range(16):
                        turn(q, k16 + LAG)
                        add(q, k16)
                q = NS // 4 - 1
                for k16 in range(16):
                    if k16 + LAG < 16:
                        turn(q, k16 + LAG)
                    add(q, k16, stop=(k16 >= 12))

                for c in range(2):
                    pe.wait_ge(s_yg, b * DT + DT + YG0)
                    o = start_job(b, J_OUT + c)
                    for t in range(TPH):
                        for dt in range(DT):
                            last = nc.tensor.matmul(o[:, t * P:(t + 1) * P], gate[:, dt, (c * TPH + t) * P:(c * TPH + t + 1) * P],
                                                    w_out[:, dt, :], start=(dt == 0), stop=(dt == DT - 1))
                    last.then_inc(s_full, 1)
                for c in range(2):
                    pe.wait_ge(s_xn, 4 * b + 2 + c + 1)
                    transposes(b, J_HT + c, [xn[:, c * TPH + t, :] for t in range(TPH)])
                for c in range(2):
                    pe.wait_ge(s_empty[c], b * (NJOB // 2) + J_HT // 2 + 2)
                    o = start_job(b, J_FFN + c)
                    nc.tensor.matmul(o, ones_row[:, :], f_brow[:, :, :].rearrange("a t n -> a (t n)"), start=True, stop=False,
                                     skip_group_check=True)
                    for t in range(TPH):
                        last = nc.tensor.matmul(o[:, t * P:(t + 1) * P], hT[:, (c * TPH + t) * P:(c * TPH + t + 1) * P],
                                                f_w[:, :], start=False, stop=True, skip_group_check=True)
                    last.then_inc(s_full, 1)


            def turn4(src, need, full, j, freed):
                pe.wait_ge(need, j + 1)
                if freed is not None:
                    pe.wait_ge(*freed)
                for t in range(NB):
                    last = nc.tensor.transpose(p_tr[:, 1, t * P:(t + 1) * P], src[:, t, :], ident[:, :])
                last.then_inc(full, 1)

            def project(j, first=False):
                pe.wait_ge(c_e1, j + 1)
                if not first:
                    pe.wait_ge(c_vp, j)
                nc.tensor.matmul(p_y[:, 0, 0, :], w_q[:, :], xT3[:, :], start=True, stop=True)
                nc.tensor.matmul(p_y[:, 0, 1, :], w_k[:, :], xT3[:, :], start=True, stop=True).then_inc(c_proj, 1)
                for t in range(NB):
                    nc.tensor.matmul(p_y[:, 1, 0, t * DM:(t + 1) * DM], xT3[:, t * P:(t + 1) * P], w_v[:, :], start=True, stop=True)
                pe.wait_ge(c_qk, j + 1)
                for t in range(NB):
                    last = nc.tensor.matmul(p_y[:, 1, 1, t * PW:(t + 1) * PW], qT[:, t, :],
                                            emb_blocks[:, :, :].rearrange("p m h -> p (m h)"), start=True, stop=True)
                last.then_inc(c_p, 1)

            def scores(j, first=False):
                pe.wait_ge(c_prod, j + 1)
                if not first:
                    pe.wait_ge(c_lgp, j)
                for a in range(NB):
                    for t in range(NB):
                        last = nc.tensor.matmul(p_tr[:, 0, (a * NB + t) * NH:(a * NB + t + 1) * NH], qk[:, a, t, :], head_mask[:, :],
                                                start=True, stop=True)
                last.then_inc(c_L, 1)

            def rows(bank, bias, lhs, w, done):
                nc.tensor.matmul(p_a[:, bank, :], ones_row[:, :], bias[:, :, :].rearrange("a t n -> a (t n)"), start=True, stop=False,
                                 skip_group_check=True)
                for t in range(NB):
                    last = nc.tensor.matmul(p_a[:, bank, t * P:(t + 1) * P], lhs[:, t * P:(t + 1) * P], w[:, :],
                                            start=False, stop=True, skip_group_check=True)
                last.then_inc(done, 1)

            def out_project(j, first=False):
                pe.wait_ge(c_e2, j + 1)
                if not first:
                    pe.wait_ge(c_x3, j)
                rows(0, bo_row, oT, w_o, c_wo)

            def ffn(j, first=False):
                pe.wait_ge(c_e3, j + 1)
                if not first:
                    pe.wait_ge(c_tanh, j)
                rows(1, f_brow, xT4, f_w, c_ffn)

            def pe_step(j, first=False, last=False, second=False):
                if not first:
                    turn4(xn4, c_xn[1], c_t3, j - 1, (c_e2, j))
                if not last:
                    turn4(xn3, c_xn[0], c_t1, j + 1, (c_e1, 1) if first else (c_e3, j))
                if not first:
                    ffn(j - 1, first=second)
                if not last:
                    project(j + 1)
                turn4(o_tok, c_o, c_t2, j, (c_e3, j) if last else (c_e1, j + 2))
                out_project(j, first=first)
                if not last:
                    scores(j + 1)

            pe.wait_ge(s_empty[0], NB * NJOB // 2 + 1)
            pe.wait_ge(s_empty[1], NB * NJOB // 2 + 1)
            turn4(xn3, c_xn[0], c_t1, 0, None)
            project(0, first=True)
            scores(0, first=True)
            pe_step(0, first=True)
            pe_step(1, second=True)
            with pe.Fori(2, TT - 1) as j:
                pe_step(j)
            pe_step(TT - 1, last=True)
            turn4(xn4, c_xn[1], c_t3, TT - 1, (c_e2, TT))
            ffn(TT - 1)


_INS = [("L0_attn_a_x", 0), ("L0_attn_a_W_in", 0), ("L0_attn_a_conv_w", 1), ("L0_attn_a_conv_b", 0), ("L0_attn_a_W_x", 0),
        ("L0_attn_a_W_dt", 0), ("L0_attn_a_b_dt", 0), ("L0_attn_a_A_log", 0), ("L0_attn_a_D", 0), ("L0_attn_a_W_out", 0),
        ("L0_attn_b_Wq", 0), ("L0_attn_b_bq", 0), ("L0_attn_b_Wk", 0), ("L0_attn_b_bk", 0),
        ("L0_attn_b_Wv", 0), ("L0_attn_b_bv", 0), ("L0_attn_b_Wo", 0), ("L0_attn_b_bo", 0), ("L0_attn_b_pos_emb", 0),
        ("L0_ffn_weight", 1), ("L0_ffn_aux_weight1", 0), ("L0_ffn_aux_weight2", 0), ("L0_ffn_bias", 0)]
_OUT = (4, 1024, 128)


def kernel(**inputs):
    import numpy as _np
    import concourse.bacc as _bacc
    from concourse import mybir as _mybir
    from concourse.bass_utils import run_bass_kernel_spmd as _run

    nc = _bacc.Bacc("TRN2", target_bir_lowering=False, num_devices=1)
    arrays, args = {}, []
    for name, turned in _INS:
        a = _np.ascontiguousarray(_np.asarray(inputs[name]).T if turned else inputs[name])
        key = f"in_{name}{'_T' if turned else ''}_dram"
        arrays[key] = a
        args.append(nc.dram_tensor(key, a.shape, _mybir.dt.from_np(a.dtype), kind="ExternalInput").ap())
    args.append(nc.dram_tensor("out_0_dram", _OUT, _mybir.dt.float32, kind="ExternalOutput").ap())
    build_hybrid_block(nc, *args)
    r = _run(nc, [arrays], core_ids=[0])
    return r.results[0]["out_0_dram"]
```

```python
import concourse.bass as bass
from concourse import mybir
from contextlib import ExitStack

F32 = mybir.dt.float32
ALU = mybir.AluOpType
ACT = mybir.ActivationFunctionType
AX = mybir.AxisListType


def build_hybrid_block(nc, x, W_in, conv_wT, conv_b, W_x, W_dt, b_dt, A_log, D, W_out,
                       Wq, bq, Wk, bk, Wv, bv, Wo, bo, pos_emb,
                       ffn_wT, ffn_a1, ffn_a2, ffn_b, out):
    P = 128
    NB, L, DM = x.shape
    TT = L // P
    DT = W_out.shape[0] // P
    DI = DT * P
    NS = A_log.shape[1]
    TAPS = conv_wT.shape[0]
    R = W_dt.shape[0]
    XD = R + 2 * NS
    HALF = 512
    TPH = HALF // P
    NH = 16
    HD = DM // NH
    SCALE = 1.0 / HD ** 0.5
    EPS = 1e-5
    NKNOT = NB + 1
    PW = NKNOT * NH
    SP_CAP = 30.0

    xf = x.rearrange("s (j p) c -> p s j c", p=P)
    of = out.rearrange("s (j p) c -> p s j c", p=P)
    c_scratch = nc.dram_tensor("c_scratch", [NB, NS, L], F32).ap()

    ctx = ExitStack()
    with ctx:
        def sb(name, shape, scope=ctx):
            return scope.enter_context(nc.sbuf_tensor(name, shape, F32))

        def ps(name, shape):
            return ctx.enter_context(nc.psum_tensor(name, shape, F32))

        def sem(name):
            return ctx.enter_context(nc.semaphore(name))

        ident = sb("ident", [P, P])
        ones_row = sb("ones_row", [1, P])
        head_mask = sb("head_mask", [P, NH])
        neg_half = sb("neg_half", [P, TT])
        w_in = sb("w_in", [P, 2 * DI])
        w_tap = sb("w_tap", [P, TAPS, DI])
        conv_bias = sb("conv_bias", [P, DT])
        w_x = sb("w_x", [P, DT, XD])
        w_dt = sb("w_dt", [R, DI])
        dt_bias = sb("dt_bias", [P, DT])
        a_log = sb("a_log", [P, DT * NS])
        a_exp = sb("a_exp", [P, DT * NS])
        a_neg = sb("a_neg", [P, DT * NS])
        d_col = sb("d_col", [P, DT])
        d_diag = sb("d_diag", [P, DT, P])
        w_out = sb("w_out", [P, DT, DM])
        w_q = sb("w_q", [P, DM])
        w_k = sb("w_k", [P, DM])
        w_v = sb("w_v", [P, DM])
        bq_col = sb("bq_col", [P, 1])
        bk_col = sb("bk_col", [P, 1])
        bv_col = sb("bv_col", [P, 1])
        w_o = sb("w_o", [P, DM])
        bo_row = sb("bo_row", [1, NB, DM])
        emb = sb("emb", [P, NKNOT])
        emb_step = sb("emb_step", [P, NKNOT])
        emb_blocks = sb("emb_blocks", [P, NKNOT, NH])
        f_wT = sb("f_wT", [P, DM])
        f_a1 = sb("f_a1", [P, DM])
        f_a2 = sb("f_a2", [P, DM])
        f_pT = sb("f_pT", [P, DM])
        f_w = sb("f_w", [P, DM])
        f_brow = sb("f_brow", [1, TPH, DM])

        xs = sb("xs", [P, NB * L])

        mamba = ExitStack()
        x_in = sb("x_in", [P, TT, P], mamba)
        x_res = sb("x_res", [P, TT, P], mamba)
        stats = sb("stats", [P, 2, TT, 6], mamba)
        mv = sb("mv", [P, 2, TT, 2], mamba)
        var_eps = sb("var_eps", [P, 2, TT], mamba)
        rstd = sb("rstd", [P, 2, TT], mamba)
        xn = sb("xn", [P, 2, TT, P], mamba)
        xnT = sb("xnT", [P, TAPS - 1 + L], mamba)
        hT = sb("hT", [P, L], mamba)
        u = sb("u", [P, DT, L], mamba)
        gate = sb("gate", [P, 2 * DT * L], mamba)
        yg = sb("yg", [P, DT, L], mamba)
        xdbl = sb("xdbl", [XD, L], mamba)
        b_tok = sb("b_tok", [P, 2 * TT * NS], mamba)
        z_exp = sb("z_exp", [P, DT, L], mamba)
        delta = sb("delta", [P, 2 * DT * L], mamba)
        duT = sb("duT", [P, 2 * TT * DI], mamba)
        ffn_t = sb("ffn_t", [P, 2, HALF], mamba)

        NDA, NC = 2, 4
        dA = sb("dA", [P, NDA, DT, L], mamba)
        duB = sb("duB", [P, 4, TPH, DI], mamba)
        h = sb("h", [P, 4, HALF], mamba)
        conv_w_all = h[:, 0:TAPS * DI // HALF, :].rearrange("p a n -> p (a n)").rearrange("p (k n) -> p k n", n=DI)
        hC = sb("hC", [P, 4, HALF], mamba)
        c_all = sb("c_all", [P, NC, L], mamba)

        mamba.close()

        xa = sb("xa", [P, NB, P])
        c_stats = sb("c_stats", [P, 2, NB, 6])
        c_mv = sb("c_mv", [P, 2, NB, 2])
        c_ve = sb("c_ve", [P, 2, NB])
        c_rstd = sb("c_rstd", [P, 2, NB])
        c_negm = sb("c_negm", [P, 2, NB])
        c_shift = sb("c_shift", [P, 2, NB])
        xn3 = sb("xn3", [P, NB, P])
        xn4 = sb("xn4", [P, NB, P])
        xT3 = sb("xT3", [P, NB * P])
        xT4 = sb("xT4", [P, NB * P])
        qT = sb("qT", [P, NB, P])
        kT = sb("kT", [P, NB, P])
        vt = sb("vt", [P, 2 * NB * DM])
        pk = sb("pk", [P, 2 * NB * PW])
        qk = sb("qk", [P, NB, NB, P])
        g = sb("g", [P, NB, NB, NH])
        cl = sb("cl", [P, NB, NB * NB * NH])
        lg = sb("lg", [P, NB, NB, NH])
        mx = sb("mx", [P, NB, NH])
        sm = sb("sm", [P, NB, NH])
        rc = sb("rc", [P, NB, NH])
        at = sb("at", [P, NB, NB * NH])
        pv = sb("pv", [P, NB, NB, DM])
        o_tok = sb("o_tok", [P, NB, DM])
        oT = sb("oT", [P, NB * P])
        x3 = sb("x3", [P, NB * P])
        ft = sb("ft", [P, NB * P])
        ob = sb("ob", [P, NB * P])

        p_y = ps("p_y", [P, DT, 2, HALF])
        p_tr = ps("p_tr", [P, 2, HALF])
        p_a = ps("p_a", [P, 2, HALF])

        s_xin, s_xres, s_out = sem("x_in_loaded"), sem("x_res_loaded"), sem("out_stored")
        s_w0, s_w1, s_w2 = sem("in_weights"), sem("mamba_weights"), sem("other_weights")
        s_mask = sem("masks_step")
        s_cst = sem("constants_ready")
        s_aexp = sem("a_exp_ready")
        s_taps = sem("tap_weights_ready")
        s_prep = sem("dve_prep_step")
        s_pprep = sem("pe_prep_step")
        s_bn, s_var, s_ve, s_rstd, s_xn = ([sem(f"{name}{a}") for a in (1, 2)] for name in
                                           ("bn_stats_done", "var_ready", "var_eps_ready", "rstd_ready", "xn_ready"))
        s_full = sem("pa_full")
        s_empty = [sem("pa_empty0"), sem("pa_empty1")]
        s_cst_dram = sem("c_stored")
        s_cld = [sem(f"c_loaded{i}") for i in range(NC)]
        s_zmin, s_zexp, s_zln, s_delta, s_du = sem("z_capped"), sem("z_exp_ready"), sem("z_ln_ready"), sem("delta_ready"), sem("du_ready")
        s_u, s_gate = sem("u_ready"), sem("gate_ready")
        s_duB, s_tr, s_dA, s_scan, s_hC, s_sum = sem("duB_ready"), sem("tr_ready"), sem("dA_ready"), sem("scan_done"), sem("hC_ready"), sem("sum_done")
        s_yg = sem("y_gated")
        s_x2 = sem("x2_ready")
        s_stage3 = sem("attn_constants_step")
        c_xa, c_bn = sem("attn_x_loaded"), sem("attn_bn_stats_done")
        c_var = [sem("attn_var3"), sem("attn_var4")]
        c_vep = [sem("attn_ve3"), sem("attn_ve4")]
        c_rs = [sem("attn_rstd3"), sem("attn_rstd4")]
        c_sh = [sem("attn_shift3"), sem("attn_shift4")]
        c_xn = [sem("attn_xn3"), sem("attn_xn4")]
        c_bnd = [sem("attn_bn3"), sem("attn_bn4")]
        c_t1, c_t2, c_t3 = sem("x_turned"), sem("o_turned"), sem("x3_turned")
        c_e1, c_e2, c_e3 = sem("xT3_ready"), sem("oT_ready"), sem("xT4_ready")
        c_proj, c_qk, c_p, c_vp, c_prod, c_L = sem("qkv_projected"), sem("qkT_ready"), sem("p_projected"), sem("v_p_ready"), sem("qk_products"), sem("scores_ready")
        c_th, c_lgp, c_sub, c_exp, c_step = sem("gates_tanh"), sem("scores_read"), sem("logits_ready"), sem("exp_ready"), sem("attention_step")
        c_pvd, c_o, c_wo, c_x3, c_ffn, c_tanh, c_out = sem("pv_products"), sem("o_ready"), sem("wo_ready"), sem("x3_ready"), sem("ffn_ready"), sem("ffn_tanh"), sem("out_tile")
        SCAN0, TR0, HC0, SUM0, YG0 = 8, 8, 16, 4, 2

        block = ctx.enter_context(nc.Block())
        NU = 4 * NS

        A_JOBS = ["xnT0", "xnT1", "conv0", "conv1", "conv2", "conv3", "xdbl0", "xdbl1", "bt0", "bt1",
                  "z0", "z1", "z2", "z3", "gate0", "gate1", "gate2", "gate3", "duT0", "duT1", "duT2", "duT3"]
        D_JOBS = ["out0", "out1", "hT0", "hT1", "ffn0", "ffn1"]
        BOTH = ["out0", "out1", "xnT0", "xnT1", "conv0", "conv1", "conv2", "conv3", "hT0", "hT1", "ffn0", "ffn1"] + A_JOBS[6:]

        def turn_of(b):
            if isinstance(b, int):
                if b == -1:
                    return b, 0, A_JOBS, 0
                if b == 0:
                    return b, len(A_JOBS), A_JOBS, len(A_JOBS) // 2
                if b >= NB - 1:
                    before = 2 * len(A_JOBS) + (NB - 2) * len(BOTH) + (b - NB + 1) * len(D_JOBS)
                    return b, before, D_JOBS, before // 2
            return (b, b * len(BOTH) + 2 * len(A_JOBS) - len(BOTH), BOTH,
                    b * (len(BOTH) // 2) + len(A_JOBS) - len(BOTH) // 2)

        def bank_of(turn, job):
            return turn[2].index(job) % 2

        def wait_full(eng, turn, job):
            eng.wait_ge(s_full, turn[1] + turn[2].index(job) + 1)

        def empty_count(turn, job):
            k = turn[2].index(job)
            return turn[3] + k // 2 + 2

        def wait_emptied(eng, turn, job):
            eng.wait_ge(s_empty[bank_of(turn, job)], empty_count(turn, job))

        def cut(t, start, n):
            return t[:, start:start + n] if isinstance(start, int) else t[:, bass.ds(start, n)]

        def side(b, size):
            return (b % 2) * size

        def xcols(b, c):
            return cut(xs, b * L + c * HALF, HALF)

        def x_at(j):
            v = xs[:, :].rearrange("p (s j c) -> p s j c", s=NB, c=P)
            return v[:, :, j, :] if isinstance(j, int) else v[:, :, bass.ds(j, 1), :].rearrange("p s j c -> p (s j) c")

        def ends(j, ahead):
            return isinstance(j, int) and j + ahead >= TT

        AT = {"out0": (1, 2), "out1": (3, 4), "xnT0": (6,), "xnT1": (7,),
              "conv0": (9, 10, 11, 12), "conv1": (13, 14, 15, 16), "conv2": (17, 18, 19, 20), "conv3": (21, 22, 23, 24),
              "hT0": (25,), "hT1": (26,), "ffn0": (27, 28), "ffn1": (29, 30), "xdbl0": (33, 34), "xdbl1": (35, 36),
              "bt0": (37,), "bt1": (38,), "z0": (39,), "z1": (40,), "z2": (42,), "z3": (43,),
              "gate0": (44,), "gate1": (45,), "gate2": (47,), "gate3": (48,), "duT0": (54,), "duT1": (55,), "duT2": (57,), "duT3": (58,),
              "yg": 1, "ln1": 0, "norm1": (4, 5), "x1": (5, 7), "ln2": 9, "norm2": (14, 15), "x2": (34, 36),
              "silu": 28, "zmin": 46, "exp": 47, "delta": 51, "du": (52, 53)}

        ACT_AFTER = 3
        DVE_AFTER = 3

        NW1 = 10
        NW2 = 3 + TPH + 4 + 3 + NB + NH

        @block.sync
        def _(sp):
            sp.dma_start(x_in[:, :, :], xf[:, 0]).then_inc(s_xin, 16)
            sp.dma_start(w_in[:, :], W_in).then_inc(s_w0, 16)
            sp.dma_start(conv_w_all, conv_wT.partition_broadcast(P)).then_inc(s_w0, 16)
            sp.dma_start(w_x[:, :, :], W_x.rearrange("(t p) n -> p t n", p=P)).then_inc(s_w1, 16)
            sp.dma_start(w_dt[:, :], W_dt).then_inc(s_w1, 16)
            sp.dma_start(w_out[:, :, :], W_out.rearrange("(t p) n -> p t n", p=P)).then_inc(s_w1, 16)

            def load_x_in(b):
                sp.dma_start(x_in[:, :, :], xf[:, b] if isinstance(b, int) else
                             xf[:, bass.ds(b, 1)].rearrange("p s j c -> p (s j) c")).then_inc(s_xin, 16)

            def load_x_res(b):
                sp.dma_start(x_res[:, :, :], xf[:, b] if isinstance(b, int) else
                             xf[:, bass.ds(b, 1)].rearrange("p s j c -> p (s j) c")).then_inc(s_xres, 16)

            def store_c(turn):
                b = turn[0] + 1
                wait_emptied(sp, turn, "xdbl0")
                wait_emptied(sp, turn, "xdbl1")
                sp.dma_start(c_scratch[b] if isinstance(b, int) else c_scratch[bass.ds(b, 1)].rearrange("b n t -> (b n) t"),
                             xdbl[R + NS:XD, :]).then_inc(s_cst_dram, 16)

            def sp_turn(b):
                turn = turn_of(b)
                sp.wait_ge(s_cst_dram, 16 * b + 16)
                sp.nop(nofuse=True)
                for i in range(NS):
                    sp.wait_ge(s_hC, (b * NS + i - NC + 1) * 4 + HC0)
                    row = (c_scratch[b, i, :] if isinstance(b, int) else
                           c_scratch[bass.ds(b, 1), i, :].rearrange("b t -> (b t)"))
                    sp.dma_start(c_all[:, i % NC, :], row.partition_broadcast(P)).then_inc(s_cld[i % NC], 16)
                    if i == 6 and turn[2] is not D_JOBS and not (isinstance(b, int) and b + 2 >= NB):
                        sp.wait_ge(s_xn[0], 2 * b + 4)
                        load_x_in(b + 2)
                    if i == 12 and turn[2] is not D_JOBS:
                        store_c(turn)
                    if i == 14 and not (isinstance(b, int) and b == 0):
                        sp.wait_ge(s_x2, 2 * b)
                        load_x_res(b)

            load_x_res(0)
            sp.wait_ge(s_xn[0], 2)
            load_x_in(1)
            sp.dma_start(f_wT[:, :], ffn_wT).then_inc(s_w2, 16)
            sp.dma_start(f_a1[:, :], ffn_a1).then_inc(s_w2, 16)
            sp.dma_start(f_a2[:, :], ffn_a2).then_inc(s_w2, 16)
            for k in range(TPH):
                sp.dma_start(f_brow[0:1, k, :], ffn_b.rearrange("(a n) -> a n", a=1)).then_inc(s_w2, 16)
            for w, src in ((w_q, Wq), (w_k, Wk), (w_v, Wv), (w_o, Wo)):
                sp.dma_start(w[:, :], src).then_inc(s_w2, 16)
            for w, src in ((bq_col, bq), (bk_col, bk), (bv_col, bv)):
                sp.dma_start(w[:, :], src.rearrange("(p a) -> p a", a=1)).then_inc(s_w2, 16)
            for k in range(NB):
                sp.dma_start(bo_row[0:1, k, :], bo.rearrange("(a n) -> a n", a=1)).then_inc(s_w2, 16)
            for hd in range(NH):
                sp.dma_start(emb[hd * HD:(hd + 1) * HD, :], pos_emb[0, :, 0:NKNOT]).then_inc(s_w2, 16)
            store_c(turn_of(-1))
            for b in range(NB):
                sp_turn(b)

            def load_x(j):
                sp.dma_start(xa[:, :, :], x_at(j)).then_inc(c_xa, 16)

            def store(j):
                sp.wait_ge(c_out, j + 1)
                sp.dma_start(of[:, :, j, :] if isinstance(j, int) else of[:, :, bass.ds(j, 1), :].rearrange("p s j c -> p (s j) c"),
                             ob[:, :].rearrange("p (s c) -> p s c", c=P)).then_inc(s_out, 16)

            sp.wait_ge(s_x2, 2 * NB)
            load_x(0)
            sp.wait_ge(c_xn[0], 1)
            load_x(1)
            for j in range(2):
                sp.wait_ge(c_xn[0], j + 2)
                load_x(j + 2)
            with sp.Fori(2, TT - 2) as j:
                sp.wait_ge(c_xn[0], j + 2)
                load_x(j + 2)
                store(j - 2)
            for j in range(TT - 4, TT):
                store(j)
            sp.wait_ge(s_out, 16 * TT)

        @block.gpsimd
        def _(pool):
            pool.memset(ident[:, :], 0.0).then_inc(s_mask, 1)
            pool.memset(head_mask[:, :], 1.0).then_inc(s_mask, 1)
            pool.memset(ones_row[:, :], 1.0)
            pool.memset(xnT[:, 0:TAPS - 1], 0.0)
            pool.memset(neg_half[:, :], -0.5).then_inc(s_cst, 1)
            pool.wait_ge(s_mask, 2)
            pool.affine_select(out=ident[:, :], in_=ident[:, :], compare_op=ALU.not_equal, fill=1.0,
                               base=0, pattern=[[-1, P]], channel_multiplier=1).then_inc(s_cst, 1)
            pool.affine_select(out=head_mask[:, :], in_=head_mask[:, :], compare_op=ALU.is_ge, fill=0.0,
                               base=0, pattern=[[-HD, NH]], channel_multiplier=1).then_inc(s_mask, 1)
            pool.wait_ge(s_mask, 3)
            pool.affine_select(out=head_mask[:, :], in_=head_mask[:, :], compare_op=ALU.is_ge, fill=0.0,
                               base=HD - 1, pattern=[[HD, NH]], channel_multiplier=-1).then_inc(s_cst, 1)
            pool.wait_ge(s_cst, 3)
            pool.memset(hC[:, 0, 0:1], 0.0).then_inc(s_hC, HC0)

            def rstd_of(a, b):
                pool.wait_ge(s_var[a], b + 1)
                pool.nop(nofuse=True)
                pool.tensor_scalar(var_eps[:, a, :], mv[:, a, :, 1], EPS, None, ALU.add).then_inc(s_ve[a], 1)
                pool.wait_ge(s_ve[a], b + 1)
                pool.nop(nofuse=True)
                pool.tensor_tensor(rstd[:, a, :], var_eps[:, a, :], neg_half[:, :], ALU.pow).then_inc(s_rstd[a], 1)

            def times_u(b, dt):
                pool.wait_ge(s_delta, b * DT + dt + 1)
                pool.tensor_tensor(z_exp[:, dt, :], cut(delta, side(b, DT * L) + dt * L, L), u[:, dt, :], ALU.mult
                                   ).then_inc(s_du, 1)

            def add_ffn(turn, c):
                wait_emptied(pool, turn, f"ffn{c}")
                pool.tensor_tensor(xcols(turn[0] - 1, c), x_res[:, c * TPH:(c + 1) * TPH, :].rearrange("p j c -> p (j c)"),
                                   ffn_t[:, c, :], ALU.add).then_inc(s_x2, 1)

            def pool_turn(b):
                turn = turn_of(b)
                prepare, end = turn[2] is not D_JOBS, turn[2] is not A_JOBS
                for ku in range(NU):
                    i, k = ku // 4, ku % 4
                    half = k // 2
                    if k == 0:
                        pool.wait_ge(s_cld[i % NC], 16 * (b * (NS // NC) + i // NC) + 16)
                    pool.wait_ge(s_scan, b * NU + ku + 1 + SCAN0)
                    pool.wait_ge(s_sum, b * NU + ku - 3 + SUM0)
                    pool.tensor_tensor(hC[:, k, :], h[:, k, :], c_all[:, i % NC, half * HALF:(half + 1) * HALF],
                                       ALU.mult).then_inc(s_hC, 1)
                    if prepare:
                        if ku == AT["ln1"] + 2:
                            rstd_of(0, b + 1)
                        for dt in range(DT):
                            if ku == AT["du"][dt]:
                                times_u(b + 1, dt)
                    if end:
                        if ku == AT["ln2"] + 2:
                            rstd_of(1, b - 1)
                        for c in range(2):
                            if ku == AT["x2"][c]:
                                add_ffn(turn, c)

            rstd_of(0, 0)
            pool_turn(0)
            with pool.Fori(1, NB - 1) as b:
                pool_turn(b)
            pool_turn(NB - 1)
            rstd_of(1, NB - 1)
            for c in range(2):
                add_ffn(turn_of(NB), c)

            def attn_rstd(a, j, first=False):
                pool.wait_ge(c_var[a], j + 1)
                if not first:
                    pool.wait_ge(c_xn[a], j)
                pool.nop(nofuse=True)
                pool.tensor_scalar(c_negm[:, a, :], c_mv[:, a, :, 0], -1.0, None, ALU.mult)
                pool.tensor_scalar(c_ve[:, a, :], c_mv[:, a, :, 1], EPS, None, ALU.add).then_inc(c_vep[a], 1)
                pool.wait_ge(c_vep[a], j + 1)
                pool.nop(nofuse=True)
                pool.tensor_tensor(c_rstd[:, a, :], c_ve[:, a, :], neg_half[:, 0:NB], ALU.pow).then_inc(c_rs[a], 1)
                pool.wait_ge(c_rs[a], j + 1)
                pool.nop(nofuse=True)
                pool.tensor_tensor(c_shift[:, a, :], c_negm[:, a, :], c_rstd[:, a, :], ALU.mult).then_inc(c_sh[a], 1)

            def products(j, first=False):
                pool.wait_ge(c_qk, j + 1)
                if not first:
                    pool.wait_ge(c_L, j)
                pool.tensor_tensor(qk[:, :, :, :], qT[:, :, :].unsqueeze(2).to_broadcast([P, NB, NB, P]),
                                   kT[:, :, :].unsqueeze(1).to_broadcast([P, NB, NB, P]), ALU.mult).then_inc(c_prod, 1)

            def finish(j, first=False):
                pool.wait_ge(c_tanh, j + 1)
                if not first:
                    pool.wait_ge(s_out, 16 * j)
                pool.tensor_tensor(ob[:, :], x3[:, :], ft[:, :], ALU.add).then_inc(c_out, 1)

            def pool_step(j, first=False, second=False, finishing=True, first_out=False):
                if not ends(j, 1):
                    products(j + 1)
                if not ends(j, 2):
                    attn_rstd(0, j + 2)
                if finishing:
                    finish(j - 2, first=first_out)
                if not first:
                    attn_rstd(1, j - 1, first=second)

            attn_rstd(0, 0, first=True)
            products(0, first=True)
            attn_rstd(0, 1)
            pool_step(0, first=True, finishing=False)
            pool_step(1, second=True, finishing=False)
            pool_step(2, first_out=True)
            with pool.Fori(3, TT - 2) as j:
                pool_step(j)
            pool_step(TT - 2)
            pool_step(TT - 1)
            finish(TT - 2)
            attn_rstd(1, TT - 1)
            finish(TT - 1)

        @block.scalar
        def _(act):
            for col, src in ((conv_bias, conv_b), (dt_bias, b_dt), (d_col, D)):
                for dt in range(DT):
                    act.dma_start(col[:, dt:dt + 1], src[dt * P:(dt + 1) * P].rearrange("(p a) -> p a", a=1)).then_inc(s_w1, 16)
            act.dma_start(a_log[:, :].rearrange("p (t n) -> p t n", n=NS), A_log.rearrange("(t p) n -> p t n", p=P)).then_inc(s_w1, 16)
            act.wait_ge(s_w1, 16 * NW1)
            nc.scalar.activation(a_exp[:, :], a_log[:, :], ACT.Exp).then_inc(s_aexp, 1)

            def settle(b):
                if not isinstance(b, int):
                    act.nop(nofuse=True)

            def take_out(turn, job, dst, func, **kw):
                bank = bank_of(turn, job)
                wait_full(act, turn, job)
                if job[:2] in ("ga", "bt", "du"):
                    settle(turn[0])
                src = p_a[:, bank, :]
                if job[:2] == "bt":
                    src = src.rearrange("p (t n) -> p t n", n=P)[:, :, R:R + NS]
                nc.scalar.activation(dst, src, func, **kw).then_inc(s_empty[bank], 1)

            def xnT_out(turn, c):
                take_out(turn, f"xnT{c}", xnT[:, TAPS - 1 + c * HALF:TAPS - 1 + (c + 1) * HALF], ACT.Copy)

            def conv_out(turn, k):
                c, dt = k // 2, k % 2
                take_out(turn, f"conv{k}", u[:, dt, c * HALF:(c + 1) * HALF], ACT.Identity, bias=conv_bias[:, dt:dt + 1])

            def gate_out(turn, k):
                c, dt = k // 2, k % 2
                take_out(turn, f"gate{k}", cut(gate, side(turn[0] + 1, DT * L) + dt * L + c * HALF, HALF), ACT.Copy)

            def bt_out(turn, c):
                take_out(turn, f"bt{c}", cut(b_tok, side(turn[0] + 1, TT * NS) + c * TPH * NS, TPH * NS
                                             ).rearrange("p (t n) -> p t n", n=NS), ACT.Copy)

            def duT_out(turn, k):
                take_out(turn, f"duT{k}", cut(duT, side(turn[0] + 1, TT * DI) + 2 * k * DI, 2 * DI), ACT.Copy)

            def hT_out(turn, c):
                take_out(turn, f"hT{c}", hT[:, c * HALF:(c + 1) * HALF], ACT.Copy)

            def ffn_out_half(turn, c):
                take_out(turn, f"ffn{c}", ffn_t[:, c, :], ACT.Tanh)

            def silu_u(turn):
                for dt in range(DT):
                    if dt == 0:
                        for k in range(4):
                            wait_emptied(act, turn, f"conv{k}")
                    nc.scalar.activation(u[:, dt, :], u[:, dt, :], ACT.Silu).then_inc(s_u, 1)

            def silu_gate(turn):
                b = turn[0]
                before = turn_of(b - 1) if isinstance(b, int) else None
                for dt in range(DT):
                    if dt == 0:
                        if before is not None:
                            wait_emptied(act, before, "gate2")
                            wait_emptied(act, before, "gate3")
                        else:
                            act.wait_ge(s_empty[0], turn[3] - 1)
                            act.wait_ge(s_empty[1], turn[3] - 1)
                        settle(b)
                    gc = cut(gate, side(b, DT * L) + dt * L, L)
                    nc.scalar.activation(gc, gc, ACT.Silu).then_inc(s_gate, 1)

            def softplus(b):
                for dt in range(DT):
                    act.wait_ge(s_zmin, b * DT + dt + 1)
                    nc.scalar.activation(z_exp[:, dt, :], z_exp[:, dt, :], ACT.Exp).then_inc(s_zexp, 1)
                for dt in range(DT):
                    act.wait_ge(s_zexp, b * DT + dt + 1)
                    nc.scalar.activation(z_exp[:, dt, :], z_exp[:, dt, :], ACT.Ln, bias=1.0).then_inc(s_zln, 1)

            def act_turn(b):
                turn = turn_of(b)
                prepare, end = turn[2] is not D_JOBS, turn[2] is not A_JOBS

                def spread(i, half):
                    act.wait_ge(s_tr, b * NU + i * 4 + 2 * half - 6 + TR0)
                    settle(b)
                    for t in range(TPH):
                        last = nc.scalar.activation(duB[:, 2 * (i % 2) + half, t, :], cut(duT, side(b, TT * DI) + (half * TPH + t) * DI, DI), ACT.Copy,
                                                    scale=cut(b_tok, side(b, TT * NS) + (half * TPH + t) * NS + i, 1))
                    last.then_inc(s_duB, 1)

                def pieces(since, until):
                    def due(at):
                        return since < at <= until
                    if end:
                        for c in range(2):
                            if due(AT[f"hT{c}"][-1] + ACT_AFTER):
                                hT_out(turn, c)
                            if due(AT[f"ffn{c}"][-1] + ACT_AFTER):
                                ffn_out_half(turn, c)
                    if prepare:
                        for c in range(2):
                            if due(AT[f"xnT{c}"][-1] + ACT_AFTER):
                                xnT_out(turn, c)
                        for k in range(4):
                            if due(AT[f"conv{k}"][-1] + ACT_AFTER):
                                conv_out(turn, k)
                    if due(AT["silu"]):
                        if prepare:
                            silu_u(turn)
                        silu_gate(turn)
                    if prepare:
                        for c in range(2):
                            if due(AT[f"bt{c}"][-1] + ACT_AFTER):
                                bt_out(turn, c)
                        if due(AT["exp"]):
                            softplus(b + 1)
                        for k in range(4):
                            if due(AT[f"gate{k}"][-1] + ACT_AFTER):
                                gate_out(turn, k)
                        for k in range(4):
                            if due(AT[f"duT{k}"][-1] + ACT_AFTER):
                                duT_out(turn, k)

                for i in range(NS):
                    spread(i, 0)
                    pieces(4 * i - 6 if i else -99, 4 * i - 5)
                    act.wait_ge(s_scan, b * NU + (i - 1) * 4 + SCAN0)
                    settle(b)
                    for dt in range(DT):
                        nc.scalar.activation(dA[:, i % NDA, dt, :], cut(delta, side(b, DT * L) + dt * L, L), ACT.Exp,
                                             scale=a_neg[:, dt * NS + i:dt * NS + i + 1]).then_inc(s_dA, 1)
                    pieces(4 * i - 5, 4 * i - 4)
                    spread(i, 1)
                    pieces(4 * i - 4, 4 * i - 2)
                pieces(4 * NS - 6, 99)
                if prepare:
                    wait_emptied(act, turn, "duT2")
                    wait_emptied(act, turn, "duT3")
                    settle(b)

            start = turn_of(-1)
            for c in range(2):
                xnT_out(start, c)
            for k in range(4):
                conv_out(start, k)
            silu_u(start)
            for c in range(2):
                bt_out(start, c)
            for k in range(2):
                gate_out(start, k)
            softplus(0)
            for k in range(2, 4):
                gate_out(start, k)
            for k in range(4):
                duT_out(start, k)
            wait_emptied(act, start, "duT2")
            wait_emptied(act, start, "duT3")
            act_turn(0)
            with act.Fori(1, NB - 1) as b:
                act_turn(b)
            act_turn(NB - 1)
            for c in range(2):
                hT_out(turn_of(NB), c)
            for c in range(2):
                ffn_out_half(turn_of(NB), c)

            def normalise(a, src, dst, j):
                act.wait_ge(c_sh[a], j + 1)
                for t in range(NB):
                    last = nc.scalar.activation(dst[:, t, :], src[:, t * P:(t + 1) * P], ACT.Identity,
                                                scale=c_rstd[:, a, t:t + 1], bias=c_shift[:, a, t:t + 1])
                last.then_inc(c_xn[a], 1)

            def exps(j):
                act.wait_ge(c_sub, j + 1)
                nc.scalar.activation(lg[:, :, :, :], lg[:, :, :, :], ACT.Exp).then_inc(c_exp, 1)

            def turned(full, dst, done, j):
                act.wait_ge(full, j + 1)
                nc.scalar.activation(dst[:, :], p_tr[:, 1, :], ACT.Copy).then_inc(done, 1)

            def qk_out(j):
                act.wait_ge(c_proj, j + 1)
                nc.scalar.activation(qT[:, :, :].rearrange("p s t -> p (s t)"), p_y[:, 0, 0, :], ACT.Identity, bias=bq_col[:, :])
                nc.scalar.activation(kT[:, :, :].rearrange("p s t -> p (s t)"), p_y[:, 0, 1, :], ACT.Identity, bias=bk_col[:, :]
                                     ).then_inc(c_qk, 1)

            def vp_out(j):
                act.wait_ge(c_p, j + 1)
                settle(j)
                nc.scalar.activation(cut(vt, side(j, NB * DM), NB * DM), p_y[:, 1, 0, :], ACT.Copy)
                nc.scalar.activation(cut(pk, side(j, NB * PW), NB * PW).rearrange("p (m s h) -> p m s h", s=NB, h=NH),
                                     p_y[:, 1, 1, 0:NB * PW].rearrange("p (s m h) -> p m s h", s=NB, h=NH), ACT.Copy
                                     ).then_inc(c_vp, 1)

            def gates(j):
                act.wait_ge(c_L, j + 1)
                nc.scalar.activation(g[:, :, :, :].rearrange("p s t h -> p (s t h)"), p_tr[:, 0, 0:NB * NB * NH], ACT.Tanh,
                                     scale=0.5 * SCALE).then_inc(c_th, 1)

            def ffn_out(j, first=False):
                act.wait_ge(c_ffn, j + 1)
                if not first:
                    act.wait_ge(c_out, j)
                nc.scalar.activation(ft[:, :], p_a[:, 1, :], ACT.Tanh).then_inc(c_tanh, 1)

            def act_step(j, first=False, finishing=True, first_out=False):
                if not ends(j, 1):
                    turned(c_t1, xT3, c_e1, j + 1)
                    qk_out(j + 1)
                if not first:
                    turned(c_t2, oT, c_e2, j - 1)
                if finishing:
                    normalise(1, x3, xn4, j - 2)
                exps(j)
                if finishing:
                    turned(c_t3, xT4, c_e3, j - 2)
                if not ends(j, 1):
                    vp_out(j + 1)
                if not ends(j, 2):
                    normalise(0, xaf, xn3, j + 2)
                if finishing:
                    ffn_out(j - 2, first=first_out)
                if not ends(j, 1):
                    gates(j + 1)

            xaf = xa[:, :, :].rearrange("p s c -> p (s c)")
            normalise(0, xaf, xn3, 0)
            turned(c_t1, xT3, c_e1, 0)
            qk_out(0)
            vp_out(0)
            gates(0)
            normalise(0, xaf, xn3, 1)
            act_step(0, first=True, finishing=False)
            act_step(1, finishing=False)
            act_step(2, first_out=True)
            with act.Fori(3, TT - 2) as j:
                act_step(j)
            act_step(TT - 2)
            act_step(TT - 1)
            turned(c_t2, oT, c_e2, TT - 1)
            normalise(1, x3, xn4, TT - 2)
            turned(c_t3, xT4, c_e3, TT - 2)
            ffn_out(TT - 2)
            normalise(1, x3, xn4, TT - 1)
            turned(c_t3, xT4, c_e3, TT - 1)
            ffn_out(TT - 1)

        @block.vector
        def _(dve):
            def ln_stats(a, xb, b, part):
                for j in range(part * TPH, (part + 1) * TPH):
                    last = nc.vector.bn_stats(stats[:, a, j, :], xb[:, j, :])
                if part:
                    last.then_inc(s_bn[a], 1)
                    dve.wait_ge(s_bn[a], b + 1)
                    dve.nop(nofuse=True)
                    for j in range(TT):
                        last = nc.vector.bn_aggr(mv[:, a, j, :], stats[:, a, j, :])
                    last.then_inc(s_var[a], 1)

            def ln_norm(a, xb, b, c):
                if c == 0:
                    dve.wait_ge(s_rstd[a], b + 1)
                for j in range(c * TPH, (c + 1) * TPH):
                    last = nc.vector.tensor_scalar(xn[:, a, j, :], xb[:, j, :], mv[:, a, j, 0:1], rstd[:, a, j:j + 1],
                                                   ALU.subtract, ALU.mult)
                last.then_inc(s_xn[a], 1)

            def ln1_stats(b, part):
                if part == 0:
                    dve.wait_ge(s_xin, 16 * b + 16)
                    dve.nop(nofuse=True)
                ln_stats(0, x_in, b, part)

            def ln2_stats(turn, part):
                if part == 0:
                    for c in range(2):
                        wait_emptied(dve, turn, f"out{c}")
                    dve.nop(nofuse=True)
                ln_stats(1, x_res, turn[0] - 1, part)

            def xdbl_out(turn, c):
                bank = bank_of(turn, f"xdbl{c}")
                wait_full(dve, turn, f"xdbl{c}")
                nc.vector.tensor_copy(xdbl[:, c * HALF:(c + 1) * HALF], p_a[0:XD, bank, :]).then_inc(s_empty[bank], 1)

            def z_out(turn, k):
                c, dt = k // 2, k % 2
                bank = bank_of(turn, f"z{k}")
                wait_full(dve, turn, f"z{k}")
                nc.vector.tensor_scalar(cut(delta, side(turn[0] + 1, DT * L) + dt * L + c * HALF, HALF), p_a[:, bank, :],
                                        dt_bias[:, dt:dt + 1], None, ALU.add).then_inc(s_empty[bank], 1)

            def z_min(turn):
                for k in range(2, 4):
                    wait_emptied(dve, turn, f"z{k}")
                for dt in range(DT):
                    nc.vector.tensor_scalar(z_exp[:, dt, :], cut(delta, side(turn[0] + 1, DT * L) + dt * L, L), SP_CAP, None,
                                            ALU.min).then_inc(s_zmin, 1)

            def z_max(b, dt):
                dve.wait_ge(s_zln, b * DT + dt + 1)
                d = cut(delta, side(b, DT * L) + dt * L, L)
                nc.vector.tensor_tensor(d, d, z_exp[:, dt, :], ALU.max).then_inc(s_delta, 1)

            def gate_y(b):
                dve.wait_ge(s_sum, b * NU + NU + SUM0)
                dve.wait_ge(s_gate, b * DT + DT)
                for dt in range(DT):
                    nc.vector.tensor_tensor(yg[:, dt, :], p_y[:, dt, :, :].rearrange("p a t -> p (a t)"),
                                            cut(gate, side(b, DT * L) + dt * L, L), ALU.mult).then_inc(s_yg, 1)

            def add_out(turn, c):
                b = turn[0] - 1
                bank = bank_of(turn, f"out{c}")
                if c == 0:
                    dve.wait_ge(s_xres, 16 * b + 16)
                wait_full(dve, turn, f"out{c}")
                xh = x_res[:, c * TPH:(c + 1) * TPH, :].rearrange("p j c -> p (j c)")
                nc.vector.tensor_tensor(xh, p_a[:, bank, :], xh, ALU.add).then_inc(s_empty[bank], 1)

            def dve_turn(b):
                turn = turn_of(b)
                prepare, end = turn[2] is not D_JOBS, turn[2] is not A_JOBS
                for ku in range(NU):
                    i, k = ku // 4, ku % 4
                    half, dt = k // 2, k % 2
                    if half == 0:
                        dve.wait_ge(s_dA, (b * NS + i) * DT + dt + 1)
                    dve.wait_ge(s_tr, b * NU + ku + 1 + TR0)
                    dve.wait_ge(s_hC, b * NU + ku - 3 + HC0)
                    dve.wait_ge(s_scan, b * NU + ku - 1 + SCAN0)
                    nc.vector.tensor_tensor_scan(h[:, k, :], dA[:, i % NDA, dt, half * HALF:(half + 1) * HALF],
                                                 p_tr[:, k % 2, :],
                                                 0.0 if half == 0 else h[:, dt, HALF - 1:HALF],
                                                 ALU.mult, ALU.add).then_inc(s_scan, 1)
                    if end:
                        if ku == AT["yg"]:
                            gate_y(b - 1)
                        for c in range(2):
                            if ku == AT["x1"][c]:
                                add_out(turn, c)
                            if ku == AT["ln2"] + c:
                                ln2_stats(turn, c)
                            if ku == AT["norm2"][c]:
                                ln_norm(1, x_res, b - 1, c)
                    if prepare:
                        for c in range(2):
                            if ku == AT["ln1"] + c:
                                ln1_stats(b + 1, c)
                            if ku == AT["norm1"][c]:
                                ln_norm(0, x_in, b + 1, c)
                            if ku == AT[f"xdbl{c}"][-1] + DVE_AFTER:
                                xdbl_out(turn, c)
                        for j in range(4):
                            if ku == AT[f"z{j}"][-1] + DVE_AFTER:
                                z_out(turn, j)
                        if ku == AT["zmin"]:
                            z_min(turn)
                        for dt in range(DT):
                            if ku == AT["delta"] + dt:
                                z_max(b + 1, dt)

            start = turn_of(-1)
            for c in range(2):
                ln1_stats(0, c)
            for c in range(2):
                ln_norm(0, x_in, 0, c)
            dve.wait_ge(s_w0, 16 * 2)
            nc.vector.tensor_tensor(w_tap[:, :, :], conv_w_all,
                                    w_in[:, 0:DI].unsqueeze(1).to_broadcast([P, TAPS, DI]), ALU.mult).then_inc(s_taps, 1)
            dve.wait_ge(s_aexp, 1)
            nc.vector.tensor_scalar(a_neg[:, :], a_exp[:, :], -1.0, None, ALU.mult)
            dve.wait_ge(s_cst, 3)
            for dt in range(DT):
                nc.vector.tensor_scalar(d_diag[:, dt, :], ident[:, :], d_col[:, dt:dt + 1], None, ALU.mult)
            nc.vector.memset(stats[:, 0, 0:1], 0.0).then_inc(s_prep, 1)
            dve.wait_ge(s_prep, 1)
            nc.vector.memset(stats[:, 0, 0:1], 0.0).then_inc(s_scan, SCAN0)
            for c in range(2):
                xdbl_out(start, c)
            for k in range(4):
                z_out(start, k)
            z_min(start)
            dve.wait_ge(s_pprep, 1)
            nc.vector.tensor_copy(f_pT[:, :], p_tr[:, 0, 0:DM]).then_inc(s_prep, 1)
            dve.wait_ge(s_pprep, 2)
            nc.vector.tensor_copy(f_w[:, :], p_tr[:, 1, 0:DM]).then_inc(s_prep, 1)

            dve.wait_ge(s_w2, 16 * NW2)
            nc.vector.tensor_copy(emb_step[:, 0:1], emb[:, 0:1])
            nc.vector.tensor_tensor(emb_step[:, 1:NKNOT], emb[:, 1:NKNOT], emb[:, 0:NKNOT - 1], ALU.subtract).then_inc(s_stage3, 1)
            dve.wait_ge(s_stage3, 1)
            for m in range(1, NB):
                nc.vector.scalar_tensor_tensor(emb_step[:, 0:1], emb_step[:, m + 1:m + 2], float(-m), emb_step[:, 0:1], ALU.mult, ALU.add
                                               ).then_inc(s_stage3, 1)
                dve.wait_ge(s_stage3, 1 + m)
            nc.vector.tensor_tensor(emb_blocks[:, :, :], emb_step[:, :].unsqueeze(2).to_broadcast([P, NKNOT, NH]),
                                    head_mask[:, :].unsqueeze(1).to_broadcast([P, NKNOT, NH]), ALU.mult).then_inc(s_stage3, 1)
            dve.wait_ge(s_pprep, 3)
            nc.vector.tensor_tensor(bo_row[:, :, :], bo_row[:, :, :], p_tr[0:1, 0, HALF // 2:HALF // 2 + DM].unsqueeze(1).to_broadcast([1, NB, DM]),
                                    ALU.add).then_inc(s_stage3, 1)
            for dt in range(DT):
                z_max(0, dt)
            for dt in range(DT):
                dve.wait_ge(s_delta, dt + 1)
                nc.vector.tensor_tensor(z_exp[:, dt, :], delta[:, dt * L:(dt + 1) * L], u[:, dt, :], ALU.mult).then_inc(s_du, 1)
            dve_turn(0)
            with dve.Fori(1, NB - 1) as b:
                dve_turn(b)
            dve_turn(NB - 1)
            gate_y(NB - 1)
            for c in range(2):
                add_out(turn_of(NB), c)
            for c in range(2):
                ln2_stats(turn_of(NB), c)
            for c in range(2):
                ln_norm(1, x_res, NB - 1, c)

            NSTEP = 13

            def attn_stats(a, xb, j, first=False):
                for t in range(NB):
                    last = nc.vector.bn_stats(c_stats[:, a, t, :], xb[:, t * P:(t + 1) * P])
                last.then_inc(c_bnd[a], 1)
                dve.wait_ge(c_bnd[a], j + 1)
                if not first:
                    dve.wait_ge(c_sh[a], j)
                dve.nop(nofuse=True)
                for t in range(NB):
                    last = nc.vector.bn_aggr(c_mv[:, a, t, :], c_stats[:, a, t, :])
                last.then_inc(c_var[a], 1)

            xaf = xa[:, :, :].rearrange("p s c -> p (s c)")

            def stats3(j, first=False):
                dve.wait_ge(c_xa, 16 * j + 16)
                dve.nop(nofuse=True)
                attn_stats(0, xaf, j, first)

            def residual(j, first=False):
                dve.wait_ge(c_wo, j + 1)
                if not first:
                    dve.wait_ge(c_out, j)
                    dve.wait_ge(c_xn[1], j)
                nc.vector.tensor_tensor(x3[:, :].rearrange("p (s c) -> p s c", c=P), p_a[:, 0, :].rearrange("p (s c) -> p s c", c=P),
                                        x_at(j), ALU.add).then_inc(c_x3, 1)
                dve.wait_ge(c_x3, j + 1)
                dve.nop(nofuse=True)
                attn_stats(1, x3, j, first)

            def logits(j):
                k = [0]

                def link(ins):
                    k[0] += 1
                    ins.then_inc(c_step, 1)
                    dve.wait_ge(c_step, j * NSTEP + k[0])

                gf = g[:, :, :, :].rearrange("p s t h -> p (s t h)")
                lf = lg[:, :, :, :].rearrange("p s t h -> p (s t h)")
                dve.wait_ge(c_th, j + 1)
                link(nc.vector.tensor_scalar(gf, gf, 0.5, 0.5, ALU.mult, ALU.add))
                for t in range(NB - 2, -1, -1):
                    link(nc.vector.tensor_tensor(g[:, :, t, :], g[:, :, t, :], g[:, :, t + 1, :], ALU.add))
                for m in range(NB):
                    last = nc.vector.tensor_scalar(cl[:, m, :], gf, float(m), float(m + 1), ALU.max, ALU.min)
                link(last)
                dve.wait_ge(c_vp, j + 1)
                pieces = cut(pk, side(j, NB * PW), NB * PW)
                for a in range(NB):
                    last = nc.vector.scalar_tensor_tensor(lg[:, a, :, :], p_tr[:, 0, a * NB * NH:(a + 1) * NB * NH].rearrange("p (t h) -> p t h", h=NH),
                                                          SCALE, pieces[:, a * NH:(a + 1) * NH].unsqueeze(1).to_broadcast([P, NB, NH]),
                                                          ALU.mult, ALU.add)
                last.then_inc(c_lgp, 1)
                ca = cl[:, :, :].rearrange("p m (s t h) -> p (m s) t h", s=NB, h=NH)
                link(nc.vector.tensor_tensor(ca, ca, pieces[:, NB * NH:NB * PW].rearrange("p (a h) -> p a h", h=NH).unsqueeze(2).to_broadcast([P, NB * NB, NB, NH]),
                                             ALU.mult))
                nc.vector.tensor_tensor(cl[:, 0, :], cl[:, 0, :], cl[:, 1, :], ALU.add)
                link(nc.vector.tensor_tensor(cl[:, 2, :], cl[:, 2, :], cl[:, 3, :], ALU.add))
                link(nc.vector.tensor_tensor(cl[:, 0, :], cl[:, 0, :], cl[:, 2, :], ALU.add))
                link(nc.vector.tensor_tensor(lf, lf, cl[:, 0, :], ALU.add))
                link(nc.vector.tensor_reduce(mx[:, :, :], lg[:, :, :, :].rearrange("p s t h -> p s h t"), AX.X, ALU.max))
                nc.vector.tensor_tensor(lg[:, :, :, :], lg[:, :, :, :], mx[:, :, :].unsqueeze(2).to_broadcast([P, NB, NB, NH]),
                                        ALU.subtract).then_inc(c_sub, 1)
                return k[0]

            def weights(j, k0):
                k = [k0]

                def link(ins):
                    k[0] += 1
                    ins.then_inc(c_step, 1)
                    dve.wait_ge(c_step, j * NSTEP + k[0])

                dve.wait_ge(c_exp, j + 1)
                link(nc.vector.tensor_reduce(sm[:, :, :], lg[:, :, :, :].rearrange("p s t h -> p s h t"), AX.X, ALU.add))
                link(nc.vector.reciprocal(rc[:, :, :], sm[:, :, :]))
                link(nc.vector.tensor_tensor(at[:, :, :].rearrange("p s (t h) -> p s t h", h=NH), lg[:, :, :, :],
                                             rc[:, :, :].unsqueeze(2).to_broadcast([P, NB, NB, NH]), ALU.mult))
                nc.vector.tensor_tensor(pv[:, :, :, :].rearrange("p s t (h d) -> p s (t h) d", d=HD),
                                        at[:, :, :].unsqueeze(3).to_broadcast([P, NB, NB * NH, HD]),
                                        cut(vt, side(j, NB * DM), NB * DM).rearrange("p (a d) -> p a d", d=HD).unsqueeze(1).to_broadcast([P, NB, NB * NH, HD]),
                                        ALU.mult).then_inc(c_pvd, 1)
                assert k[0] == NSTEP, k[0]

            def mix(j):
                dve.wait_ge(c_pvd, j + 1)
                nc.vector.tensor_reduce(o_tok[:, :, :], pv[:, :, :, :].rearrange("p s t c -> p s c t"), AX.X, ALU.add).then_inc(c_o, 1)

            def dve_step(j, first=False, second=False):
                k = logits(j)
                if not ends(j, 2):
                    stats3(j + 2)
                weights(j, k)
                mix(j)
                if not first:
                    residual(j - 1, first=second)

            stats3(0, first=True)
            stats3(1)
            dve_step(0, first=True)
            dve_step(1, second=True)
            with dve.Fori(2, TT - 2) as j:
                dve_step(j)
            dve_step(TT - 2)
            dve_step(TT - 1)
            residual(TT - 1)

        @block.tensor
        def _(pe):
            pe.wait_ge(s_cst, 3)
            nc.tensor.matmul(p_tr[:, 0, 0:2], ident[:, :], ident[:, 0:2], start=True, stop=True).then_inc(s_tr, TR0)
            pe.sem_inc(s_sum, SUM0)
            pe.sem_inc(s_yg, YG0)
            for bank in range(2):
                pe.sem_inc(s_empty[bank], 1)

            def start_job(turn, job):
                k = turn[2].index(job)
                pe.wait_ge(s_empty[k % 2], turn[3] + k // 2 + 1)
                return p_a[:, k % 2, :]

            def bank(turn, job):
                return p_a[:, bank_of(turn, job), :]

            def transposes(turn, job, src, cols=P):
                o = start_job(turn, job)
                for t, a in enumerate(src):
                    last = nc.tensor.transpose(o[:, t * P:t * P + cols], a, ident[0:cols, 0:cols])
                last.then_inc(s_full, 1)

            def do_xnT(turn, c):
                pe.wait_ge(s_xn[0], 2 * (turn[0] + 1) + c + 1)
                transposes(turn, f"xnT{c}", [xn[:, 0, c * TPH + t, :] for t in range(TPH)])

            def do_conv(turn, k, tap):
                c, dt = k // 2, k % 2
                if tap == 0:
                    wait_emptied(pe, turn, f"xnT{c}")
                    start_job(turn, f"conv{k}")
                mm = nc.tensor.matmul(bank(turn, f"conv{k}"), w_tap[:, tap, dt * P:(dt + 1) * P],
                                      xnT[:, c * HALF + tap:c * HALF + tap + HALF], start=(tap == 0), stop=(tap == TAPS - 1))
                if tap == TAPS - 1:
                    mm.then_inc(s_full, 1)

            def do_gate(turn, k):
                c, dt = k // 2, k % 2
                nc.tensor.matmul(start_job(turn, f"gate{k}"), w_in[:, DI + dt * P:DI + (dt + 1) * P],
                                 xnT[:, TAPS - 1 + c * HALF:TAPS - 1 + (c + 1) * HALF],
                                 start=True, stop=True).then_inc(s_full, 1)

            def do_xdbl(turn, c, dt):
                if dt == 0:
                    start_job(turn, f"xdbl{c}")
                pe.wait_ge(s_u, (turn[0] + 1) * DT + dt + 1)
                mm = nc.tensor.matmul(bank(turn, f"xdbl{c}")[0:XD, :], w_x[:, dt, :], u[:, dt, c * HALF:(c + 1) * HALF],
                                      start=(dt == 0), stop=(dt == DT - 1))
                if dt == DT - 1:
                    mm.then_inc(s_full, 1)

            def do_bt(turn, c):
                wait_emptied(pe, turn, f"xdbl{c}")
                transposes(turn, f"bt{c}", [xdbl[:, (c * TPH + t) * P:(c * TPH + t + 1) * P] for t in range(TPH)], XD)

            def do_z(turn, k):
                c, dt = k // 2, k % 2
                nc.tensor.matmul(start_job(turn, f"z{k}"), w_dt[:, dt * P:(dt + 1) * P], xdbl[0:R, c * HALF:(c + 1) * HALF],
                                 start=True, stop=True).then_inc(s_full, 1)

            def do_duT(turn, k):
                pe.wait_ge(s_du, (turn[0] + 1) * DT + DT)
                transposes(turn, f"duT{k}", [z_exp[:, dt, (2 * k + t) * P:(2 * k + t + 1) * P] for t in range(2) for dt in range(DT)])

            def do_out(turn, c, part):
                if part == 0:
                    pe.wait_ge(s_yg, (turn[0] - 1) * DT + DT + YG0)
                    start_job(turn, f"out{c}")
                o = bank(turn, f"out{c}")
                for t in range(2 * part, 2 * part + 2):
                    for dt in range(DT):
                        last = nc.tensor.matmul(o[:, t * P:(t + 1) * P], yg[:, dt, (c * TPH + t) * P:(c * TPH + t + 1) * P],
                                                w_out[:, dt, :], start=(dt == 0), stop=(dt == DT - 1))
                if part:
                    last.then_inc(s_full, 1)

            def do_hT(turn, c):
                pe.wait_ge(s_xn[1], 2 * (turn[0] - 1) + c + 1)
                transposes(turn, f"hT{c}", [xn[:, 1, c * TPH + t, :] for t in range(TPH)])

            def do_ffn(turn, c, part):
                if part == 0:
                    wait_emptied(pe, turn, f"hT{c}")
                    nc.tensor.matmul(start_job(turn, f"ffn{c}"), ones_row[:, :], f_brow[:, :, :].rearrange("a t n -> a (t n)"),
                                     start=True, stop=False, skip_group_check=True)
                    return
                o = bank(turn, f"ffn{c}")
                for t in range(TPH):
                    last = nc.tensor.matmul(o[:, t * P:(t + 1) * P], hT[:, (c * TPH + t) * P:(c * TPH + t + 1) * P],
                                            f_w[:, :], start=False, stop=True, skip_group_check=True)
                last.then_inc(s_full, 1)

            def pe_turn(b):
                turn = turn_of(b)
                prepare, end = turn[2] is not D_JOBS, turn[2] is not A_JOBS

                def turn_back(ku):
                    k = ku % 4
                    half, dt = k // 2, k % 2
                    pe.wait_ge(s_duB, (b * NS + ku // 4) * 2 + half + 1)
                    pe.wait_ge(s_scan, b * NU + ku - 1 + SCAN0)
                    for t in range(TPH):
                        last = nc.tensor.transpose(p_tr[:, k % 2, t * P:(t + 1) * P], duB[:, 2 * (ku // 4 % 2) + half, t, dt * P:(dt + 1) * P], ident[:, :])
                    last.then_inc(s_tr, 1)

                LAG = 3
                for ku in range(LAG):
                    turn_back(ku)
                for dt in range(DT):
                    pe.wait_ge(s_yg, (b - 1) * DT + dt + 1 + YG0)
                    for c in range(2):
                        nc.tensor.matmul(p_y[:, dt, c, :], d_diag[:, dt, :], u[:, dt, c * HALF:(c + 1) * HALF],
                                         start=True, stop=False, skip_group_check=True)
                for ku in range(NU):
                    k = ku % 4
                    if ku + LAG < NU:
                        turn_back(ku + LAG)
                    pe.wait_ge(s_hC, b * NU + ku + 1 + HC0)
                    nc.tensor.matmul(p_y[:, k % 2, k // 2, :], ident[:, :], hC[:, k, :], start=False, stop=(ku >= NU - 4),
                                     skip_group_check=True).then_inc(s_sum, 1)
                    if end:
                        for c in range(2):
                            if ku in AT[f"out{c}"]:
                                do_out(turn, c, AT[f"out{c}"].index(ku))
                    if prepare:
                        for c in range(2):
                            if ku in AT[f"xnT{c}"]:
                                do_xnT(turn, c)
                        for j in range(4):
                            if ku in AT[f"conv{j}"]:
                                do_conv(turn, j, AT[f"conv{j}"].index(ku))
                    if end:
                        for c in range(2):
                            if ku in AT[f"hT{c}"]:
                                do_hT(turn, c)
                            if ku in AT[f"ffn{c}"]:
                                do_ffn(turn, c, AT[f"ffn{c}"].index(ku))
                    if prepare:
                        for c in range(2):
                            if ku in AT[f"xdbl{c}"]:
                                do_xdbl(turn, c, AT[f"xdbl{c}"].index(ku))
                            if ku in AT[f"bt{c}"]:
                                do_bt(turn, c)
                        for j in range(4):
                            if ku in AT[f"z{j}"]:
                                do_z(turn, j)
                            if ku in AT[f"gate{j}"]:
                                do_gate(turn, j)
                            if ku in AT[f"duT{j}"]:
                                do_duT(turn, j)

            start = turn_of(-1)
            for c in range(2):
                do_xnT(start, c)
            pe.wait_ge(s_taps, 1)
            for k in range(4):
                for tap in range(TAPS):
                    do_conv(start, k, tap)
            pe.wait_ge(s_w1, 16 * NW1)
            for c in range(2):
                for dt in range(DT):
                    do_xdbl(start, c, dt)
            for c in range(2):
                do_bt(start, c)
            for k in range(4):
                do_z(start, k)
            for k in range(2):
                do_gate(start, k)
            pe.wait_ge(s_w2, 16 * NW2)
            nc.tensor.matmul(p_tr[:, 0, 0:DM], f_a1[:, :], f_wT[:, :], start=True, stop=True).then_inc(s_pprep, 1)
            pe.wait_ge(s_prep, 2)
            nc.tensor.matmul(p_tr[:, 1, 0:DM], f_pT[:, :], f_a2[:, :], start=True, stop=True).then_inc(s_pprep, 1)
            nc.tensor.matmul(p_tr[0:1, 0, HALF // 2:HALF // 2 + DM], bv_col[:, :], w_o[:, :], start=True, stop=True).then_inc(s_pprep, 1)
            pe.wait_ge(s_prep, 3)
            pe.wait_ge(s_stage3, 3 + NB - 1)
            for k in range(2, 4):
                do_gate(start, k)
            for k in range(4):
                do_duT(start, k)
            pe_turn(0)
            with pe.Fori(1, NB - 1) as b:
                pe_turn(b)
            pe_turn(NB - 1)
            final = turn_of(NB)
            for c in range(2):
                for part in range(2):
                    do_out(final, c, part)
            for c in range(2):
                do_hT(final, c)
            for c in range(2):
                for part in range(2):
                    do_ffn(final, c, part)

            def turn4(src, need, full, j, freed):
                pe.wait_ge(need, j + 1)
                if freed is not None:
                    pe.wait_ge(*freed)
                for t in range(NB):
                    last = nc.tensor.transpose(p_tr[:, 1, t * P:(t + 1) * P], src[:, t, :], ident[:, :])
                last.then_inc(full, 1)

            def project_qk(j):
                pe.wait_ge(c_e1, j + 1)
                nc.tensor.matmul(p_y[:, 0, 0, :], w_q[:, :], xT3[:, :], start=True, stop=True)
                nc.tensor.matmul(p_y[:, 0, 1, :], w_k[:, :], xT3[:, :], start=True, stop=True).then_inc(c_proj, 1)

            def project_v(j, first=False):
                if not first:
                    pe.wait_ge(c_vp, j)
                for t in range(NB):
                    nc.tensor.matmul(p_y[:, 1, 0, t * DM:(t + 1) * DM], xT3[:, t * P:(t + 1) * P], w_v[:, :], start=True, stop=True)

            def project_p(j):
                pe.wait_ge(c_qk, j + 1)
                for t in range(NB):
                    last = nc.tensor.matmul(p_y[:, 1, 1, t * PW:(t + 1) * PW], qT[:, t, :],
                                            emb_blocks[:, :, :].rearrange("p m h -> p (m h)"), start=True, stop=True)
                last.then_inc(c_p, 1)

            def scores(j, first=False):
                pe.wait_ge(c_prod, j + 1)
                if not first:
                    pe.wait_ge(c_lgp, j)
                for a in range(NB):
                    for t in range(NB):
                        last = nc.tensor.matmul(p_tr[:, 0, (a * NB + t) * NH:(a * NB + t + 1) * NH], qk[:, a, t, :], head_mask[:, :],
                                                start=True, stop=True)
                last.then_inc(c_L, 1)

            def rows(bank, bias, lhs, w, done):
                nc.tensor.matmul(p_a[:, bank, :], ones_row[:, :], bias[:, :, :].rearrange("a t n -> a (t n)"), start=True, stop=False,
                                 skip_group_check=True)
                for t in range(NB):
                    last = nc.tensor.matmul(p_a[:, bank, t * P:(t + 1) * P], lhs[:, t * P:(t + 1) * P], w[:, :],
                                            start=False, stop=True, skip_group_check=True)
                last.then_inc(done, 1)

            def out_project(j, first=False):
                pe.wait_ge(c_e2, j + 1)
                if not first:
                    pe.wait_ge(c_x3, j)
                rows(0, bo_row, oT, w_o, c_wo)

            def ffn(j, first=False):
                pe.wait_ge(c_e3, j + 1)
                if not first:
                    pe.wait_ge(c_tanh, j)
                rows(1, f_brow, xT4, f_w, c_ffn)

            def pe_step(j, first=False, second=False, third=False):
                finishing = not (first or second)
                if not ends(j, 1):
                    turn4(xn3, c_xn[0], c_t1, j + 1, (c_e1, j + 1) if first or second else (c_e2, 1) if third else (c_e3, j - 2))
                    project_qk(j + 1)
                if not first:
                    turn4(o_tok, c_o, c_t2, j - 1, (c_e3, j - 2) if ends(j, 1) else (c_e1, j + 2))
                if not first:
                    out_project(j - 1, first=second)
                if not ends(j, 1):
                    project_v(j + 1)
                if finishing:
                    turn4(xn4, c_xn[1], c_t3, j - 2, (c_e2, j))
                if not ends(j, 1):
                    project_p(j + 1)
                if finishing:
                    ffn(j - 2, first=third)
                if not ends(j, 1):
                    scores(j + 1)

            for c in range(2):
                wait_emptied(pe, turn_of(NB), f"ffn{c}")
            turn4(xn3, c_xn[0], c_t1, 0, None)
            project_qk(0)
            project_v(0, first=True)
            project_p(0)
            scores(0, first=True)
            pe_step(0, first=True)
            pe_step(1, second=True)
            pe_step(2, third=True)
            with pe.Fori(3, TT - 1) as j:
                pe_step(j)
            pe_step(TT - 1)
            turn4(o_tok, c_o, c_t2, TT - 1, (c_e3, TT - 2))
            out_project(TT - 1)
            turn4(xn4, c_xn[1], c_t3, TT - 2, (c_e2, TT))
            ffn(TT - 2)
            turn4(xn4, c_xn[1], c_t3, TT - 1, (c_e3, TT - 1))
            ffn(TT - 1)


_INS = [("L0_attn_a_x", 0), ("L0_attn_a_W_in", 0), ("L0_attn_a_conv_w", 1), ("L0_attn_a_conv_b", 0), ("L0_attn_a_W_x", 0),
        ("L0_attn_a_W_dt", 0), ("L0_attn_a_b_dt", 0), ("L0_attn_a_A_log", 0), ("L0_attn_a_D", 0), ("L0_attn_a_W_out", 0),
        ("L0_attn_b_Wq", 0), ("L0_attn_b_bq", 0), ("L0_attn_b_Wk", 0), ("L0_attn_b_bk", 0),
        ("L0_attn_b_Wv", 0), ("L0_attn_b_bv", 0), ("L0_attn_b_Wo", 0), ("L0_attn_b_bo", 0), ("L0_attn_b_pos_emb", 0),
        ("L0_ffn_weight", 1), ("L0_ffn_aux_weight1", 0), ("L0_ffn_aux_weight2", 0), ("L0_ffn_bias", 0)]
_OUT = (4, 1024, 128)


def kernel(**inputs):
    import numpy as _np
    import concourse.bacc as _bacc
    from concourse import mybir as _mybir
    from concourse.bass_utils import run_bass_kernel_spmd as _run

    nc = _bacc.Bacc("TRN2", target_bir_lowering=False, num_devices=1)
    arrays, args = {}, []
    for name, turned in _INS:
        a = _np.ascontiguousarray(_np.asarray(inputs[name]).T if turned else inputs[name])
        key = f"in_{name}{'_T' if turned else ''}_dram"
        arrays[key] = a
        args.append(nc.dram_tensor(key, a.shape, _mybir.dt.from_np(a.dtype), kind="ExternalInput").ap())
    args.append(nc.dram_tensor("out_0_dram", _OUT, _mybir.dt.float32, kind="ExternalOutput").ap())
    build_hybrid_block(nc, *args)
    r = _run(nc, [arrays], core_ids=[0])
    return r.results[0]["out_0_dram"]
```

```python
import concourse.bass as bass
from concourse import mybir
from contextlib import ExitStack

F32 = mybir.dt.float32
ALU = mybir.AluOpType
ACT = mybir.ActivationFunctionType
AX = mybir.AxisListType


def build_hybrid_block(nc, x, W_in, conv_w, conv_b, W_x, W_dt, b_dt, A_log, D, W_out,
                       Wq, bq, Wk, bk, Wv, bv, Wo, bo, pos_emb,
                       ffn_wT, ffn_a1, ffn_a2, ffn_b, out):
    P = 128
    NB, L, DM = x.shape
    TT = L // P
    DT = W_out.shape[0] // P
    DI = DT * P
    NS = A_log.shape[1]
    TAPS = conv_w.shape[1]
    PAD = TAPS - 1
    R = W_dt.shape[0]
    XD = R + 2 * NS
    HALF = 512
    TPH = HALF // P
    NH = 16
    HD = DM // NH
    SCALE = 1.0 / HD ** 0.5
    EPS = 1e-5
    NKNOT = NB + 1
    PW = NKNOT * NH
    SP_CAP = 30.0

    xf = x.rearrange("s (j p) c -> p s j c", p=P)
    of = out.rearrange("s (j p) c -> p s j c", p=P)
    c_scratch = nc.dram_tensor("c_scratch", [NB, NS, L], F32).ap()

    ctx = ExitStack()
    with ctx:
        def sb(name, shape, scope=ctx):
            return scope.enter_context(nc.sbuf_tensor(name, shape, F32))

        def ps(name, shape):
            return ctx.enter_context(nc.psum_tensor(name, shape, F32))

        def sem(name):
            return ctx.enter_context(nc.semaphore(name))

        ident = sb("ident", [P, P])
        ones_row = sb("ones_row", [1, P])
        head_mask = sb("head_mask", [P, NH])
        neg_half = sb("neg_half", [P, TT])
        w_in = sb("w_in", [P, 2 * DI])
        tap_w = sb("tap_w", [P, DT, TAPS])
        conv_bias = sb("conv_bias", [P, DT])
        w_x = sb("w_x", [P, DT, XD])
        w_dt = sb("w_dt", [R, DI])
        dt_bias = sb("dt_bias", [P, DT])
        a_log = sb("a_log", [P, DT * NS])
        a_exp = sb("a_exp", [P, DT * NS])
        a_neg = sb("a_neg", [P, DT * NS])
        d_col = sb("d_col", [P, DT])
        w_out = sb("w_out", [P, DT, DM])
        w_q = sb("w_q", [P, DM])
        w_k = sb("w_k", [P, DM])
        w_v = sb("w_v", [P, DM])
        bq_col = sb("bq_col", [P, 1])
        bk_col = sb("bk_col", [P, 1])
        bv_col = sb("bv_col", [P, 1])
        w_o = sb("w_o", [P, DM])
        bo_row = sb("bo_row", [1, DM])
        emb = sb("emb", [P, NKNOT])
        emb_step = sb("emb_step", [P, NKNOT])
        emb_blocks = sb("emb_blocks", [P, NKNOT, NH])
        f_wT = sb("f_wT", [P, DM])
        f_a1 = sb("f_a1", [P, DM])
        f_a2 = sb("f_a2", [P, DM])
        f_pT = sb("f_pT", [P, DM])
        f_w = sb("f_w", [P, DM])
        f_brow = sb("f_brow", [1, TPH, DM])

        xs = sb("xs", [P, NB * L])

        mamba = ExitStack()
        x_in = sb("x_in", [P, TT, P], mamba)
        x_res = sb("x_res", [P, TT, P], mamba)
        stats = sb("stats", [P, 2, TT, 6], mamba)
        mv = sb("mv", [P, 2, TT, 2], mamba)
        var_eps = sb("var_eps", [P, 2, TT], mamba)
        rstd = sb("rstd", [P, 2, TT], mamba)
        xn = sb("xn", [P, 2, TT, P], mamba)
        xnT = sb("xnT", [P, L], mamba)
        hT = sb("hT", [P, L], mamba)
        u = sb("u", [P, DT, L], mamba)
        gate = sb("gate", [P, 2 * DT * L], mamba)
        yg = sb("yg", [P, DT, L], mamba)
        xdbl = sb("xdbl", [XD, L], mamba)
        b_tok = sb("b_tok", [P, 2 * TT * NS], mamba)
        xs_in = sb("xs_in", [P, DT, PAD + L], mamba)
        z_exp = xs_in[:, :, PAD:]
        delta = sb("delta", [P, 2 * DT * L], mamba)
        duT = sb("duT", [P, 2 * TT * DI], mamba)
        ffn_t = sb("ffn_t", [P, 2, HALF], mamba)

        NDA, NC = 2, 4
        dA = sb("dA", [P, NDA, DT, L], mamba)
        duB = sb("duB", [P, 4, TPH, DI], mamba)
        h = sb("h", [P, 4, HALF], mamba)
        hC = sb("hC", [P, 4, HALF], mamba)
        c_all = sb("c_all", [P, NC, L], mamba)

        mamba.close()

        xa = sb("xa", [P, NB, P])
        c_stats = sb("c_stats", [P, 2, NB, 6])
        c_mv = sb("c_mv", [P, 2, NB, 2])
        c_ve = sb("c_ve", [P, 2, NB])
        c_rstd = sb("c_rstd", [P, 2, NB])
        c_negm = sb("c_negm", [P, 2, NB])
        c_shift = sb("c_shift", [P, 2, NB])
        xn3 = sb("xn3", [P, NB, P])
        xn4 = sb("xn4", [P, NB, P])
        xT3 = sb("xT3", [P, NB * P])
        xT4 = sb("xT4", [P, NB * P])
        qT = sb("qT", [P, NB, P])
        kT = sb("kT", [P, NB, P])
        vt = sb("vt", [P, 2 * NB * DM])
        pk = sb("pk", [P, 2 * NB * PW])
        qk = sb("qk", [P, NB, NB, P])
        g = sb("g", [P, NB, NB, NH])
        cl = sb("cl", [P, NB, NB * NB * NH])
        lg = sb("lg", [P, NB, NB, NH])
        mx = sb("mx", [P, NB, NH])
        sm = sb("sm", [P, NB, NH])
        rc = sb("rc", [P, NB, NH])
        at = sb("at", [P, NB, NB * NH])
        pv = sb("pv", [P, NB, NB, DM])
        o_tok = sb("o_tok", [P, NB, DM])
        oT = sb("oT", [P, NB * P])
        x3 = sb("x3", [P, NB * P])
        bo_all = sb("bo_all", [P, DM])
        xb = sb("xb", [P, NB, P])
        ft = sb("ft", [P, NB * P])
        ob = sb("ob", [P, NB * P])

        p_y = ps("p_y", [P, DT, 2, HALF])
        p_tr = ps("p_tr", [P, 2, HALF])
        p_a = ps("p_a", [P, 2, HALF])

        s_xin, s_xres, s_out = sem("x_in_loaded"), sem("x_res_loaded"), sem("out_stored")
        s_w0, s_w1, s_w2 = sem("in_weights"), sem("mamba_weights"), sem("other_weights")
        s_mask = sem("masks_step")
        s_cst = sem("constants_ready")
        s_aexp = sem("a_exp_ready")
        s_conv = sem("conv_step")
        s_prep = sem("dve_prep_step")
        s_pprep = sem("pe_prep_step")
        s_bn, s_var, s_ve, s_rstd, s_xn = ([sem(f"{name}{a}") for a in (1, 2)] for name in
                                           ("bn_stats_done", "var_ready", "var_eps_ready", "rstd_ready", "xn_ready"))
        s_full = sem("pa_full")
        s_empty = [sem("pa_empty0"), sem("pa_empty1")]
        s_cst_dram = sem("c_stored")
        s_cld = [sem(f"c_loaded{i}") for i in range(NC)]
        s_zmin, s_zexp, s_zln, s_delta, s_du = sem("z_capped"), sem("z_exp_ready"), sem("z_ln_ready"), sem("delta_ready"), sem("du_ready")
        s_u, s_gate = sem("u_ready"), sem("gate_ready")
        s_duB, s_tr, s_dA, s_scan, s_hC, s_sum = [sem("duB_by_act"), sem("duB_by_dve")], sem("tr_ready"), sem("dA_ready"), sem("scan_done"), sem("hC_ready"), sem("sum_done")
        s_skip = sem("du_added")
        s_yg = sem("y_gated")
        s_x2 = sem("x2_ready")
        s_stage3 = sem("attn_constants_step")
        c_xa = sem("attn_x_loaded")
        c_var = [sem("attn_var3"), sem("attn_var4")]
        c_vep = [sem("attn_ve3"), sem("attn_ve4")]
        c_rs = [sem("attn_rstd3"), sem("attn_rstd4")]
        c_sh = [sem("attn_shift3"), sem("attn_shift4")]
        c_xn = [sem("attn_xn3"), sem("attn_xn4")]
        c_bnd = [sem("attn_bn3"), sem("attn_bn4")]
        c_kept = sem("x3_kept")
        c_bo, c_xb = sem("bo_all_step"), sem("x_with_bo_ready")
        c_t1, c_t2, c_t3 = sem("x_turned"), sem("o_turned"), sem("x3_turned")
        c_e1, c_e2, c_e3 = sem("xT3_ready"), sem("oT_ready"), sem("xT4_ready")
        c_proj, c_qk, c_p, c_vp, c_prod, c_L = sem("qkv_projected"), sem("qkT_ready"), sem("p_projected"), sem("v_p_ready"), sem("qk_products"), sem("scores_ready")
        c_th, c_lgp, c_sub, c_exp, c_step = sem("gates_tanh"), sem("scores_read"), sem("logits_ready"), sem("exp_ready"), sem("attention_step")
        c_pvd, c_o, c_wo, c_x3, c_ffn, c_tanh, c_out = sem("pv_products"), sem("o_ready"), sem("wo_ready"), sem("x3_ready"), sem("ffn_ready"), sem("ffn_tanh"), sem("out_tile")
        SCAN0, TR0, HC0, SUM0, YG0 = 8, 8, 16, 4, 4

        block = ctx.enter_context(nc.Block())
        NU = 4 * NS

        A_JOBS = ["xnT0", "xnT1", "xs0", "xs1", "xs2", "xs3", "xdbl0", "xdbl1", "bt0", "bt1",
                  "z0", "z1", "z2", "z3", "gate0", "gate1", "gate2", "gate3", "duT0", "duT1", "duT2", "duT3"]
        D_JOBS = ["out0", "out1", "hT0", "hT1", "ffn0", "ffn1"]
        LAST_JOBS = ["out0", "out1", "hT0", "ffn0", "hT1", "ffn1"]
        BOTH = ["out0", "out1", "xnT0", "xnT1", "xs0", "xs1", "xs2", "xs3", "hT0", "hT1", "ffn0", "ffn1"] + A_JOBS[6:]

        def turn_of(b):
            if isinstance(b, int):
                if b == -1:
                    return b, 0, A_JOBS, 0
                if b == 0:
                    return b, len(A_JOBS), A_JOBS, len(A_JOBS) // 2
                if b >= NB - 1:
                    before = 2 * len(A_JOBS) + (NB - 2) * len(BOTH) + (b - NB + 1) * len(D_JOBS)
                    return b, before, D_JOBS if b < NB else LAST_JOBS, before // 2
            return (b, b * len(BOTH) + 2 * len(A_JOBS) - len(BOTH), BOTH,
                    b * (len(BOTH) // 2) + len(A_JOBS) - len(BOTH) // 2)

        def bank_of(turn, job):
            return turn[2].index(job) % 2

        def wait_full(eng, turn, job):
            eng.wait_ge(s_full, turn[1] + turn[2].index(job) + 1)

        def empty_count(turn, job):
            k = turn[2].index(job)
            return turn[3] + k // 2 + 2

        def wait_emptied(eng, turn, job):
            eng.wait_ge(s_empty[bank_of(turn, job)], empty_count(turn, job))

        def cut(t, start, n):
            return t[:, start:start + n] if isinstance(start, int) else t[:, bass.ds(start, n)]

        def side(b, size):
            return (b % 2) * size

        def xcols(b, c):
            return cut(xs, b * L + c * HALF, HALF)

        def x_at(j):
            v = xs[:, :].rearrange("p (s j c) -> p s j c", s=NB, c=P)
            return v[:, :, j, :] if isinstance(j, int) else v[:, :, bass.ds(j, 1), :].rearrange("p s j c -> p (s j) c")

        def ends(j, ahead):
            return isinstance(j, int) and j + ahead >= TT

        def begun(j, back):
            return not isinstance(j, int) or j >= back

        def conv_count(turn, tap, dt):
            return ((turn[0] + 1) * TAPS + tap) * DT + dt + 1

        SKIP_STATE = 2

        DVE_STATES = (2, 8, 13)

        def duB_ready(b, i, half):
            mine = [n for n in range(NS) if (n in DVE_STATES) == (i in DVE_STATES)]
            return s_duB[i in DVE_STATES], (b * len(mine) + mine.index(i)) * 2 + half + 1

        AT = {"out0": (1, 2), "out1": (3, 4), "xnT0": (6,), "xnT1": (7,), "xs0": (9,), "xs1": (10,), "xs2": (12,),
              "xs3": (13,), "hT0": (18,), "hT1": (19,), "ffn0": (21, 22), "ffn1": (23, 24), "xdbl0": (30, 31),
              "xdbl1": (32, 33), "bt0": (35,), "bt1": (36,), "z0": (38,), "z1": (39,), "z2": (41,), "z3": (42,),
              "gate0": (44,), "gate1": (45,), "gate2": (47,), "gate3": (48,), "duT0": (54,), "duT1": (55,), "duT2": (57,),
              "duT3": (57,),
              "yg": 1, "ln1": 0, "norm1": (4, 5), "x1": (5, 7), "ln2": 9, "norm2": (13, 14), "conv": 18, "x2": (27, 29),
              "silu": 26, "zmin": 45, "exp": 46, "delta": 50, "du": (51, 52)}

        ACT_AFTER = 3
        DVE_AFTER = 3

        NW1 = 11
        NW2 = 3 + TPH + 4 + 3 + 1 + NH

        @block.sync
        def _(sp):
            sp.dma_start(x_in[:, :, :], xf[:, 0]).then_inc(s_xin, 16)
            sp.dma_start(w_in[:, :], W_in).then_inc(s_w0, 16)
            sp.dma_start(tap_w[:, :, :], conv_w.rearrange("(t p) k -> p t k", p=P)).then_inc(s_w1, 16)
            sp.dma_start(w_x[:, :, :], W_x.rearrange("(t p) n -> p t n", p=P)).then_inc(s_w1, 16)
            sp.dma_start(w_dt[:, :], W_dt).then_inc(s_w1, 16)
            sp.dma_start(w_out[:, :, :], W_out.rearrange("(t p) n -> p t n", p=P)).then_inc(s_w1, 16)

            def load_x_in(b):
                sp.dma_start(x_in[:, :, :], xf[:, b] if isinstance(b, int) else
                             xf[:, bass.ds(b, 1)].rearrange("p s j c -> p (s j) c")).then_inc(s_xin, 16)

            def load_x_res(b):
                sp.dma_start(x_res[:, :, :], xf[:, b] if isinstance(b, int) else
                             xf[:, bass.ds(b, 1)].rearrange("p s j c -> p (s j) c")).then_inc(s_xres, 16)

            def store_c(turn):
                b = turn[0] + 1
                wait_emptied(sp, turn, "xdbl0")
                wait_emptied(sp, turn, "xdbl1")
                sp.dma_start(c_scratch[b] if isinstance(b, int) else c_scratch[bass.ds(b, 1)].rearrange("b n t -> (b n) t"),
                             xdbl[R + NS:XD, :]).then_inc(s_cst_dram, 16)

            def sp_turn(b):
                turn = turn_of(b)
                sp.wait_ge(s_cst_dram, 16 * b + 16)
                sp.nop(nofuse=True)
                for i in range(NS):
                    sp.wait_ge(s_hC, (b * NS + i - NC + 1) * 4 + HC0)
                    row = (c_scratch[b, i, :] if isinstance(b, int) else
                           c_scratch[bass.ds(b, 1), i, :].rearrange("b t -> (b t)"))
                    sp.dma_start(c_all[:, i % NC, :], row.partition_broadcast(P)).then_inc(s_cld[i % NC], 16)
                    if i == 6 and turn[2] is not D_JOBS and not (isinstance(b, int) and b + 2 >= NB):
                        sp.wait_ge(s_xn[0], 2 * b + 4)
                        load_x_in(b + 2)
                    if i == 12 and turn[2] is not D_JOBS:
                        store_c(turn)
                    if i == 14 and not (isinstance(b, int) and b == 0):
                        sp.wait_ge(s_x2, 2 * b)
                        load_x_res(b)

            load_x_res(0)
            sp.wait_ge(s_xn[0], 2)
            load_x_in(1)
            sp.dma_start(f_wT[:, :], ffn_wT).then_inc(s_w2, 16)
            sp.dma_start(f_a1[:, :], ffn_a1).then_inc(s_w2, 16)
            sp.dma_start(f_a2[:, :], ffn_a2).then_inc(s_w2, 16)
            for k in range(TPH):
                sp.dma_start(f_brow[0:1, k, :], ffn_b.rearrange("(a n) -> a n", a=1)).then_inc(s_w2, 16)
            for w, src in ((w_q, Wq), (w_k, Wk), (w_v, Wv), (w_o, Wo)):
                sp.dma_start(w[:, :], src).then_inc(s_w2, 16)
            for w, src in ((bq_col, bq), (bk_col, bk), (bv_col, bv)):
                sp.dma_start(w[:, :], src.rearrange("(p a) -> p a", a=1)).then_inc(s_w2, 16)
            sp.dma_start(bo_row[:, :], bo.rearrange("(a n) -> a n", a=1)).then_inc(s_w2, 16)
            for hd in range(NH):
                sp.dma_start(emb[hd * HD:(hd + 1) * HD, :], pos_emb[0, :, 0:NKNOT]).then_inc(s_w2, 16)
            store_c(turn_of(-1))
            for b in range(NB):
                sp_turn(b)

            def load_x(j):
                sp.dma_start(xa[:, :, :], x_at(j)).then_inc(c_xa, 16)

            def store(j):
                sp.wait_ge(c_out, j + 1)
                sp.dma_start(of[:, :, j, :] if isinstance(j, int) else of[:, :, bass.ds(j, 1), :].rearrange("p s j c -> p (s j) c"),
                             ob[:, :].rearrange("p (s c) -> p s c", c=P)).then_inc(s_out, 16)

            sp.wait_ge(s_x2, 2 * NB - 1)
            load_x(0)
            sp.wait_ge(c_xn[0], 1)
            sp.wait_ge(s_x2, 2 * NB)
            load_x(1)
            for j in range(2, 6):
                sp.wait_ge(c_xn[0], j)
                load_x(j)
            with sp.Fori(3, TT - 3) as j:
                sp.wait_ge(c_xn[0], j + 3)
                load_x(j + 3)
                store(j - 3)
            for j in range(TT - 6, TT):
                store(j)
            sp.wait_ge(s_out, 16 * TT)

        @block.gpsimd
        def _(pool):
            pool.memset(ident[:, :], 0.0).then_inc(s_mask, 1)
            pool.memset(head_mask[:, :], 1.0).then_inc(s_mask, 1)
            pool.memset(ones_row[:, :], 1.0)
            pool.memset(xs_in[:, :, 0:PAD], 0.0)
            pool.memset(neg_half[:, :], -0.5).then_inc(s_cst, 1)
            pool.wait_ge(s_mask, 2)
            pool.affine_select(out=ident[:, :], in_=ident[:, :], compare_op=ALU.not_equal, fill=1.0,
                               base=0, pattern=[[-1, P]], channel_multiplier=1).then_inc(s_cst, 1)
            pool.affine_select(out=head_mask[:, :], in_=head_mask[:, :], compare_op=ALU.is_ge, fill=0.0,
                               base=0, pattern=[[-HD, NH]], channel_multiplier=1).then_inc(s_mask, 1)
            pool.wait_ge(s_mask, 3)
            pool.affine_select(out=head_mask[:, :], in_=head_mask[:, :], compare_op=ALU.is_ge, fill=0.0,
                               base=HD - 1, pattern=[[HD, NH]], channel_multiplier=-1).then_inc(s_cst, 1)
            pool.wait_ge(s_cst, 3)
            pool.memset(hC[:, 0, 0:1], 0.0).then_inc(s_hC, HC0)

            def rstd_of(a, b):
                pool.wait_ge(s_var[a], b + 1)
                pool.nop(nofuse=True)
                pool.tensor_scalar(var_eps[:, a, :], mv[:, a, :, 1], EPS, None, ALU.add).then_inc(s_ve[a], 1)
                pool.wait_ge(s_ve[a], b + 1)
                pool.nop(nofuse=True)
                pool.tensor_tensor(rstd[:, a, :], var_eps[:, a, :], neg_half[:, :], ALU.pow).then_inc(s_rstd[a], 1)

            def times_u(b, dt):
                pool.wait_ge(s_delta, b * DT + dt + 1)
                pool.tensor_tensor(z_exp[:, dt, :], cut(delta, side(b, DT * L) + dt * L, L), u[:, dt, :], ALU.mult
                                   ).then_inc(s_du, 1)

            def add_ffn(turn, c):
                wait_emptied(pool, turn, f"ffn{c}")
                pool.tensor_tensor(xcols(turn[0] - 1, c), x_res[:, c * TPH:(c + 1) * TPH, :].rearrange("p j c -> p (j c)"),
                                   ffn_t[:, c, :], ALU.add).then_inc(s_x2, 1)

            def pool_turn(b):
                turn = turn_of(b)
                prepare, end = turn[2] is not D_JOBS, turn[2] is not A_JOBS
                for ku in range(NU):
                    i, k = ku // 4, ku % 4
                    half = k // 2
                    if k == 0:
                        pool.wait_ge(s_cld[i % NC], 16 * (b * (NS // NC) + i // NC) + 16)
                    pool.wait_ge(s_scan, b * NU + ku + 1 + SCAN0)
                    pool.wait_ge(s_sum, b * NU + ku - 3 + SUM0)
                    pool.tensor_tensor(hC[:, k, :], h[:, k, :], c_all[:, i % NC, half * HALF:(half + 1) * HALF],
                                       ALU.mult).then_inc(s_hC, 1)
                    if prepare:
                        if ku == AT["ln1"] + 2:
                            rstd_of(0, b + 1)
                        for dt in range(DT):
                            if ku == AT["du"][dt]:
                                times_u(b + 1, dt)
                    if end:
                        if ku == AT["ln2"] + 2:
                            rstd_of(1, b - 1)
                        for c in range(2):
                            if ku == AT["x2"][c]:
                                add_ffn(turn, c)

            rstd_of(0, 0)
            pool_turn(0)
            with pool.Fori(1, NB - 1) as b:
                pool_turn(b)
            pool_turn(NB - 1)
            for c in range(2):
                half = slice(c * TPH, (c + 1) * TPH)
                pool.wait_ge(s_var[1], NB + c)
                pool.tensor_scalar(var_eps[:, 1, half], mv[:, 1, half, 1], EPS, None, ALU.add).then_inc(s_ve[1], 1)
                pool.wait_ge(s_ve[1], NB + c)
                pool.tensor_tensor(rstd[:, 1, half], var_eps[:, 1, half], neg_half[:, half], ALU.pow).then_inc(s_rstd[1], 1)
            for c in range(2):
                add_ffn(turn_of(NB), c)

            def attn_rstd(a, j, first=False):
                pool.wait_ge(c_var[a], j + 1)
                if not first:
                    pool.wait_ge(c_xn[a], j)
                pool.nop(nofuse=True)
                pool.tensor_scalar(c_negm[:, a, :], c_mv[:, a, :, 0], -1.0, None, ALU.mult)
                pool.tensor_scalar(c_ve[:, a, :], c_mv[:, a, :, 1], EPS, None, ALU.add).then_inc(c_vep[a], 1)
                pool.wait_ge(c_vep[a], j + 1)
                pool.nop(nofuse=True)
                pool.tensor_tensor(c_rstd[:, a, :], c_ve[:, a, :], neg_half[:, 0:NB], ALU.pow).then_inc(c_rs[a], 1)
                pool.wait_ge(c_rs[a], j + 1)
                pool.nop(nofuse=True)
                pool.tensor_tensor(c_shift[:, a, :], c_negm[:, a, :], c_rstd[:, a, :], ALU.mult).then_inc(c_sh[a], 1)

            def products(j, first=False):
                pool.wait_ge(c_qk, j + 1)
                if not first:
                    pool.wait_ge(c_L, j)
                pool.tensor_tensor(qk[:, :, :, :], qT[:, :, :].unsqueeze(2).to_broadcast([P, NB, NB, P]),
                                   kT[:, :, :].unsqueeze(1).to_broadcast([P, NB, NB, P]), ALU.mult).then_inc(c_prod, 1)

            def finish(j):
                pool.wait_ge(c_tanh, j + 1)
                pool.wait_ge(s_out, 16 * j)
                pool.wait_ge(c_kept, j + 1)
                pool.tensor_tensor(ob[:, :].rearrange("p (s c) -> p s c", c=P), x_at(j), ft[:, :].rearrange("p (s c) -> p s c", c=P),
                                   ALU.add).then_inc(c_out, 1)

            def add_bias(j):
                pool.wait_ge(c_x3, j)
                pool.tensor_tensor(xb[:, :, :], x_at(j), bo_all[:, :].unsqueeze(1).to_broadcast([P, NB, P]), ALU.add).then_inc(c_xb, 1)

            def pool_step(j):
                if not ends(j, 1):
                    products(j + 1)
                if begun(j, 3):
                    finish(j - 3)
                if begun(j, 2):
                    attn_rstd(1, j - 2, first=isinstance(j, int) and j == 2)
                if not ends(j, 3):
                    attn_rstd(0, j + 3)
                if begun(j, 1):
                    add_bias(j - 1)

            attn_rstd(0, 0, first=True)
            attn_rstd(0, 1)
            pool.wait_ge(c_bo, 2)
            products(0, first=True)
            attn_rstd(0, 2)
            for j in range(3):
                pool_step(j)
            with pool.Fori(3, TT - 3) as j:
                pool_step(j)
            for j in range(TT - 3, TT):
                pool_step(j)
            finish(TT - 3)
            add_bias(TT - 1)
            attn_rstd(1, TT - 2)
            finish(TT - 2)
            attn_rstd(1, TT - 1)
            finish(TT - 1)

        @block.scalar
        def _(act):
            for col, src in ((conv_bias, conv_b), (dt_bias, b_dt), (d_col, D)):
                for dt in range(DT):
                    act.dma_start(col[:, dt:dt + 1], src[dt * P:(dt + 1) * P].rearrange("(p a) -> p a", a=1)).then_inc(s_w1, 16)
            act.dma_start(a_log[:, :].rearrange("p (t n) -> p t n", n=NS), A_log.rearrange("(t p) n -> p t n", p=P)).then_inc(s_w1, 16)
            act.wait_ge(s_w1, 16 * NW1)
            nc.scalar.activation(a_exp[:, :], a_log[:, :], ACT.Exp).then_inc(s_aexp, 1)

            def settle(b):
                if not isinstance(b, int):
                    act.nop(nofuse=True)

            def take_out(turn, job, dst, func, **kw):
                bank = bank_of(turn, job)
                wait_full(act, turn, job)
                if job[:2] in ("ga", "bt", "du"):
                    settle(turn[0])
                src = p_a[:, bank, :]
                if job[:2] == "bt":
                    src = src.rearrange("p (t n) -> p t n", n=P)[:, :, R:R + NS]
                nc.scalar.activation(dst, src, func, **kw).then_inc(s_empty[bank], 1)

            def xnT_out(turn, c):
                take_out(turn, f"xnT{c}", xnT[:, c * HALF:(c + 1) * HALF], ACT.Copy)

            def xs_out(turn, k):
                c, dt = k // 2, k % 2
                take_out(turn, f"xs{k}", xs_in[:, dt, PAD + c * HALF:PAD + (c + 1) * HALF], ACT.Copy)

            def gate_out(turn, k):
                c, dt = k // 2, k % 2
                take_out(turn, f"gate{k}", cut(gate, side(turn[0] + 1, DT * L) + dt * L + c * HALF, HALF), ACT.Copy)

            def bt_out(turn, c):
                take_out(turn, f"bt{c}", cut(b_tok, side(turn[0] + 1, TT * NS) + c * TPH * NS, TPH * NS
                                             ).rearrange("p (t n) -> p t n", n=NS), ACT.Copy)

            def duT_out(turn, k):
                take_out(turn, f"duT{k}", cut(duT, side(turn[0] + 1, TT * DI) + 2 * k * DI, 2 * DI), ACT.Copy)

            def hT_out(turn, c):
                take_out(turn, f"hT{c}", hT[:, c * HALF:(c + 1) * HALF], ACT.Copy)

            def ffn_out_half(turn, c):
                take_out(turn, f"ffn{c}", ffn_t[:, c, :], ACT.Tanh)

            def silu_u(turn):
                for dt in range(DT):
                    act.wait_ge(s_conv, conv_count(turn, TAPS - 1, dt))
                    nc.scalar.activation(u[:, dt, :], u[:, dt, :], ACT.Silu).then_inc(s_u, 1)

            def silu_gate(turn):
                b = turn[0]
                before = turn_of(b - 1) if isinstance(b, int) else None
                for dt in range(DT):
                    if dt == 0:
                        if before is not None:
                            wait_emptied(act, before, "gate2")
                            wait_emptied(act, before, "gate3")
                        else:
                            act.wait_ge(s_empty[0], turn[3] - 1)
                            act.wait_ge(s_empty[1], turn[3] - 1)
                        settle(b)
                    gc = cut(gate, side(b, DT * L) + dt * L, L)
                    nc.scalar.activation(gc, gc, ACT.Silu).then_inc(s_gate, 1)

            def softplus(b):
                for dt in range(DT):
                    act.wait_ge(s_zmin, b * DT + dt + 1)
                    nc.scalar.activation(z_exp[:, dt, :], z_exp[:, dt, :], ACT.Exp).then_inc(s_zexp, 1)
                for dt in range(DT):
                    act.wait_ge(s_zexp, b * DT + dt + 1)
                    nc.scalar.activation(z_exp[:, dt, :], z_exp[:, dt, :], ACT.Ln, bias=1.0).then_inc(s_zln, 1)

            def act_turn(b):
                turn = turn_of(b)
                prepare, end = turn[2] is not D_JOBS, turn[2] is not A_JOBS

                def spread(i, half):
                    act.wait_ge(s_tr, b * NU + i * 4 + 2 * half - 6 + TR0)
                    settle(b)
                    for t in range(TPH):
                        last = nc.scalar.activation(duB[:, 2 * (i % 2) + half, t, :], cut(duT, side(b, TT * DI) + (half * TPH + t) * DI, DI), ACT.Copy,
                                                    scale=cut(b_tok, side(b, TT * NS) + (half * TPH + t) * NS + i, 1))
                    last.then_inc(duB_ready(b, i, half)[0], 1)

                def pieces(since, until):
                    def due(at):
                        return since < at <= until
                    if end:
                        for c in range(2):
                            if due(AT[f"hT{c}"][-1] + ACT_AFTER):
                                hT_out(turn, c)
                            if due(AT[f"ffn{c}"][-1] + ACT_AFTER):
                                ffn_out_half(turn, c)
                    if prepare:
                        for c in range(2):
                            if due(AT[f"xnT{c}"][-1] + ACT_AFTER):
                                xnT_out(turn, c)
                        for k in range(4):
                            if due(AT[f"xs{k}"][-1] + ACT_AFTER):
                                xs_out(turn, k)
                    if due(AT["silu"]):
                        if prepare:
                            silu_u(turn)
                        silu_gate(turn)
                    if prepare:
                        for c in range(2):
                            if due(AT[f"bt{c}"][-1] + ACT_AFTER):
                                bt_out(turn, c)
                        if due(AT["exp"]):
                            softplus(b + 1)
                        for k in range(4):
                            if due(AT[f"gate{k}"][-1] + ACT_AFTER):
                                gate_out(turn, k)
                        for k in range(4):
                            if due(AT[f"duT{k}"][-1] + ACT_AFTER):
                                duT_out(turn, k)

                for i in range(NS):
                    if i not in DVE_STATES:
                        spread(i, 0)
                    pieces(4 * i - 6 if i else -99, 4 * i - 5)
                    act.wait_ge(s_scan, b * NU + (i - 1) * 4 + SCAN0)
                    settle(b)
                    for dt in range(DT):
                        nc.scalar.activation(dA[:, i % NDA, dt, :], cut(delta, side(b, DT * L) + dt * L, L), ACT.Exp,
                                             scale=a_neg[:, dt * NS + i:dt * NS + i + 1]).then_inc(s_dA, 1)
                    pieces(4 * i - 5, 4 * i - 4)
                    if i not in DVE_STATES:
                        spread(i, 1)
                    pieces(4 * i - 4, 4 * i - 2)
                pieces(4 * NS - 6, 99)
                if prepare:
                    wait_emptied(act, turn, "duT2")
                    wait_emptied(act, turn, "duT3")
                    settle(b)

            start = turn_of(-1)
            for c in range(2):
                xnT_out(start, c)
            for k in range(4):
                xs_out(start, k)
            silu_u(start)
            for c in range(2):
                bt_out(start, c)
            for k in range(2):
                gate_out(start, k)
            softplus(0)
            for k in range(2, 4):
                gate_out(start, k)
            for k in range(4):
                duT_out(start, k)
            wait_emptied(act, start, "duT2")
            wait_emptied(act, start, "duT3")
            act_turn(0)
            with act.Fori(1, NB - 1) as b:
                act_turn(b)
            act_turn(NB - 1)
            for c in range(2):
                hT_out(turn_of(NB), c)
                ffn_out_half(turn_of(NB), c)

            def normalise(a, src, dst, j):
                act.wait_ge(c_sh[a], j + 1)
                for t in range(NB):
                    last = nc.scalar.activation(dst[:, t, :], src[:, t * P:(t + 1) * P], ACT.Identity,
                                                scale=c_rstd[:, a, t:t + 1], bias=c_shift[:, a, t:t + 1])
                last.then_inc(c_xn[a], 1)

            def keep(j):
                settle(j)
                nc.scalar.activation(x_at(j), x3[:, :].rearrange("p (s c) -> p s c", c=P), ACT.Copy).then_inc(c_kept, 1)

            def exps(j):
                act.wait_ge(c_sub, j + 1)
                nc.scalar.activation(lg[:, :, :, :], lg[:, :, :, :], ACT.Exp).then_inc(c_exp, 1)

            def turned(full, dst, done, j):
                act.wait_ge(full, j + 1)
                nc.scalar.activation(dst[:, :], p_tr[:, 1, :], ACT.Copy).then_inc(done, 1)

            def qk_out(j):
                act.wait_ge(c_proj, j + 1)
                if begun(j, 1):
                    act.wait_ge(c_prod, j)
                nc.scalar.activation(qT[:, :, :].rearrange("p s t -> p (s t)"), p_y[:, 0, 0, :], ACT.Identity, bias=bq_col[:, :])
                nc.scalar.activation(kT[:, :, :].rearrange("p s t -> p (s t)"), p_y[:, 0, 1, :], ACT.Identity, bias=bk_col[:, :]
                                     ).then_inc(c_qk, 1)

            def vp_out(j):
                act.wait_ge(c_p, j + 1)
                if begun(j, 2):
                    act.wait_ge(c_pvd, j - 1)
                settle(j)
                nc.scalar.activation(cut(vt, side(j, NB * DM), NB * DM), p_y[:, 1, 0, :], ACT.Copy)
                nc.scalar.activation(cut(pk, side(j, NB * PW), NB * PW).rearrange("p (m s h) -> p m s h", s=NB, h=NH),
                                     p_y[:, 1, 1, 0:NB * PW].rearrange("p (s m h) -> p m s h", s=NB, h=NH), ACT.Copy
                                     ).then_inc(c_vp, 1)

            def gates(j):
                act.wait_ge(c_L, j + 1)
                nc.scalar.activation(g[:, :, :, :].rearrange("p s t h -> p (s t h)"), p_tr[:, 0, 0:NB * NB * NH], ACT.Tanh,
                                     scale=0.5 * SCALE).then_inc(c_th, 1)

            def ffn_out(j):
                act.wait_ge(c_ffn, j + 1)
                act.wait_ge(c_out, j)
                nc.scalar.activation(ft[:, :], p_a[:, 1, :], ACT.Tanh).then_inc(c_tanh, 1)

            xaf = xa[:, :, :].rearrange("p s c -> p (s c)")

            def act_step(j):
                if not ends(j, 2):
                    turned(c_t1, xT3, c_e1, j + 2)
                if not ends(j, 1):
                    vp_out(j + 1)
                if begun(j, 1):
                    turned(c_t2, oT, c_e2, j - 1)
                if not ends(j, 2):
                    qk_out(j + 2)
                exps(j)
                if begun(j, 2):
                    normalise(1, x3, xn4, j - 2)
                    keep(j - 2)
                if not ends(j, 1):
                    gates(j + 1)
                if begun(j, 2):
                    turned(c_t3, xT4, c_e3, j - 2)
                if not ends(j, 3):
                    normalise(0, xaf, xn3, j + 3)
                if begun(j, 2):
                    ffn_out(j - 2)

            normalise(0, xaf, xn3, 0)
            turned(c_t1, xT3, c_e1, 0)
            normalise(0, xaf, xn3, 1)
            qk_out(0)
            vp_out(0)
            turned(c_t1, xT3, c_e1, 1)
            qk_out(1)
            gates(0)
            normalise(0, xaf, xn3, 2)
            for j in range(3):
                act_step(j)
            with act.Fori(3, TT - 3) as j:
                act_step(j)
            for j in range(TT - 3, TT):
                act_step(j)
            turned(c_t2, oT, c_e2, TT - 1)
            for j in range(TT - 2, TT):
                normalise(1, x3, xn4, j)
                keep(j)
                turned(c_t3, xT4, c_e3, j)
                ffn_out(j)

        @block.vector
        def _(dve):
            def ln_stats(a, xb, b, part):
                for j in range(part * TPH, (part + 1) * TPH):
                    last = nc.vector.bn_stats(stats[:, a, j, :], xb[:, j, :])
                if part:
                    last.then_inc(s_bn[a], 1)
                    dve.wait_ge(s_bn[a], b + 1)
                    dve.nop(nofuse=True)
                    for j in range(TT):
                        last = nc.vector.bn_aggr(mv[:, a, j, :], stats[:, a, j, :])
                    last.then_inc(s_var[a], 1)

            def ln_norm(a, xb, b, c):
                if c == 0:
                    dve.wait_ge(s_rstd[a], b + 1)
                for j in range(c * TPH, (c + 1) * TPH):
                    last = nc.vector.tensor_scalar(xn[:, a, j, :], xb[:, j, :], mv[:, a, j, 0:1], rstd[:, a, j:j + 1],
                                                   ALU.subtract, ALU.mult)
                last.then_inc(s_xn[a], 1)

            def ln1_stats(b, part):
                if part == 0:
                    dve.wait_ge(s_xin, 16 * b + 16)
                    dve.nop(nofuse=True)
                ln_stats(0, x_in, b, part)

            def ln2_stats(turn, part):
                if part == 0:
                    for c in range(2):
                        wait_emptied(dve, turn, f"out{c}")
                    dve.nop(nofuse=True)
                ln_stats(1, x_res, turn[0] - 1, part)

            def conv_step(turn, step):
                tap, dt = step // DT, step % DT
                if step == 0:
                    for k in range(2, 4):
                        wait_emptied(dve, turn, f"xs{k}")
                w = tap_w[:, dt, PAD - tap:TAPS - tap]
                xs_back = xs_in[:, dt, PAD - tap:PAD - tap + L]
                if tap == 0:
                    ins = nc.vector.tensor_scalar(u[:, dt, :], xs_back, w, conv_bias[:, dt:dt + 1], ALU.mult, ALU.add)
                else:
                    dve.wait_ge(s_conv, conv_count(turn, tap - 1, dt))
                    ins = nc.vector.scalar_tensor_tensor(u[:, dt, :], xs_back, w, u[:, dt, :], ALU.mult, ALU.add)
                ins.then_inc(s_conv, 1)

            def spread_dve(b, i, half):
                dve.wait_ge(s_tr, b * NU + i * 4 + 2 * half - 6 + TR0)
                for t in range(TPH):
                    last = nc.vector.tensor_scalar(duB[:, 2 * (i % 2) + half, t, :], cut(duT, side(b, TT * DI) + (half * TPH + t) * DI, DI),
                                                   cut(b_tok, side(b, TT * NS) + (half * TPH + t) * NS + i, 1), None, ALU.mult)
                last.then_inc(duB_ready(b, i, half)[0], 1)

            def xdbl_out(turn, c):
                bank = bank_of(turn, f"xdbl{c}")
                wait_full(dve, turn, f"xdbl{c}")
                nc.vector.tensor_copy(xdbl[:, c * HALF:(c + 1) * HALF], p_a[0:XD, bank, :]).then_inc(s_empty[bank], 1)

            def z_out(turn, k):
                c, dt = k // 2, k % 2
                bank = bank_of(turn, f"z{k}")
                wait_full(dve, turn, f"z{k}")
                nc.vector.tensor_scalar(cut(delta, side(turn[0] + 1, DT * L) + dt * L + c * HALF, HALF), p_a[:, bank, :],
                                        dt_bias[:, dt:dt + 1], None, ALU.add).then_inc(s_empty[bank], 1)

            def z_min(turn):
                for k in range(2, 4):
                    wait_emptied(dve, turn, f"z{k}")
                for dt in range(DT):
                    nc.vector.tensor_scalar(z_exp[:, dt, :], cut(delta, side(turn[0] + 1, DT * L) + dt * L, L), SP_CAP, None,
                                            ALU.min).then_inc(s_zmin, 1)

            def z_max(b, dt):
                dve.wait_ge(s_zln, b * DT + dt + 1)
                d = cut(delta, side(b, DT * L) + dt * L, L)
                nc.vector.tensor_tensor(d, d, z_exp[:, dt, :], ALU.max).then_inc(s_delta, 1)

            def add_skip(b, k):
                c, dt = k // 2, k % 2
                dve.wait_ge(s_hC, b * NU + 4 * SKIP_STATE + k + 1 + HC0)
                nc.vector.scalar_tensor_tensor(hC[:, k, :], u[:, dt, c * HALF:(c + 1) * HALF], d_col[:, dt:dt + 1], hC[:, k, :],
                                               ALU.mult, ALU.add).then_inc(s_skip, 1)

            def gate_y(b, k):
                c, dt = k // 2, k % 2
                dve.wait_ge(s_sum, b * NU + NU - 3 + k + SUM0)
                if k == 0:
                    dve.wait_ge(s_gate, b * DT + DT)
                nc.vector.tensor_tensor(yg[:, dt, c * HALF:(c + 1) * HALF], p_y[:, dt, c, :],
                                        cut(gate, side(b, DT * L) + dt * L + c * HALF, HALF), ALU.mult).then_inc(s_yg, 1)

            def ln2_half(c):
                tiles = range(c * TPH, (c + 1) * TPH)
                for j in tiles:
                    last = nc.vector.bn_stats(stats[:, 1, j, :], x_res[:, j, :])
                last.then_inc(s_bn[1], 1)
                dve.wait_ge(s_bn[1], NB + c)
                for j in tiles:
                    last = nc.vector.bn_aggr(mv[:, 1, j, :], stats[:, 1, j, :])
                last.then_inc(s_var[1], 1)

            def add_out(turn, c):
                b = turn[0] - 1
                bank = bank_of(turn, f"out{c}")
                if c == 0:
                    dve.wait_ge(s_xres, 16 * b + 16)
                wait_full(dve, turn, f"out{c}")
                xh = x_res[:, c * TPH:(c + 1) * TPH, :].rearrange("p j c -> p (j c)")
                nc.vector.tensor_tensor(xh, p_a[:, bank, :], xh, ALU.add).then_inc(s_empty[bank], 1)

            def dve_turn(b):
                turn = turn_of(b)
                prepare, end = turn[2] is not D_JOBS, turn[2] is not A_JOBS
                for ku in range(NU):
                    i, k = ku // 4, ku % 4
                    half, dt = k // 2, k % 2
                    if half == 0:
                        dve.wait_ge(s_dA, (b * NS + i) * DT + dt + 1)
                    dve.wait_ge(s_tr, b * NU + ku + 1 + TR0)
                    dve.wait_ge(s_hC, b * NU + ku - 3 + HC0)
                    dve.wait_ge(s_scan, b * NU + ku - 1 + SCAN0)
                    nc.vector.tensor_tensor_scan(h[:, k, :], dA[:, i % NDA, dt, half * HALF:(half + 1) * HALF],
                                                 p_tr[:, k % 2, :],
                                                 0.0 if half == 0 else h[:, dt, HALF - 1:HALF],
                                                 ALU.mult, ALU.add).then_inc(s_scan, 1)
                    if (ku - 2) // 4 == SKIP_STATE:
                        add_skip(b, (ku - 2) % 4)
                    for n in DVE_STATES:
                        for nh in range(2):
                            if ku == 4 * n + 2 * nh - 5:
                                spread_dve(b, n, nh)
                    if end:
                        for j in range(4):
                            if ku == AT["yg"] + j:
                                gate_y(b - 1, j)
                        for c in range(2):
                            if ku == AT["x1"][c]:
                                add_out(turn, c)
                            if ku == AT["ln2"] + c:
                                ln2_stats(turn, c)
                            if ku == AT["norm2"][c]:
                                ln_norm(1, x_res, b - 1, c)
                    if prepare:
                        for c in range(2):
                            if ku == AT["ln1"] + c:
                                ln1_stats(b + 1, c)
                            if ku == AT["norm1"][c]:
                                ln_norm(0, x_in, b + 1, c)
                        if 0 <= ku - AT["conv"] < TAPS * DT:
                            conv_step(turn, ku - AT["conv"])
                        for c in range(2):
                            if ku == AT[f"xdbl{c}"][-1] + DVE_AFTER:
                                xdbl_out(turn, c)
                        for j in range(4):
                            if ku == AT[f"z{j}"][-1] + DVE_AFTER:
                                z_out(turn, j)
                        if ku == AT["zmin"]:
                            z_min(turn)
                        for dt in range(DT):
                            if ku == AT["delta"] + dt:
                                z_max(b + 1, dt)

            start = turn_of(-1)
            for c in range(2):
                ln1_stats(0, c)
            for c in range(2):
                ln_norm(0, x_in, 0, c)
            dve.wait_ge(s_aexp, 1)
            nc.vector.tensor_scalar(a_neg[:, :], a_exp[:, :], -1.0, None, ALU.mult)
            dve.wait_ge(s_cst, 3)
            nc.vector.memset(stats[:, 0, 0:1], 0.0).then_inc(s_prep, 1)
            dve.wait_ge(s_prep, 1)
            nc.vector.memset(stats[:, 0, 0:1], 0.0).then_inc(s_scan, SCAN0)
            for step in range(TAPS * DT):
                conv_step(start, step)
            for c in range(2):
                xdbl_out(start, c)
            for k in range(4):
                z_out(start, k)
            z_min(start)
            dve.wait_ge(s_pprep, 1)
            nc.vector.tensor_copy(f_pT[:, :], p_tr[:, 0, 0:DM]).then_inc(s_prep, 1)
            dve.wait_ge(s_pprep, 2)
            nc.vector.tensor_copy(f_w[:, :], p_tr[:, 1, 0:DM]).then_inc(s_prep, 1)

            dve.wait_ge(s_w2, 16 * NW2)
            nc.vector.tensor_copy(emb_step[:, 0:1], emb[:, 0:1])
            nc.vector.tensor_tensor(emb_step[:, 1:NKNOT], emb[:, 1:NKNOT], emb[:, 0:NKNOT - 1], ALU.subtract).then_inc(s_stage3, 1)
            dve.wait_ge(s_stage3, 1)
            for m in range(1, NB):
                nc.vector.scalar_tensor_tensor(emb_step[:, 0:1], emb_step[:, m + 1:m + 2], float(-m), emb_step[:, 0:1], ALU.mult, ALU.add
                                               ).then_inc(s_stage3, 1)
                dve.wait_ge(s_stage3, 1 + m)
            nc.vector.tensor_tensor(emb_blocks[:, :, :], emb_step[:, :].unsqueeze(2).to_broadcast([P, NKNOT, NH]),
                                    head_mask[:, :].unsqueeze(1).to_broadcast([P, NKNOT, NH]), ALU.mult).then_inc(s_stage3, 1)
            dve.wait_ge(s_pprep, 3)
            nc.vector.tensor_tensor(bo_row[:, :], bo_row[:, :], p_tr[0:1, 0, HALF // 2:HALF // 2 + DM], ALU.add).then_inc(s_stage3, 1)
            for dt in range(DT):
                z_max(0, dt)
            for dt in range(DT):
                dve.wait_ge(s_delta, dt + 1)
                nc.vector.tensor_tensor(z_exp[:, dt, :], delta[:, dt * L:(dt + 1) * L], u[:, dt, :], ALU.mult).then_inc(s_du, 1)
            dve_turn(0)
            with dve.Fori(1, NB - 1) as b:
                dve_turn(b)
            dve_turn(NB - 1)
            final = turn_of(NB)
            for k in range(4):
                gate_y(NB - 1, k)
            for c in range(2):
                add_out(final, c)
                dve.wait_ge(s_empty[bank_of(final, f"out{c}")], empty_count(final, f"out{c}"))
                dve.nop(nofuse=True)
                ln2_half(c)
            for c in range(2):
                dve.wait_ge(s_rstd[1], NB + c)
                for j in range(c * TPH, (c + 1) * TPH):
                    last = nc.vector.tensor_scalar(xn[:, 1, j, :], x_res[:, j, :], mv[:, 1, j, 0:1], rstd[:, 1, j:j + 1],
                                                   ALU.subtract, ALU.mult)
                last.then_inc(s_xn[1], 1)

            NSTEP = 13

            def attn_stats(a, xb, j, first=False):
                for t in range(NB):
                    last = nc.vector.bn_stats(c_stats[:, a, t, :], xb[:, t * P:(t + 1) * P])
                last.then_inc(c_bnd[a], 1)
                dve.wait_ge(c_bnd[a], j + 1)
                if not first:
                    dve.wait_ge(c_sh[a], j)
                dve.nop(nofuse=True)
                for t in range(NB):
                    last = nc.vector.bn_aggr(c_mv[:, a, t, :], c_stats[:, a, t, :])
                last.then_inc(c_var[a], 1)

            xaf = xa[:, :, :].rearrange("p s c -> p (s c)")

            def stats3(j, first=False):
                dve.wait_ge(c_xa, 16 * j + 16)
                dve.nop(nofuse=True)
                attn_stats(0, xaf, j, first)

            def residual(j, first=False):
                dve.wait_ge(c_wo, j + 1)
                dve.wait_ge(c_kept, j)
                dve.wait_ge(c_xb, j + 1)
                nc.vector.tensor_tensor(x3[:, :].rearrange("p (s c) -> p s c", c=P), p_a[:, 0, :].rearrange("p (s c) -> p s c", c=P),
                                        xb[:, :, :], ALU.add).then_inc(c_x3, 1)
                dve.wait_ge(c_x3, j + 1)
                dve.nop(nofuse=True)
                attn_stats(1, x3, j, first)

            def logits(j):
                k = [0]

                def link(ins):
                    k[0] += 1
                    ins.then_inc(c_step, 1)
                    dve.wait_ge(c_step, j * NSTEP + k[0])

                gf = g[:, :, :, :].rearrange("p s t h -> p (s t h)")
                lf = lg[:, :, :, :].rearrange("p s t h -> p (s t h)")
                dve.wait_ge(c_th, j + 1)
                link(nc.vector.tensor_scalar(gf, gf, 0.5, 0.5, ALU.mult, ALU.add))
                for t in range(NB - 2, -1, -1):
                    link(nc.vector.tensor_tensor(g[:, :, t, :], g[:, :, t, :], g[:, :, t + 1, :], ALU.add))
                for m in range(NB):
                    last = nc.vector.tensor_scalar(cl[:, m, :], gf, float(m), float(m + 1), ALU.max, ALU.min)
                link(last)
                dve.wait_ge(c_vp, j + 1)
                pieces = cut(pk, side(j, NB * PW), NB * PW)
                for a in range(NB):
                    last = nc.vector.scalar_tensor_tensor(lg[:, a, :, :], p_tr[:, 0, a * NB * NH:(a + 1) * NB * NH].rearrange("p (t h) -> p t h", h=NH),
                                                          SCALE, pieces[:, a * NH:(a + 1) * NH].unsqueeze(1).to_broadcast([P, NB, NH]),
                                                          ALU.mult, ALU.add)
                last.then_inc(c_lgp, 1)
                ca = cl[:, :, :].rearrange("p m (s t h) -> p (m s) t h", s=NB, h=NH)
                link(nc.vector.tensor_tensor(ca, ca, pieces[:, NB * NH:NB * PW].rearrange("p (a h) -> p a h", h=NH).unsqueeze(2).to_broadcast([P, NB * NB, NB, NH]),
                                             ALU.mult))
                nc.vector.tensor_tensor(cl[:, 0, :], cl[:, 0, :], cl[:, 1, :], ALU.add)
                link(nc.vector.tensor_tensor(cl[:, 2, :], cl[:, 2, :], cl[:, 3, :], ALU.add))
                link(nc.vector.tensor_tensor(cl[:, 0, :], cl[:, 0, :], cl[:, 2, :], ALU.add))
                link(nc.vector.tensor_tensor(lf, lf, cl[:, 0, :], ALU.add))
                link(nc.vector.tensor_reduce(mx[:, :, :], lg[:, :, :, :].rearrange("p s t h -> p s h t"), AX.X, ALU.max))
                nc.vector.tensor_tensor(lg[:, :, :, :], lg[:, :, :, :], mx[:, :, :].unsqueeze(2).to_broadcast([P, NB, NB, NH]),
                                        ALU.subtract).then_inc(c_sub, 1)
                return k[0]

            def weights(j, k0):
                k = [k0]

                def link(ins):
                    k[0] += 1
                    ins.then_inc(c_step, 1)
                    dve.wait_ge(c_step, j * NSTEP + k[0])

                dve.wait_ge(c_exp, j + 1)
                link(nc.vector.tensor_reduce(sm[:, :, :], lg[:, :, :, :].rearrange("p s t h -> p s h t"), AX.X, ALU.add))
                link(nc.vector.reciprocal(rc[:, :, :], sm[:, :, :]))
                link(nc.vector.tensor_tensor(at[:, :, :].rearrange("p s (t h) -> p s t h", h=NH), lg[:, :, :, :],
                                             rc[:, :, :].unsqueeze(2).to_broadcast([P, NB, NB, NH]), ALU.mult))
                nc.vector.tensor_tensor(pv[:, :, :, :].rearrange("p s t (h d) -> p s (t h) d", d=HD),
                                        at[:, :, :].unsqueeze(3).to_broadcast([P, NB, NB * NH, HD]),
                                        cut(vt, side(j, NB * DM), NB * DM).rearrange("p (a d) -> p a d", d=HD).unsqueeze(1).to_broadcast([P, NB, NB * NH, HD]),
                                        ALU.mult).then_inc(c_pvd, 1)
                assert k[0] == NSTEP, k[0]

            def mix(j):
                dve.wait_ge(c_pvd, j + 1)
                dve.wait_ge(c_t2, j)
                nc.vector.tensor_reduce(o_tok[:, :, :], pv[:, :, :, :].rearrange("p s t c -> p s c t"), AX.X, ALU.add).then_inc(c_o, 1)

            def dve_step(j):
                k = logits(j)
                if begun(j, 2):
                    residual(j - 2, first=isinstance(j, int) and j == 2)
                if not ends(j, 3):
                    stats3(j + 3)
                weights(j, k)
                mix(j)

            stats3(0, first=True)
            stats3(1)
            dve.wait_ge(c_bo, 1)
            nc.vector.tensor_copy(bo_all[:, :], p_a[:, 0, 0:DM]).then_inc(c_bo, 1)
            stats3(2)
            for j in range(3):
                dve_step(j)
            with dve.Fori(3, TT - 3) as j:
                dve_step(j)
            for j in range(TT - 3, TT):
                dve_step(j)
            residual(TT - 2)
            residual(TT - 1)

        @block.tensor
        def _(pe):
            pe.wait_ge(s_cst, 3)
            nc.tensor.matmul(p_tr[:, 0, 0:2], ident[:, :], ident[:, 0:2], start=True, stop=True).then_inc(s_tr, TR0)
            pe.sem_inc(s_sum, SUM0)
            pe.sem_inc(s_yg, YG0)
            for bank in range(2):
                pe.sem_inc(s_empty[bank], 1)

            def start_job(turn, job):
                k = turn[2].index(job)
                pe.wait_ge(s_empty[k % 2], turn[3] + k // 2 + 1)
                return p_a[:, k % 2, :]

            def bank(turn, job):
                return p_a[:, bank_of(turn, job), :]

            def transposes(turn, job, src, cols=P):
                o = start_job(turn, job)
                for t, a in enumerate(src):
                    last = nc.tensor.transpose(o[:, t * P:t * P + cols], a, ident[0:cols, 0:cols])
                last.then_inc(s_full, 1)

            def do_xnT(turn, c):
                pe.wait_ge(s_xn[0], 2 * (turn[0] + 1) + c + 1)
                transposes(turn, f"xnT{c}", [xn[:, 0, c * TPH + t, :] for t in range(TPH)])

            def do_xs(turn, k):
                c, dt = k // 2, k % 2
                wait_emptied(pe, turn, f"xnT{c}")
                nc.tensor.matmul(start_job(turn, f"xs{k}"), w_in[:, dt * P:(dt + 1) * P], xnT[:, c * HALF:(c + 1) * HALF],
                                 start=True, stop=True).then_inc(s_full, 1)

            def do_gate(turn, k):
                c, dt = k // 2, k % 2
                nc.tensor.matmul(start_job(turn, f"gate{k}"), w_in[:, DI + dt * P:DI + (dt + 1) * P],
                                 xnT[:, c * HALF:(c + 1) * HALF],
                                 start=True, stop=True).then_inc(s_full, 1)

            def do_xdbl(turn, c, dt):
                if dt == 0:
                    start_job(turn, f"xdbl{c}")
                pe.wait_ge(s_u, (turn[0] + 1) * DT + dt + 1)
                mm = nc.tensor.matmul(bank(turn, f"xdbl{c}")[0:XD, :], w_x[:, dt, :], u[:, dt, c * HALF:(c + 1) * HALF],
                                      start=(dt == 0), stop=(dt == DT - 1))
                if dt == DT - 1:
                    mm.then_inc(s_full, 1)

            def do_bt(turn, c):
                wait_emptied(pe, turn, f"xdbl{c}")
                transposes(turn, f"bt{c}", [xdbl[:, (c * TPH + t) * P:(c * TPH + t + 1) * P] for t in range(TPH)], XD)

            def do_z(turn, k):
                c, dt = k // 2, k % 2
                nc.tensor.matmul(start_job(turn, f"z{k}"), w_dt[:, dt * P:(dt + 1) * P], xdbl[0:R, c * HALF:(c + 1) * HALF],
                                 start=True, stop=True).then_inc(s_full, 1)

            def do_duT(turn, k):
                pe.wait_ge(s_du, (turn[0] + 1) * DT + DT)
                transposes(turn, f"duT{k}", [z_exp[:, dt, (2 * k + t) * P:(2 * k + t + 1) * P] for t in range(2) for dt in range(DT)])

            def do_out(turn, c, part):
                if part == 0:
                    pe.wait_ge(s_yg, (turn[0] - 1) * 4 + 2 * (c + 1) + YG0)
                    start_job(turn, f"out{c}")
                o = bank(turn, f"out{c}")
                for t in range(2 * part, 2 * part + 2):
                    for dt in range(DT):
                        last = nc.tensor.matmul(o[:, t * P:(t + 1) * P], yg[:, dt, (c * TPH + t) * P:(c * TPH + t + 1) * P],
                                                w_out[:, dt, :], start=(dt == 0), stop=(dt == DT - 1))
                if part:
                    last.then_inc(s_full, 1)

            def do_hT(turn, c):
                pe.wait_ge(s_xn[1], 2 * (turn[0] - 1) + c + 1)
                transposes(turn, f"hT{c}", [xn[:, 1, c * TPH + t, :] for t in range(TPH)])

            def do_ffn(turn, c, part):
                if part == 0:
                    wait_emptied(pe, turn, f"hT{c}")
                    nc.tensor.matmul(start_job(turn, f"ffn{c}"), ones_row[:, :], f_brow[:, :, :].rearrange("a t n -> a (t n)"),
                                     start=True, stop=False, skip_group_check=True)
                    return
                o = bank(turn, f"ffn{c}")
                for t in range(TPH):
                    last = nc.tensor.matmul(o[:, t * P:(t + 1) * P], hT[:, (c * TPH + t) * P:(c * TPH + t + 1) * P],
                                            f_w[:, :], start=False, stop=True, skip_group_check=True)
                last.then_inc(s_full, 1)

            def pe_turn(b):
                turn = turn_of(b)
                prepare, end = turn[2] is not D_JOBS, turn[2] is not A_JOBS

                def turn_back(b, ku):
                    k = ku % 4
                    half, dt = k // 2, k % 2
                    pe.wait_ge(*duB_ready(b, ku // 4, half))
                    pe.wait_ge(s_scan, b * NU + ku - 1 + SCAN0)
                    for t in range(TPH):
                        last = nc.tensor.transpose(p_tr[:, k % 2, t * P:(t + 1) * P], duB[:, 2 * (ku // 4 % 2) + half, t, dt * P:(dt + 1) * P], ident[:, :])
                    last.then_inc(s_tr, 1)

                LAG = 3
                if isinstance(b, int) and b == 0:
                    for ku in range(LAG):
                        turn_back(b, ku)
                for ku in range(NU):
                    k = ku % 4
                    if ku + LAG < NU:
                        turn_back(b, ku + LAG)
                    elif not (isinstance(b, int) and b == NB - 1):
                        turn_back(b + 1, ku + LAG - NU)
                    if ku // 4 == SKIP_STATE:
                        pe.wait_ge(s_skip, b * 4 + k + 1)
                    else:
                        pe.wait_ge(s_hC, b * NU + ku + 1 + HC0)
                    if ku < 4:
                        pe.wait_ge(s_yg, (b - 1) * 4 + k + 1 + YG0)
                    nc.tensor.matmul(p_y[:, k % 2, k // 2, :], ident[:, :], hC[:, k, :], start=(ku < 4), stop=(ku >= NU - 4),
                                     skip_group_check=True).then_inc(s_sum, 1)
                    if end:
                        for c in range(2):
                            if ku in AT[f"out{c}"]:
                                do_out(turn, c, AT[f"out{c}"].index(ku))
                    if prepare:
                        for c in range(2):
                            if ku in AT[f"xnT{c}"]:
                                do_xnT(turn, c)
                        for j in range(4):
                            if ku in AT[f"xs{j}"]:
                                do_xs(turn, j)
                    if end:
                        for c in range(2):
                            if ku in AT[f"hT{c}"]:
                                do_hT(turn, c)
                            if ku in AT[f"ffn{c}"]:
                                do_ffn(turn, c, AT[f"ffn{c}"].index(ku))
                    if prepare:
                        for c in range(2):
                            if ku in AT[f"xdbl{c}"]:
                                do_xdbl(turn, c, AT[f"xdbl{c}"].index(ku))
                            if ku in AT[f"bt{c}"]:
                                do_bt(turn, c)
                        for j in range(4):
                            if ku in AT[f"z{j}"]:
                                do_z(turn, j)
                            if ku in AT[f"gate{j}"]:
                                do_gate(turn, j)
                            if ku in AT[f"duT{j}"]:
                                do_duT(turn, j)

            start = turn_of(-1)
            for c in range(2):
                do_xnT(start, c)
            pe.wait_ge(s_w0, 16)
            for k in range(4):
                do_xs(start, k)
            pe.wait_ge(s_w1, 16 * NW1)
            for c in range(2):
                for dt in range(DT):
                    do_xdbl(start, c, dt)
            for c in range(2):
                do_bt(start, c)
            for k in range(4):
                do_z(start, k)
            for k in range(2):
                do_gate(start, k)
            pe.wait_ge(s_w2, 16 * NW2)
            nc.tensor.matmul(p_tr[:, 0, 0:DM], f_a1[:, :], f_wT[:, :], start=True, stop=True).then_inc(s_pprep, 1)
            pe.wait_ge(s_prep, 2)
            nc.tensor.matmul(p_tr[:, 1, 0:DM], f_pT[:, :], f_a2[:, :], start=True, stop=True).then_inc(s_pprep, 1)
            nc.tensor.matmul(p_tr[0:1, 0, HALF // 2:HALF // 2 + DM], bv_col[:, :], w_o[:, :], start=True, stop=True).then_inc(s_pprep, 1)
            pe.wait_ge(s_prep, 3)
            pe.wait_ge(s_stage3, 3 + NB - 1)
            for k in range(2, 4):
                do_gate(start, k)
            for k in range(4):
                do_duT(start, k)
            pe_turn(0)
            with pe.Fori(1, NB - 1) as b:
                pe_turn(b)
            pe_turn(NB - 1)
            final = turn_of(NB)
            for c in range(2):
                for part in range(2):
                    do_out(final, c, part)
            for c in range(2):
                do_hT(final, c)
                for part in range(2):
                    do_ffn(final, c, part)

            def turn4(src, need, full, j, freed):
                pe.wait_ge(need, j + 1)
                if freed is not None:
                    pe.wait_ge(*freed)
                for t in range(NB):
                    last = nc.tensor.transpose(p_tr[:, 1, t * P:(t + 1) * P], src[:, t, :], ident[:, :])
                last.then_inc(full, 1)

            def project_qk(j):
                pe.wait_ge(c_e1, j + 1)
                nc.tensor.matmul(p_y[:, 0, 0, :], w_q[:, :], xT3[:, :], start=True, stop=True)
                nc.tensor.matmul(p_y[:, 0, 1, :], w_k[:, :], xT3[:, :], start=True, stop=True).then_inc(c_proj, 1)

            def project_v(j, first=False):
                if not first:
                    pe.wait_ge(c_vp, j)
                for t in range(NB):
                    nc.tensor.matmul(p_y[:, 1, 0, t * DM:(t + 1) * DM], xT3[:, t * P:(t + 1) * P], w_v[:, :], start=True, stop=True)

            def project_p(j):
                pe.wait_ge(c_qk, j + 1)
                for t in range(NB):
                    last = nc.tensor.matmul(p_y[:, 1, 1, t * PW:(t + 1) * PW], qT[:, t, :],
                                            emb_blocks[:, :, :].rearrange("p m h -> p (m h)"), start=True, stop=True)
                last.then_inc(c_p, 1)

            def scores(j, first=False):
                pe.wait_ge(c_prod, j + 1)
                if not first:
                    pe.wait_ge(c_lgp, j)
                for a in range(NB):
                    for t in range(NB):
                        last = nc.tensor.matmul(p_tr[:, 0, (a * NB + t) * NH:(a * NB + t + 1) * NH], qk[:, a, t, :], head_mask[:, :],
                                                start=True, stop=True)
                last.then_inc(c_L, 1)

            def out_project(j):
                pe.wait_ge(c_e2, j + 1)
                if isinstance(j, int) and j == 0:
                    pe.wait_ge(c_bo, 2)
                else:
                    pe.wait_ge(c_x3, j)
                for t in range(NB):
                    last = nc.tensor.matmul(p_a[:, 0, t * P:(t + 1) * P], oT[:, t * P:(t + 1) * P], w_o[:, :], start=True, stop=True)
                last.then_inc(c_wo, 1)

            def ffn(j):
                pe.wait_ge(c_e3, j + 1)
                pe.wait_ge(c_tanh, j)
                nc.tensor.matmul(p_a[:, 1, :], ones_row[:, :], f_brow[:, :, :].rearrange("a t n -> a (t n)"), start=True, stop=False,
                                 skip_group_check=True)
                for t in range(NB):
                    last = nc.tensor.matmul(p_a[:, 1, t * P:(t + 1) * P], xT4[:, t * P:(t + 1) * P], f_w[:, :],
                                            start=False, stop=True, skip_group_check=True)
                last.then_inc(c_ffn, 1)

            def pe_step(j):
                if not ends(j, 1):
                    project_v(j + 1)
                free = (c_e3, j - 2) if begun(j, 3) else (c_e2, 1) if j == 2 else (c_e1, j + 2)
                if not ends(j, 2):
                    turn4(xn3, c_xn[0], c_t1, j + 2, free)
                    free = (c_e1, j + 3)
                if not ends(j, 1):
                    project_p(j + 1)
                if begun(j, 1):
                    turn4(o_tok, c_o, c_t2, j - 1, free)
                if not ends(j, 2):
                    project_qk(j + 2)
                if not ends(j, 1):
                    scores(j + 1)
                if begun(j, 2):
                    turn4(xn4, c_xn[1], c_t3, j - 2, (c_e2, j))
                if begun(j, 1):
                    out_project(j - 1)
                if begun(j, 2):
                    ffn(j - 2)

            for c in range(2):
                wait_emptied(pe, turn_of(NB), f"ffn{c}")
            nc.tensor.matmul(p_a[:, 0, 0:DM], ones_row[:, :], bo_row[:, :], start=True, stop=True).then_inc(c_bo, 1)
            turn4(xn3, c_xn[0], c_t1, 0, None)
            project_qk(0)
            project_v(0, first=True)
            project_p(0)
            turn4(xn3, c_xn[0], c_t1, 1, (c_e1, 1))
            project_qk(1)
            scores(0, first=True)
            for j in range(3):
                pe_step(j)
            with pe.Fori(3, TT - 3) as j:
                pe_step(j)
            for j in range(TT - 3, TT):
                pe_step(j)
            turn4(o_tok, c_o, c_t2, TT - 1, (c_e3, TT - 2))
            out_project(TT - 1)
            turn4(xn4, c_xn[1], c_t3, TT - 2, (c_e2, TT))
            ffn(TT - 2)
            turn4(xn4, c_xn[1], c_t3, TT - 1, (c_e3, TT - 1))
            ffn(TT - 1)


_INS = [("L0_attn_a_x", 0), ("L0_attn_a_W_in", 0), ("L0_attn_a_conv_w", 0), ("L0_attn_a_conv_b", 0), ("L0_attn_a_W_x", 0),
        ("L0_attn_a_W_dt", 0), ("L0_attn_a_b_dt", 0), ("L0_attn_a_A_log", 0), ("L0_attn_a_D", 0), ("L0_attn_a_W_out", 0),
        ("L0_attn_b_Wq", 0), ("L0_attn_b_bq", 0), ("L0_attn_b_Wk", 0), ("L0_attn_b_bk", 0),
        ("L0_attn_b_Wv", 0), ("L0_attn_b_bv", 0), ("L0_attn_b_Wo", 0), ("L0_attn_b_bo", 0), ("L0_attn_b_pos_emb", 0),
        ("L0_ffn_weight", 1), ("L0_ffn_aux_weight1", 0), ("L0_ffn_aux_weight2", 0), ("L0_ffn_bias", 0)]
_OUT = (4, 1024, 128)


def kernel(**inputs):
    import numpy as _np
    import concourse.bacc as _bacc
    from concourse import mybir as _mybir
    from concourse.bass_utils import run_bass_kernel_spmd as _run

    nc = _bacc.Bacc("TRN2", target_bir_lowering=False, num_devices=1)
    arrays, args = {}, []
    for name, turned in _INS:
        a = _np.ascontiguousarray(_np.asarray(inputs[name]).T if turned else inputs[name])
        key = f"in_{name}{'_T' if turned else ''}_dram"
        arrays[key] = a
        args.append(nc.dram_tensor(key, a.shape, _mybir.dt.from_np(a.dtype), kind="ExternalInput").ap())
    args.append(nc.dram_tensor("out_0_dram", _OUT, _mybir.dt.float32, kind="ExternalOutput").ap())
    build_hybrid_block(nc, *args)
    r = _run(nc, [arrays], core_ids=[0])
    return r.results[0]["out_0_dram"]
```
